# Optimizing a Trainium2 kernel written in Bass

```python
import numpy as np
import jax
import jax.numpy as jnp

def _softmax(x, axis=-1):
    return jax.nn.softmax(x, axis=axis)

def _gelu(x):
    return jax.nn.gelu(x, approximate=True)

def _silu(x):
    return jax.nn.silu(x)

def _sigmoid(x):
    return jax.nn.sigmoid(x)

def _layernorm(x, axis=-1, eps=1e-05):
    m = jnp.mean(x, axis=axis, keepdims=True)
    v = jnp.var(x, axis=axis, keepdims=True)
    return (x - m) / jnp.sqrt(v + eps)

def _scatter_add(tgt, idx, src, axis=0):
    return tgt.at[idx].add(src)

def _segment_sum(src, seg, n):
    return jax.ops.segment_sum(src, seg, n)
kernel_name = 'mk_gnn_ffn_d2_gnn_r8_88ab1f'

def setup_inputs(seed: int=0):
    np.random.seed(seed)
    _w = jnp.asarray

    def _rec_inputs():
        import jax
        import jax.numpy as jnp
        _gk = jax.random.key(seed)
        x = -0.0003713 + 1 * jax.random.normal(jax.random.fold_in(_gk, 1), (6250, 256), jnp.float32)
        src = jax.random.randint(jax.random.fold_in(_gk, 2), (200000,), 0, 6250, jnp.int32)
        dst = jnp.minimum((6250 * jax.random.uniform(jax.random.fold_in(_gk, 3), (200000,)) ** 2.0).astype(jnp.int32), 49999)
        _o = jnp.argsort(dst, stable=True)
        src = src[_o]
        dst = dst[_o]
        edge_attr_16 = -0.000153872 + 1.00011 * jax.random.normal(jax.random.fold_in(_gk, 11), (200000, 16), jnp.float32)
        edge_attr_4 = 0.0007022 + 0.999661 * jax.random.normal(jax.random.fold_in(_gk, 12), (200000, 4), jnp.float32)
        return (x, src, dst, edge_attr_16, edge_attr_4)
    x, src, dst, edge_attr_16, edge_attr_4 = _rec_inputs()

    def _L0_gnn_setup():
        import jax, jax.numpy as jnp
        import numpy as np
        N_NODES = 6250
        N_EDGES = 100000
        D_IN = 256
        D_OUT = 256
        BN_EPS = 1e-05
        L2_EPS = 1e-12
        key = jax.random.key(seed)
        ks = jax.random.split(key, 8)
        x = jax.random.normal(ks[0], (N_NODES, D_IN), dtype=jnp.float32)
        edge_index = jax.random.randint(ks[1], (2, N_EDGES), 0, N_NODES, dtype=jnp.int64)
        s = 1.0 / np.sqrt(D_IN)
        W_l = jax.random.uniform(ks[2], (D_OUT, D_IN), jnp.float32, -s, s)
        b_l = jax.random.uniform(ks[3], (D_OUT,), jnp.float32, -s, s)
        W_r = jax.random.uniform(ks[4], (D_OUT, D_IN), jnp.float32, -s, s)
        gamma = jnp.ones((D_OUT,), jnp.float32)
        beta = jnp.zeros((D_OUT,), jnp.float32)
        return {'x': x, 'edge_index': edge_index, 'W_l': W_l, 'b_l': b_l, 'W_r': W_r, 'gamma': gamma, 'beta': beta}
    _L0_gnn_all = _L0_gnn_setup()
    _L0_gnn_in = {k: v for k, v in _L0_gnn_all.items() if k in ('W_l', 'b_l', 'W_r', 'gamma', 'beta')}
    del _L0_gnn_all

    def _L0_ffn_setup():
        import jax, jax.numpy as jnp
        import numpy as np
        BN_EPS = 0.001

        def _bn(h, g, b, m, v):
            return g * (h - m) * jax.lax.rsqrt(v + BN_EPS) + b
        key = jax.random.key(seed)
        ks = jax.random.split(key, 8)
        B, F, Df = (256, 64, 256)
        E, H, D = (8, 256, 256)
        s1 = 1.0 / np.sqrt(Df)
        s2 = 1.0 / np.sqrt(H)
        return {'x': jax.random.normal(ks[0], (B, F, Df), jnp.float32), 'Wr': jax.random.normal(ks[1], (Df, E), jnp.float32) * s1, 'br': jnp.zeros((E,), jnp.float32), 'W1': jax.random.normal(ks[2], (E, Df, H), jnp.float32) * s1, 'b1': jnp.zeros((E, H), jnp.float32), 'g1': jnp.ones((E, H), jnp.float32), 'be1': jnp.zeros((E, H), jnp.float32), 'm1': jnp.zeros((E, H), jnp.float32), 'v1': jnp.ones((E, H), jnp.float32), 'W2': jax.random.normal(ks[3], (E, H, H), jnp.float32) * s2, 'b2': jnp.zeros((E, H), jnp.float32), 'g2': jnp.ones((E, H), jnp.float32), 'be2': jnp.zeros((E, H), jnp.float32), 'm2': jnp.zeros((E, H), jnp.float32), 'v2': jnp.ones((E, H), jnp.float32), 'Wo': jax.random.normal(ks[4], (E, H, D), jnp.float32) * s2, 'bo': jnp.zeros((E, D), jnp.float32)}
    _L0_ffn_all = _L0_ffn_setup()
    _L0_ffn_in = {k: v for k, v in _L0_ffn_all.items() if k in ('Wr', 'br', 'W1', 'b1', 'g1', 'be1', 'm1', 'v1', 'W2', 'b2', 'g2', 'be2', 'm2', 'v2', 'Wo', 'bo')}
    del _L0_ffn_all

    def _L1_gnn_setup():
        import jax, jax.numpy as jnp
        import numpy as np
        N, E, C, R, HID = (6250, 62500, 64, 16, 64)
        key = jax.random.key(seed)
        ks = jax.random.split(key, 24)
        g = lambda k, shape, s=1.0: jax.random.normal(k, shape, dtype=jnp.float32) * s
        cs = C ** (-0.5)
        inp = {'h': g(ks[0], (N, 4 * C)), 'edge_index': jax.random.randint(ks[1], (2, E), 0, N), 'edge_sh': g(ks[2], (E, 4)), 'edge_rbf': g(ks[3], (E, R)), 'W_up0': g(ks[4], (C, C), cs), 'W_up1': g(ks[5], (C, C), cs), 'M1': g(ks[6], (R, HID), R ** (-0.5)), 'M2': g(ks[7], (HID, HID), HID ** (-0.5)), 'M3': g(ks[8], (HID, HID), HID ** (-0.5)), 'M4': g(ks[9], (HID, 4 * C), HID ** (-0.5)), 'W_lin0': g(ks[10], (C, C), cs), 'W_lin1': g(ks[11], (C, C), cs), 'Wsc0': g(ks[12], (C, C), cs), 'Wsc1': g(ks[13], (C, C), cs), 'Wc0': g(ks[14], (C, 5)), 'Wc1': g(ks[15], (C, 4)), 'WB0': g(ks[16], (C, C), cs), 'WB1': g(ks[17], (C, C), cs), 'gamma0': jnp.ones((C,), jnp.float32), 'beta0': jnp.zeros((C,), jnp.float32), 'gamma1': jnp.ones((C,), jnp.float32)}
        return inp
    _L1_gnn_all = _L1_gnn_setup()
    _L1_gnn_in = {k: v for k, v in _L1_gnn_all.items() if k in ('W_up0', 'W_up1', 'M1', 'M2', 'M3', 'M4', 'W_lin0', 'W_lin1', 'Wsc0', 'Wsc1', 'Wc0', 'Wc1', 'WB0', 'WB1', 'gamma0', 'beta0', 'gamma1')}
    del _L1_gnn_all

    def _L1_ffn_setup():
        import jax, jax.numpy as jnp
        import numpy as np
        E, D, H, TOP_K = (6, 256, 256, 2)
        ROUTER_H = D // 2
        key = jax.random.key(seed)
        ks = jax.random.split(key, 12)
        s = 1.0 / np.sqrt(D)
        sh = 1.0 / np.sqrt(H)
        sr = 1.0 / np.sqrt(ROUTER_H)
        return {'features': jax.random.normal(ks[0], (8, 512, D), dtype=jnp.float32), 'router_w1': jax.random.uniform(ks[1], (D, ROUTER_H), jnp.float32, -s, s), 'router_b1': jnp.zeros((ROUTER_H,), jnp.float32), 'router_w2': jax.random.uniform(ks[2], (ROUTER_H, E), jnp.float32, -sr, sr), 'router_b2': jnp.zeros((E,), jnp.float32), 'expert_w1': jax.random.uniform(ks[3], (E, D, H), jnp.float32, -s, s), 'expert_b1': jnp.zeros((E, H), jnp.float32), 'expert_w2': jax.random.uniform(ks[4], (E, H, H), jnp.float32, -sh, sh), 'expert_b2': jnp.zeros((E, H), jnp.float32), 'expert_w3': jax.random.uniform(ks[5], (E, H, D), jnp.float32, -sh, sh), 'expert_b3': jnp.zeros((E, D), jnp.float32)}
    _L1_ffn_all = _L1_ffn_setup()
    _L1_ffn_in = {k: v for k, v in _L1_ffn_all.items() if k in ('router_w1', 'router_b1', 'router_w2', 'router_b2', 'expert_w1', 'expert_b1', 'expert_w2', 'expert_b2', 'expert_w3', 'expert_b3')}
    del _L1_ffn_all
    return {'x': x, 'src': src, 'dst': dst, 'edge_attr_16': edge_attr_16, 'edge_attr_4': edge_attr_4, 'L0_gnn_W_l': _L0_gnn_in['W_l'], 'L0_gnn_b_l': _L0_gnn_in['b_l'], 'L0_gnn_W_r': _L0_gnn_in['W_r'], 'L0_gnn_gamma': _L0_gnn_in['gamma'], 'L0_gnn_beta': _L0_gnn_in['beta'], 'L0_ffn_Wr': _L0_ffn_in['Wr'], 'L0_ffn_br': _L0_ffn_in['br'], 'L0_ffn_W1': _L0_ffn_in['W1'], 'L0_ffn_b1': _L0_ffn_in['b1'], 'L0_ffn_g1': _L0_ffn_in['g1'], 'L0_ffn_be1': _L0_ffn_in['be1'], 'L0_ffn_m1': _L0_ffn_in['m1'], 'L0_ffn_v1': _L0_ffn_in['v1'], 'L0_ffn_W2': _L0_ffn_in['W2'], 'L0_ffn_b2': _L0_ffn_in['b2'], 'L0_ffn_g2': _L0_ffn_in['g2'], 'L0_ffn_be2': _L0_ffn_in['be2'], 'L0_ffn_m2': _L0_ffn_in['m2'], 'L0_ffn_v2': _L0_ffn_in['v2'], 'L0_ffn_Wo': _L0_ffn_in['Wo'], 'L0_ffn_bo': _L0_ffn_in['bo'], 'L1_gnn_W_up0': _L1_gnn_in['W_up0'], 'L1_gnn_W_up1': _L1_gnn_in['W_up1'], 'L1_gnn_M1': _L1_gnn_in['M1'], 'L1_gnn_M2': _L1_gnn_in['M2'], 'L1_gnn_M3': _L1_gnn_in['M3'], 'L1_gnn_M4': _L1_gnn_in['M4'], 'L1_gnn_W_lin0': _L1_gnn_in['W_lin0'], 'L1_gnn_W_lin1': _L1_gnn_in['W_lin1'], 'L1_gnn_Wsc0': _L1_gnn_in['Wsc0'], 'L1_gnn_Wsc1': _L1_gnn_in['Wsc1'], 'L1_gnn_Wc0': _L1_gnn_in['Wc0'], 'L1_gnn_Wc1': _L1_gnn_in['Wc1'], 'L1_gnn_WB0': _L1_gnn_in['WB0'], 'L1_gnn_WB1': _L1_gnn_in['WB1'], 'L1_gnn_gamma0': _L1_gnn_in['gamma0'], 'L1_gnn_beta0': _L1_gnn_in['beta0'], 'L1_gnn_gamma1': _L1_gnn_in['gamma1'], 'L1_ffn_router_w1': _L1_ffn_in['router_w1'], 'L1_ffn_router_b1': _L1_ffn_in['router_b1'], 'L1_ffn_router_w2': _L1_ffn_in['router_w2'], 'L1_ffn_router_b2': _L1_ffn_in['router_b2'], 'L1_ffn_expert_w1': _L1_ffn_in['expert_w1'], 'L1_ffn_expert_b1': _L1_ffn_in['expert_b1'], 'L1_ffn_expert_w2': _L1_ffn_in['expert_w2'], 'L1_ffn_expert_b2': _L1_ffn_in['expert_b2'], 'L1_ffn_expert_w3': _L1_ffn_in['expert_w3'], 'L1_ffn_expert_b3': _L1_ffn_in['expert_b3']}

def reference(x, src, dst, edge_attr_16, edge_attr_4, L0_gnn_W_l, L0_gnn_b_l, L0_gnn_W_r, L0_gnn_gamma, L0_gnn_beta, L0_ffn_Wr, L0_ffn_br, L0_ffn_W1, L0_ffn_b1, L0_ffn_g1, L0_ffn_be1, L0_ffn_m1, L0_ffn_v1, L0_ffn_W2, L0_ffn_b2, L0_ffn_g2, L0_ffn_be2, L0_ffn_m2, L0_ffn_v2, L0_ffn_Wo, L0_ffn_bo, L1_gnn_W_up0, L1_gnn_W_up1, L1_gnn_M1, L1_gnn_M2, L1_gnn_M3, L1_gnn_M4, L1_gnn_W_lin0, L1_gnn_W_lin1, L1_gnn_Wsc0, L1_gnn_Wsc1, L1_gnn_Wc0, L1_gnn_Wc1, L1_gnn_WB0, L1_gnn_WB1, L1_gnn_gamma0, L1_gnn_beta0, L1_gnn_gamma1, L1_ffn_router_w1, L1_ffn_router_b1, L1_ffn_router_w2, L1_ffn_router_b2, L1_ffn_expert_w1, L1_ffn_expert_b1, L1_ffn_expert_w2, L1_ffn_expert_b2, L1_ffn_expert_w3, L1_ffn_expert_b3):
    import jax
    import jax.numpy as jnp

    def _L0_gnn_ref(x, edge_index, W_l, b_l, W_r, gamma, beta):
        import jax, jax.numpy as jnp
        import numpy as np
        N_NODES = 6250
        N_EDGES = 100000
        D_IN = 256
        D_OUT = 256
        BN_EPS = 1e-05
        L2_EPS = 1e-12
        N = x.shape[0]
        src = edge_index[0]
        dst = edge_index[1]
        agg = jax.ops.segment_sum(x[src], dst, num_segments=N)
        deg = jax.ops.segment_sum(jnp.ones_like(src, dtype=x.dtype), dst, num_segments=N)
        mean = agg / jnp.maximum(deg, 1.0)[:, None]
        out = mean @ W_l.T + b_l + x @ W_r.T
        nrm = jnp.sqrt(jnp.sum(out * out, axis=-1, keepdims=True))
        out = out / jnp.maximum(nrm, L2_EPS)
        mu = jnp.mean(out, axis=0)
        var = jnp.mean((out - mu) ** 2, axis=0)
        out = (out - mu) / jnp.sqrt(var + BN_EPS) * gamma + beta
        return jax.nn.relu(out)

    def _L0_ffn_ref(x, Wr, br, W1, b1, g1, be1, m1, v1, W2, b2, g2, be2, m2, v2, Wo, bo):
        import jax, jax.numpy as jnp
        import numpy as np
        BN_EPS = 0.001

        def _bn(h, g, b, m, v):
            return g * (h - m) * jax.lax.rsqrt(v + BN_EPS) + b
        feat = jnp.mean(x, axis=0)
        w = jax.nn.softmax(feat @ Wr + br, axis=-1)
        h = jnp.einsum('bfd,edh->bfeh', x, W1) + b1
        h = jax.nn.relu(_bn(h, g1, be1, m1, v1))
        h = jnp.einsum('bfeh,ehk->bfek', h, W2) + b2
        h = jax.nn.relu(_bn(h, g2, be2, m2, v2))
        y = jnp.einsum('bfeh,ehd->bfed', h, Wo) + bo
        return jnp.einsum('bfed,fe->bfd', y, w)

    def _L1_gnn_ref(h, edge_index, edge_sh, edge_rbf, W_up0, W_up1, M1, M2, M3, M4, W_lin0, W_lin1, Wsc0, Wsc1, Wc0, Wc1, WB0, WB1, gamma0, beta0, gamma1):
        import jax, jax.numpy as jnp
        import numpy as np
        N, E, C, R, HID = (6250, 62500, 64, 16, 64)
        n = h.shape[0]
        h0 = h[:, :C]
        h1 = h[:, C:].reshape(n, C, 3)
        up0 = h0 @ W_up0
        up1 = jnp.einsum('ncx,cd->ndx', h1, W_up1)
        r = jax.nn.silu(edge_rbf @ M1)
        r = jax.nn.silu(r @ M2)
        r = jax.nn.silu(r @ M3)
        tpw = (r @ M4).reshape(-1, 4, C)
        snd, rcv = (edge_index[0], edge_index[1])
        x0 = up0[snd]
        x1 = up1[snd]
        sh0 = edge_sh[:, 0]
        sh1 = edge_sh[:, 1:]
        inv3 = 1.0 / jnp.sqrt(jnp.float32(3.0))
        m0e = tpw[:, 0] * x0 * sh0[:, None] + tpw[:, 3] * jnp.einsum('ecx,ex->ec', x1, sh1) * inv3
        m1e = tpw[:, 1][:, :, None] * x0[:, :, None] * sh1[:, None, :] + tpw[:, 2][:, :, None] * x1 * sh0[:, None, None]
        msg0 = jax.ops.segment_sum(m0e, rcv, num_segments=n)
        msg1 = jax.ops.segment_sum(m1e, rcv, num_segments=n)
        A0 = msg0 @ W_lin0
        A1 = jnp.einsum('ncx,cd->ndx', msg1, W_lin1)
        sc0 = h0 @ Wsc0
        sc1 = jnp.einsum('ncx,cd->ndx', h1, Wsc1)
        vv = jnp.sum(A1 * A1, -1)
        B0 = Wc0[:, 0] * A0 + Wc0[:, 1] * A0 * A0 + Wc0[:, 2] * vv + Wc0[:, 3] * A0 ** 3 + Wc0[:, 4] * A0 * vv
        B1 = (Wc1[:, 0] + Wc1[:, 1] * A0 + Wc1[:, 2] * A0 * A0 + Wc1[:, 3] * vv)[..., None] * A1
        o0 = B0 @ WB0 + sc0
        o1 = jnp.einsum('ncx,cd->ndx', B1, WB1) + sc1
        eps = jnp.float32(1e-05)
        mu = jnp.mean(o0, 0)
        xc = o0 - mu
        var = jnp.mean(xc * xc, 0)
        n0 = xc * jax.lax.rsqrt(var + eps) * gamma0 + beta0
        nrm1 = jnp.mean(jnp.sum(o1 * o1, -1) / 3.0, 0)
        n1 = o1 * (jax.lax.rsqrt(nrm1 + eps) * gamma1)[None, :, None]
        return jnp.concatenate([n0, n1.reshape(n, 3 * C)], -1)

    def _L1_ffn_ref(features, router_w1, router_b1, router_w2, router_b2, expert_w1, expert_b1, expert_w2, expert_b2, expert_w3, expert_b3):
        import jax, jax.numpy as jnp
        import numpy as np
        E, D, H, TOP_K = (6, 256, 256, 2)
        ROUTER_H = D // 2
        rh = jax.nn.relu(features @ router_w1 + router_b1)
        expert_logits = jax.nn.softmax(rh @ router_w2 + router_b2, axis=-1)
        top_w, top_i = jax.lax.top_k(expert_logits, TOP_K)
        routing_weights = jax.nn.softmax(top_w, axis=-1)
        h1 = jax.nn.relu(jnp.einsum('bsd,edh->bseh', features, expert_w1) + expert_b1)
        h2 = jax.nn.relu(jnp.einsum('bseh,ehf->bsef', h1, expert_w2) + expert_b2)
        expert_out = jnp.einsum('bsef,efo->bseo', h2, expert_w3) + expert_b3
        sel = jnp.take_along_axis(expert_out, top_i[:, :, :, None], axis=2)
        combined = jnp.sum(sel * routing_weights[..., None], axis=2)
        return combined
    edge_index = jnp.stack([src, dst])
    x = x + _L0_gnn_ref(_layernorm(x, axis=-1), edge_index, L0_gnn_W_l, L0_gnn_b_l, L0_gnn_W_r, L0_gnn_gamma, L0_gnn_beta)
    x = x + _L0_ffn_ref(_layernorm(x, axis=-1)[None], L0_ffn_Wr, L0_ffn_br, L0_ffn_W1, L0_ffn_b1, L0_ffn_g1, L0_ffn_be1, L0_ffn_m1, L0_ffn_v1, L0_ffn_W2, L0_ffn_b2, L0_ffn_g2, L0_ffn_be2, L0_ffn_m2, L0_ffn_v2, L0_ffn_Wo, L0_ffn_bo)[0]
    x = x + _L1_gnn_ref(_layernorm(x, axis=-1), edge_index, edge_attr_4, edge_attr_16, L1_gnn_W_up0, L1_gnn_W_up1, L1_gnn_M1, L1_gnn_M2, L1_gnn_M3, L1_gnn_M4, L1_gnn_W_lin0, L1_gnn_W_lin1, L1_gnn_Wsc0, L1_gnn_Wsc1, L1_gnn_Wc0, L1_gnn_Wc1, L1_gnn_WB0, L1_gnn_WB1, L1_gnn_gamma0, L1_gnn_beta0, L1_gnn_gamma1)
    x = x + _L1_ffn_ref(_layernorm(x, axis=-1)[None], L1_ffn_router_w1, L1_ffn_router_b1, L1_ffn_router_w2, L1_ffn_router_b2, L1_ffn_expert_w1, L1_ffn_expert_b1, L1_ffn_expert_w2, L1_ffn_expert_b2, L1_ffn_expert_w3, L1_ffn_expert_b3)[0]
    return x

_drawn_inputs = setup_inputs


def setup_inputs(seed=0):
    import zlib

    import numpy as np

    out = dict(_drawn_inputs(seed))
    spreads = {'L0_gnn_gamma': (1.0, 0.2),
     'L0_gnn_beta': (0.0, 0.1),
     'L0_ffn_br': (0.0, 0.1),
     'L0_ffn_b1': (0.0, 0.3),
     'L0_ffn_g1': (1.0, 0.2),
     'L0_ffn_be1': (0.0, 0.296),
     'L0_ffn_m1': (0.0, 0.1),
     'L0_ffn_v1': (1.0, 0.2),
     'L0_ffn_b2': (0.0, 0.1),
     'L0_ffn_g2': (1.0, 0.2),
     'L0_ffn_be2': (0.0, 0.1),
     'L0_ffn_m2': (0.0, 0.1),
     'L0_ffn_v2': (1.0, 0.2),
     'L0_ffn_bo': (0.0, 0.1),
     'L1_gnn_gamma0': (1.0, 0.2),
     'L1_gnn_beta0': (0.0, 0.1),
     'L1_gnn_gamma1': (1.0, 0.2),
     'L1_ffn_router_b1': (0.0, 0.1),
     'L1_ffn_router_b2': (0.0, 0.301),
     'L1_ffn_expert_b1': (0.0, 0.8),
     'L1_ffn_expert_b2': (0.0, 0.469),
     'L1_ffn_expert_b3': (0.0, 0.1)}
    factors = {'L0_gnn_b_l': 8.0, 'L1_gnn_Wsc0': 8.0, 'L1_gnn_Wsc1': 8.0}
    for name, (base, spread) in spreads.items():
        noise = np.random.default_rng([zlib.crc32(name.encode()), seed]).standard_normal(out[name].shape)
        drawn = base * np.exp(spread * noise) if base else spread * noise
        out[name] = jnp.asarray(drawn.astype(out[name].dtype))
    for name, factor in factors.items():
        out[name] = (out[name] * factor).astype(out[name].dtype)
    return out
```

```python
from contextlib import ExitStack

import concourse.bass as bass
from concourse import mybir

F32 = mybir.dt.float32
I32 = mybir.dt.int32
ALU = mybir.AluOpType
ACT = mybir.ActivationFunctionType
AX = mybir.AxisListType

P = 128
D = 256
C = 64
KK = D // P
G = 4
GE = G * P
HALF = GE // 2
SLOTS = 4
NO_NODE = 1 << 20
LN_EPS = 1e-5
CHUNK = 4


class Shared:
    pass


class Router:

    def __init__(self, w2, bias, w1=None, b1=None):
        self.w2, self.bias, self.w1, self.b1 = w2, bias, w1, b1


class Steps:

    def __init__(self, eng, sem):
        self.eng, self.sem, self.base, self.n = eng, sem, 0, 0

    def done(self, ins):
        self.n += 1
        return ins.then_inc(self.sem, 1)

    def sync(self):
        self.eng.wait_ge(self.sem, self.base + self.n)

    def enter(self, i, per):
        if self.n:
            self.base, self.n = self.base + self.n, 0
        self.start = self.base
        self.base = i * per + self.start
        self.per = per

    def leave(self, count):
        assert self.n == self.per, (self.n, self.per)
        self.base, self.n = self.start + count * self.per, 0


class Scope:

    used = []

    def __init__(self, nc, stage):
        self.nc, self.stage, self.stack = nc, stage, ExitStack()

    def __enter__(self):
        self.stack.__enter__()
        return self

    def __exit__(self, *a):
        return self.stack.__exit__(*a)

    def sb(self, name, shape, dt=F32):
        return self.stack.enter_context(self.nc.sbuf_tensor(f"{self.stage}_{name}", shape, dt))

    def ps(self, name, shape):
        return self.stack.enter_context(self.nc.psum_tensor(f"{self.stage}_{name}", shape, F32))

    def sem(self, name):
        h = self.stack.enter_context(self.nc.semaphore(f"{self.stage}_{name}"))
        self.used.append(h)
        return h

    def sems(self, name, n):
        return [self.sem(f"{name}{i}") for i in range(n)]

    def block(self):
        return self.stack.enter_context(self.nc.Block())


def clear_semaphores(nc):
    with nc.Block() as block:
        @block.gpsimd
        def _(pool):
            for h in Scope.used:
                pool.sem_clear(h)
    Scope.used.clear()


def apart(eng, sem, value, ticks):
    eng.wait_ge(sem, value)
    eng.sem_inc(ticks, 1)


def tile_loop(eng, k, body):
    assert k.NT % 2 == 1
    with eng.Fori(0, k.NT // 2) as i:
        for s in range(2):
            body(2 * i + s, s, i, False)
    body(k.NT - 1, 0, k.NT // 2, True)


def col(buf, t):
    return buf[:, bass.ds(t, 1)] if not isinstance(t, int) else buf[:, t:t + 1]


def tile_of(buf, t, a=0, b=D):
    v = buf[:, bass.ds(t, 1), a:b] if not isinstance(t, int) else buf[:, t:t + 1, a:b]
    return v.rearrange("p t d -> p (t d)")




def setup(k):
    nc, NT, NG, NI = k.nc, k.NT, k.NG, k.NI_SORTED
    EC = NG * GE // P
    with Scope(nc, "su") as s:
        dst_a, dst_b = s.sb("dst_a", [P, EC], I32), s.sb("dst_b", [P, EC], I32)
        fa, fb = s.sb("fa", [P, EC]), s.sb("fb", [P, EC])
        falls = s.sb("falls", [P, 1])
        last_i, last_f = s.sb("last_i", [1, NG], I32), s.sb("last_f", [1, NG])
        below, passed = s.sb("below", [P, NG]), s.sb("passed", [P, NI])
        bound, ended = s.sb("bound", [P, 1]), s.sb("ended", [P, 1])
        lane_i, part_i = s.sb("lane_i", [P, P], I32), s.sb("part_i", [P, 1], I32)
        item_i, item_f = s.sb("item_i", [P, NI], I32), s.sb("item_f", [P, NI])
        part = s.sb("part", [P, 1])
        blk, grp = s.sb("blk", [1, NI]), s.sb("grp", [1, NI])
        rows, meta = s.sb("rows", [1, NI, 4], I32), s.sb("meta", [1, 4], I32)
        flag, metaf = s.sb("flag", [1, 1]), s.sb("metaf", [1, 4])
        p_falls, p_last, p_blk = s.ps("p_falls", [P, 512]), s.ps("p_last", [P, 512]), s.ps("p_blk", [P, 512])
        x_in, w_in, dst_in, last_in = (s.sem(n) for n in ("x_in", "w_in", "dst_in", "last_in"))
        iota_done, zeroed, own, pe_done = (
            s.sem(n) for n in ("iota_done", "zeroed", "own", "pe_done"))
        falls_ready, last_ready, passed_ready, rows_ready = (
            s.sem(n) for n in ("falls_ready", "last_ready", "passed_ready", "rows_ready"))
        rows_out, pairs_out = s.sem("rows_out"), s.sem("pairs_out")
        block = s.block()

        @block.sync
        def _(sp):
            line = k.dst_line
            sp.dma_start(dst_a[:, :], line[0:NG * GE].rearrange("(p c) -> p c", p=P)).then_inc(dst_in, 16)
            sp.dma_start(dst_b[:, :], line[1:NG * GE + 1].rearrange("(p c) -> p c", p=P)).then_inc(dst_in, 16)
            with nc.allow_non_contiguous_dma(reason="one word of each group"):
                sp.dma_start(last_i[:, :], line[0:NG * GE].rearrange("(a g e) -> a g e", a=1, e=GE)[:, :, GE - 1]
                             ).then_inc(last_in, 16)
            sp.wait_ge(zeroed, 1)
            sp.dma_start(k.X[:, 0:NT - 1, :], k.x[0:(NT - 1) * P, :].rearrange("(t p) d -> p t d", p=P)
                         ).then_inc(x_in, 16)
            sp.dma_start(k.X[0:k.LAST, NT - 1, :], k.x[(NT - 1) * P:, :]).then_inc(x_in, 16)
            sp.wait_ge(x_in, 32)
            sp.wait_ge(rows_ready, 1)
            sp.dma_start(k.items[0:NI, :].rearrange("(a i) f -> a i f", a=1), rows[:, :, :]).then_inc(rows_out, 16)
            sp.dma_start(k.meta[:, :], meta[:, :]).then_inc(rows_out, 16)
            sp.wait_ge(rows_out, 32)

        @block.scalar
        def _(act):
            act.dma_start(k.items[NI:NI + k.NI_ALL, :].rearrange("(a b) f -> a (b f)", a=16),
                          k.all_pairs.rearrange("(a b) f -> a (b f)", a=16)).then_inc(pairs_out, 16)
            n = 0
            act.wait_ge(zeroed, 2)
            for dst, src in k.const_loads:
                act.dma_start(dst, src).then_inc(w_in, 16)
                n += 16
            for e in range(k.E0):
                for i, w in enumerate((k.W1_0, k.W2_0, k.W3_0)):
                    act.dma_start(k.WALL[:, e, i, :, :], w[e].rearrange("(kk p) n -> p kk n", p=P)).then_inc(w_in, 16)
                    n += 16
            act.wait_ge(w_in, n)
            act.wait_ge(pairs_out, 16)

        @block.gpsimd
        def _(pool):
            pool.iota(lane_i[:, :], pattern=[[1, P]], base=0, channel_multiplier=0).then_inc(iota_done, 1)
            pool.iota(part_i[:, :], pattern=[[0, 1]], base=0, channel_multiplier=1).then_inc(iota_done, 1)
            pool.iota(item_i[:, :], pattern=[[1, NI]], base=0, channel_multiplier=0).then_inc(iota_done, 1)

        @block.vector
        def _(v):
            me = Steps(v, own)
            v.memset(k.X[:, NT - 1, :], 0.0).then_inc(zeroed, 1)
            for buf in k.cleared:
                last = v.memset(buf[:], 0.0)
            last.then_inc(zeroed, 1)
            v.memset(k.ones_valid[:, :], 0.0)
            me.done(v.memset(k.ones[:, :], 1.0))
            me.sync()
            me.done(v.memset(k.ones_valid[0:k.LAST, :], 1.0))
            v.wait_ge(iota_done, 3)
            v.tensor_copy(k.lane[:, :], lane_i[:, :])
            v.tensor_copy(part[:, :], part_i[:, :])
            me.done(v.tensor_copy(item_f[:, :], item_i[:, :]))
            me.sync()
            v.tensor_scalar(k.ident[:, :], k.lane[:, :], part[:, 0:1], None, ALU.is_equal)
            me.done(v.tensor_scalar(bound[:, :], part[:, :], float(P), float(P), ALU.mult, ALU.add))
            v.wait_ge(dst_in, 32)
            v.tensor_copy(fa[:, :], dst_a[:, :])
            me.done(v.tensor_copy(fb[:, :], dst_b[:, :]))
            v.wait_ge(last_in, 16)
            me.sync()
            v.tensor_copy(last_f[:, :], last_i[:, :]).then_inc(last_ready, 1)
            me.done(v.tensor_tensor(fa[:, :], fa[:, :], fb[:, :], ALU.is_gt))
            me.sync()
            v.reduce_sum(falls[:, :], fa[:, :], AX.X).then_inc(falls_ready, 1)
            v.wait_ge(pe_done, 1)
            me.done(v.tensor_scalar(below[:, :], p_last[:, 0:NG], bound[:, 0:1], None, ALU.is_lt))
            me.sync()
            me.done(v.reduce_sum(ended[:, :], below[:, :], AX.X))
            me.sync()
            me.done(v.tensor_scalar(ended[:, :], ended[:, :], part[:, 0:1], 1.0, ALU.add, ALU.add))
            me.sync()
            v.tensor_scalar(passed[:, :], item_f[:, :], ended[:, 0:1], None, ALU.is_ge).then_inc(passed_ready, 1)
            v.wait_ge(pe_done, 3)
            me.done(v.tensor_copy(blk[:, :], p_blk[0:1, 0:NI]))
            me.done(v.tensor_scalar(flag[:, :], p_falls[0:1, 0:1], 0.5, None, ALU.is_gt))
            me.sync()
            me.done(v.tensor_tensor(grp[:, :], item_f[0:1, :], blk[:, :], ALU.subtract))
            v.tensor_scalar(metaf[:, 0:1], flag[:, :], float((k.NI_ALL - NI) // SLOTS), float(NI // SLOTS),
                            ALU.mult, ALU.add)
            v.tensor_scalar(metaf[:, 1:2], flag[:, :], float(NI), None, ALU.mult)
            me.done(v.memset(metaf[:, 2:4], 0.0))
            me.sync()
            v.tensor_scalar(rows[:, :, 0], grp[:, :], float(NG - 1), None, ALU.min)
            v.tensor_scalar(rows[:, :, 1], blk[:, :], float(NT - 1), None, ALU.min)
            v.tensor_scalar(rows[:, :, 2], blk[:, :], float(P), None, ALU.mult)
            v.tensor_scalar(rows[:, :, 3], blk[:, :], 0.0, None, ALU.mult)
            v.tensor_copy(meta[:, :], metaf[:, :]).then_inc(rows_ready, 1)
            v.wait_ge(w_in, 16 * (len(k.const_loads) + 3 * k.E0))
            batch_norm_constants(k, v, me)

        @block.tensor
        def _(pe):
            pe.wait_ge(own, 1)
            pe.wait_ge(last_ready, 1)
            pe.matmul(p_last[:, 0:NG], k.ones[0:1, :], last_f[:, :], start=True, stop=True).then_inc(pe_done, 1)
            pe.wait_ge(falls_ready, 1)
            pe.matmul(p_falls[:, 0:1], k.ones[:, :], falls[:, :], start=True, stop=True).then_inc(pe_done, 1)
            pe.wait_ge(passed_ready, 1)
            pe.matmul(p_blk[:, 0:NI], k.ones[0:NT, :], passed[0:NT, :], start=True, stop=True).then_inc(pe_done, 1)


def batch_norm_constants(k, v, me):
    for b in (k.bn1, k.bn2):
        me.done(v.tensor_scalar(b[:, 4, :], b[:, 4, :], 1e-3, None, ALU.add))
        me.done(v.tensor_tensor(b[:, 3, :], b[:, 0, :], b[:, 3, :], ALU.subtract))
    me.done(v.tensor_scalar(k.M4[:, C:2 * C], k.M4[:, C:2 * C], float(1.0 / 3.0 ** 0.5), None, ALU.mult))


def bn_roots(k):
    with Scope(k.nc, "bn") as s:
        own, rooted = s.sem("own"), s.sem("rooted")
        block = s.block()

        @block.scalar
        def _(act):
            for b in (k.bn1, k.bn2):
                act.activation(b[:, 4, :], b[:, 4, :], ACT.Sqrt).then_inc(rooted, 1)

        @block.vector
        def _(v):
            me = Steps(v, own)
            v.wait_ge(rooted, 2)
            for b in (k.bn1, k.bn2):
                me.done(v.reciprocal(b[:, 4, :], b[:, 4, :]))
            me.sync()
            for b in (k.bn1, k.bn2):
                me.done(v.tensor_tensor(b[:, 1, :], b[:, 1, :], b[:, 4, :], ALU.mult))
            me.sync()
            for b in (k.bn1, k.bn2):
                me.done(v.tensor_tensor(b[:, 3, :], b[:, 3, :], b[:, 1, :], ALU.mult))
            me.sync()
            for b in (k.bn1, k.bn2):
                me.done(v.tensor_tensor(b[:, 2, :], b[:, 2, :], b[:, 3, :], ALU.add))




def norm_stats(k, stage):
    NT = k.NT
    with Scope(k.nc, stage) as s:
        st = s.sb("st", [P, NT, 6])
        a, b = s.sb("a", [P, NT]), s.sb("b", [P, NT])
        own, var_ready, rooted = s.sem("own"), s.sem("var_ready"), s.sem("rooted")
        block = s.block()

        @block.vector
        def _(v):
            me = Steps(v, own)
            with v.Fori(0, NT) as t:
                me.enter(t, 1)
                me.done(v.bn_stats(tile_of(st, t, 0, 6), tile_of(k.X, t)))
            me.leave(NT)
            me.sync()
            me.done(v.tensor_tensor(a[:, :], st[:, :, 1], st[:, :, 4], ALU.subtract))
            me.done(v.tensor_tensor(b[:, :], st[:, :, 2], st[:, :, 5], ALU.add))
            me.done(v.tensor_tensor(k.mean[:, :], st[:, :, 1], st[:, :, 4], ALU.add))
            me.sync()
            me.done(v.tensor_tensor(a[:, :], a[:, :], a[:, :], ALU.mult))
            me.done(v.tensor_scalar(b[:, :], b[:, :], 1.0 / D, LN_EPS, ALU.mult, ALU.add))
            me.done(v.tensor_scalar(k.mean[:, :], k.mean[:, :], 0.5, None, ALU.mult))
            me.sync()
            v.scalar_tensor_tensor(out=b[:, :], in0=a[:, :], scalar=0.25, in1=b[:, :], op0=ALU.mult,
                                   op1=ALU.add).then_inc(var_ready, 1)
            v.wait_ge(rooted, 1)
            v.reciprocal(k.rstd[:, :], b[:, :])

        @block.scalar
        def _(act):
            act.wait_ge(var_ready, 1)
            act.activation(b[:, :], b[:, :], ACT.Sqrt).then_inc(rooted, 1)


def normed(k, v, t, dst, channel_major=False):
    m, r = col(k.mean, t), col(k.rstd, t)
    if not channel_major:
        return v.tensor_scalar(dst, tile_of(k.X, t), m, r, ALU.subtract, ALU.mult)
    v.tensor_scalar(dst[:, 0:C], tile_of(k.X, t, 0, C), m, r, ALU.subtract, ALU.mult)
    return v.tensor_scalar(dst[:, C:D].rearrange("p (x c) -> p x c", x=3),
                           tile_of(k.X, t, C, D).rearrange("p (c x) -> p x c", x=3), m, r, ALU.subtract, ALU.mult)


def write_xn_table(k):
    NT = k.NT
    with Scope(k.nc, "xn") as s:
        ready, stored = s.sem("ready"), s.sem("stored")
        block = s.block()

        @block.vector
        def _(v):
            with v.Fori(0, NT) as t:
                normed(k, v, t, tile_of(k.AGG, t)).then_inc(ready, 1)

        @block.sync
        def _(sp):
            with sp.Fori(0, NT) as t:
                sp.wait_ge(ready, t + 1)
                sp.dma_start(k.xn_tab[bass.ds(t * P, P), :], tile_of(k.AGG, t)).then_inc(stored, 16)
            sp.wait_ge(stored, 16 * NT)




def edge_rounds(k, eng):
    n = eng.value_load(k.meta[0:1, 0:1], min_val=k.NI_SORTED // SLOTS, max_val=k.NI_ALL // SLOTS)
    return eng.Fori(0, n)


def load_items(k, sp, edges, row, edges_in, item_done, others):
    first = sp.value_load(k.meta[0:1, 1:2], min_val=0, max_val=k.NI_SORTED)
    with edge_rounds(k, sp) as it:
        for q in range(SLOTS):
            i = it * SLOTS + q + first
            g = sp.value_load(k.items[bass.ds(i, 1), 0:1], min_val=0, max_val=k.NG - 1)
            sp.wait_ge(item_done[q], it + 1)
            sp.dma_start(row[:, q, :], k.items[bass.ds(i, 1), :].to_broadcast([P, 4])).then_inc(edges_in[q], 16)
            sp.dma_start(edges[:, q, :], k.edges[bass.ds(g, 1), :, :].rearrange("a p c -> (a p) c")
                         ).then_inc(edges_in[q], 16)
            for dst, src in others(q, g):
                sp.dma_start(dst, src).then_inc(edges_in[q], 16)


def gather_items(k, pool, table, edges, gx, edges_in, loads, gathered, ticks):
    with edge_rounds(k, pool) as it:
        for q in range(SLOTS):
            apart(pool, edges_in[q], (it + 1) * 16 * loads, ticks)
            for j in range(G):
                pool.indirect_dma_start(gx[:, q, j, 0:D], None, table,
                                        bass.IndirectOffsetOnAxis(edges[:, q, j:j + 1], 0),
                                        bounds_check=k.NT * P - 1, oob_is_err=False).then_inc(gathered[q], 16)


def choose(k, v, q, edges, row, pick, ready):
    for j in range(G):
        last = v.tensor_scalar(pick[:, q, j, :], k.lane[:, :], row[:, q, 2:3], edges[:, q, G + j:G + j + 1],
                               ALU.add, ALU.is_equal)
    last.then_inc(ready, 1)


def add_item(k, v, q, it, row, sums, width, sums_ready, credit, item_done):
    b = v.value_load(row[0:1, q, 1:2], min_val=0, max_val=k.NT - 1)
    v.wait_ge(sums_ready[q], it + 1 + credit)
    v.wait_ge(item_done[(q - 1) % SLOTS], it + (2 if q else 1))
    v.tensor_tensor(tile_of(k.AGG, b, 0, width), tile_of(k.AGG, b, 0, width), sums[:, q, 0:width],
                    ALU.add).then_inc(item_done[q], 1)


def first_edges(k):
    with Scope(k.nc, "e0") as s:
        edges, row = s.sb("edges", [P, SLOTS, 2 * G], I32), s.sb("row", [P, SLOTS, 4], I32)
        gx, pick = s.sb("gx", [P, SLOTS, G, D + 4]), s.sb("pick", [P, SLOTS, G, P])
        attr = s.sb("attr", [32, SLOTS, HALF])
        h1, h2, h3 = (s.sb(f"h{i}", [P, 2, 2 * HALF]) for i in (1, 2, 3))
        sums, hid = s.ps("sums", [P, SLOTS, 512]), s.ps("hid", [P, 2, 512])
        edges_in, item_done = s.sems("edges_in", SLOTS), s.sems("item_done", SLOTS)
        gathered = k.gathered[0]
        pick_ready, sums_ready = s.sems("pick_ready", SLOTS), s.sems("sums_ready", SLOTS)
        hid_mm, hid_act = s.sems("hid_mm", 2), s.sems("hid_act", 2)
        hid_out, pool_ticks, act_ticks, zeroed = (s.sem(n) for n in ("hid_out", "pool_ticks", "act_ticks", "zeroed"))
        block = s.block()
        NLOAD = 3

        @block.sync
        def _(sp):
            load_items(k, sp, edges, row, edges_in, item_done,
                       lambda q, g: [(attr[:, q, :], k.attr16[bass.ds(g, 1), :, :].rearrange("a p c -> (a p) c"))])

        @block.gpsimd
        def _(pool):
            gather_items(k, pool, k.xn_tab, edges, gx, edges_in, NLOAD, gathered, pool_ticks)

        @block.vector
        def _(v):
            v.memset(k.AGG[:, :, :], 0.0)
            for q in range(SLOTS):
                v.memset(gx[:, q, :, D:D + 1], 1.0).then_inc(item_done[q], 1)
            with edge_rounds(k, v) as it:
                def pick_item(q):
                    v.wait_ge(edges_in[q], (it + 1) * 16 * NLOAD)
                    choose(k, v, q, edges, row, pick, pick_ready[q])

                def add(q):
                    add_item(k, v, q, it, row, sums, D + 1, sums_ready, 0, item_done)
                pick_item(0)
                pick_item(1)
                pick_item(2)
                add(0)
                pick_item(3)
                for q in range(1, SLOTS):
                    add(q)

        @block.tensor
        def _(pe):
            with edge_rounds(k, pe) as it:
                def hidden(b, layer):
                    if layer == 0:
                        for q in (2 * b, 2 * b + 1):
                            pe.wait_ge(edges_in[q], (it + 1) * 16 * NLOAD)
                    w, x = [(k.M1, attr[:, 2 * b:2 * b + 2, :].rearrange("p q e -> p (q e)")),
                            (k.M2, h1[:, b, :]), (k.M3, h2[:, b, :])][layer]
                    pe.wait_ge(hid_act[b], it * 3 + layer + 1)
                    pe.matmul(hid[:, b, :], w[:, :], x, start=True, stop=True).then_inc(hid_mm[b], 1)

                def add_up(q):
                    pe.wait_ge(pick_ready[q], it + 1)
                    pe.wait_ge(gathered[q], (it + 1) * 16 * G)
                    for j in range(G):
                        mm = pe.matmul(sums[:, q, 0:D + 1], pick[:, q, j, :], gx[:, q, j, 0:D + 1],
                                       start=(j == 0), stop=(j == G - 1))
                    mm.then_inc(sums_ready[q], 1)
                hidden(0, 0)
                hidden(1, 0)
                hidden(0, 1)
                add_up(0)
                hidden(1, 1)
                add_up(1)
                hidden(0, 2)
                add_up(2)
                hidden(1, 2)
                add_up(3)

        @block.scalar
        def _(act):
            for b in range(2):
                act.sem_inc(hid_act[b], 1)
            with edge_rounds(k, act) as it:
                groups = []
                for layer, h in enumerate((h1, h2, h3)):
                    for b in range(2):
                        apart(act, hid_mm[b], it * 3 + layer + 1, act_ticks)
                        if layer == 0:
                            groups += [act.value_load(row[0:1, q, 0:1], min_val=0, max_val=k.NG - 1)
                                       for q in (2 * b, 2 * b + 1)]
                        act.activation(h[:, b, :], hid[:, b, :], ACT.Silu).then_inc(hid_act[b], 1)
                        if layer == 2:
                            act.wait_ge(hid_act[b], it * 3 + 4)
                            for q in (2 * b, 2 * b + 1):
                                act.dma_start(k.hidden[bass.ds(groups[q] * SLOTS + q, 1), :, :].rearrange("a p c -> (a p) c"),
                                              h3[:, b, (q % 2) * HALF:(q % 2 + 1) * HALF]).then_inc(hid_out, 16)
                apart(act, hid_out, (it + 1) * 16 * SLOTS, act_ticks)


def second_edges(k):
    with Scope(k.nc, "e1") as s:
        edges, row = s.sb("edges", [P, SLOTS, 2 * G], I32), s.sb("row", [P, SLOTS, 4], I32)
        gx, pick = s.sb("gx", [P, SLOTS, G, D]), s.sb("pick", [P, SLOTS, G, P])
        sh = s.sb("sh", [P, SLOTS, G, 4])
        hid = s.sb("hid", [P, SLOTS, HALF])
        xs = s.sb("xs", [P, 2, G, D])
        pr = s.sb("pr", [P, 2, G, 3, C])
        mb = s.sb("mb", [P, 2, G, D])
        spare = k.WALL[:, k.E1:k.E0].rearrange("p e i a n -> p (e i a n)")
        n = 2 * G * D
        ma = spare[:, 0:n].rearrange("p (r j d) -> p r j d", r=2, j=G)
        dot, t1x = (spare[:, n + i * n // 4:n + (i + 1) * n // 4].rearrange("p (r j d) -> p r j d", r=2, j=G)
                    for i in range(2))
        sums, tw = s.ps("sums", [P, SLOTS, 512]), s.ps("tw", [P, 2, G, D])
        edges_in, item_done = s.sems("edges_in", SLOTS), s.sems("item_done", SLOTS)
        gathered = k.gathered[1]
        pick_ready, sums_ready = s.sems("pick_ready", SLOTS), s.sems("sums_ready", SLOTS)
        tw_ready, xs_ready, msg_ready = s.sems("tw_ready", SLOTS), s.sems("xs_ready", SLOTS), s.sems("msg_ready", SLOTS)
        pool_ticks, own = s.sem("pool_ticks"), s.sem("own")
        block = s.block()
        NLOAD = 4
        PER = 3

        @block.sync
        def _(sp):
            load_items(k, sp, edges, row, edges_in, item_done, lambda q, g: [
                (sh[:, q, :, :].rearrange("p j f -> p (j f)"), k.attr4[bass.ds(g, 1), :, :].rearrange("a p c -> (a p) c")),
                (hid[:, q, :], k.hidden[bass.ds(g * SLOTS + q, 1), :, :].rearrange("a p c -> (a p) c"))])

        @block.gpsimd
        def _(pool):
            gather_items(k, pool, k.up_tab, edges, gx, edges_in, NLOAD, gathered, pool_ticks)

        @block.scalar
        def _(act):
            with edge_rounds(k, act) as it:
                for q in range(SLOTS):
                    act.wait_ge(msg_ready[(q - 2) % SLOTS], it + (1 if q < 2 else 2))
                    act.wait_ge(gathered[q], (it + 1) * 16 * G)
                    for j in range(G):
                        act.activation(xs[:, q % 2, j, :], gx[:, q, j, :], ACT.Copy, scale=sh[:, q, j, 0:1])
                        for x in range(3):
                            last = act.activation(pr[:, q % 2, j, x, :], gx[:, q, j, C + C * x:2 * C + C * x],
                                                  ACT.Copy, scale=sh[:, q, j, 1 + x:2 + x])
                    last.then_inc(xs_ready[q], 1)

        @block.vector
        def _(v):
            me = Steps(v, own)
            for q in range(SLOTS):
                v.sem_inc(msg_ready[q], 1)
            for q in range(SLOTS):
                v.memset(k.AGG[:, :, q * D // SLOTS:(q + 1) * D // SLOTS], 0.0).then_inc(item_done[q], 1)
            with edge_rounds(k, v) as it:
                me.enter(it, PER * SLOTS)

                def messages(q):
                    r = q % 2
                    t0, t3, t1, t2 = (tw[:, r, :, C * i:C * i + C] for i in range(4))
                    v.wait_ge(edges_in[q], (it + 1) * 16 * NLOAD)
                    choose(k, v, q, edges, row, pick, pick_ready[q])
                    v.wait_ge(xs_ready[q], it + 1)
                    v.wait_ge(sums_ready[(q - 2) % SLOTS], it + (1 if q < 2 else 2))
                    me.done(v.tensor_tensor(dot[:, r], pr[:, r, :, 0, :], pr[:, r, :, 1, :], ALU.add))
                    v.wait_ge(tw_ready[q], it + 1)
                    v.tensor_tensor(ma[:, r, :, 0:C], t0, xs[:, r, :, 0:C], ALU.mult)
                    me.done(v.tensor_tensor(t1x[:, r], t1, gx[:, q, :, 0:C], ALU.mult))
                    me.sync()
                    me.done(v.tensor_tensor(dot[:, r], dot[:, r], pr[:, r, :, 2, :], ALU.add))
                    v.tensor_tensor(ma[:, r, :, C:D].rearrange("p j (x c) -> p j x c", x=3),
                                    t2.unsqueeze(2).to_broadcast([P, G, 3, C]),
                                    xs[:, r, :, C:D].rearrange("p j (x c) -> p j x c", x=3), ALU.mult)
                    v.tensor_tensor(mb[:, r, :, C:D].rearrange("p j (x c) -> p j x c", x=3),
                                    t1x[:, r].unsqueeze(2).to_broadcast([P, G, 3, C]),
                                    sh[:, q, :, 1:4].unsqueeze(3).to_broadcast([P, G, 3, C]), ALU.mult)
                    me.sync()
                    v.tensor_tensor(mb[:, r, :, 0:C], t3, dot[:, r], ALU.mult).then_inc(msg_ready[q], 1)

                def add(q):
                    add_item(k, v, q, it, row, sums, D, sums_ready, 1, item_done)
                messages(0)
                messages(1)
                add(0)
                messages(2)
                add(1)
                messages(3)
                add(2)
                add(3)
            me.leave(0)

        @block.tensor
        def _(pe):
            for q in range(SLOTS):
                pe.sem_inc(sums_ready[q], 1)
            with edge_rounds(k, pe) as it:
                def weights(q):
                    r = q % 2
                    pe.wait_ge(edges_in[q], (it + 1) * 16 * NLOAD)
                    pe.wait_ge(msg_ready[(q - 2) % SLOTS], it + (1 if q < 2 else 2))
                    for j in (0, 2, 1, 3):
                        h, o = j // 2 * C, j % 2 * P
                        mm = pe.matmul(tw[:, r, j, :], hid[h:h + C, q, o:o + P], k.M4[h:h + C, :],
                                       start=True, stop=True)
                    mm.then_inc(tw_ready[q], 1)

                def add_up(q):
                    r = q % 2
                    pe.wait_ge(pick_ready[q], it + 1)
                    pe.wait_ge(msg_ready[q], it + 2)
                    for j in range(G):
                        pe.matmul(sums[:, q, 0:D], pick[:, q, j, :], ma[:, r, j, :], start=(j == 0), stop=False)
                        mm = pe.matmul(sums[:, q, 0:D], pick[:, q, j, :], mb[:, r, j, :], start=False,
                                       stop=(j == G - 1))
                    mm.then_inc(sums_ready[q], 1)
                weights(0)
                weights(1)
                add_up(0)
                weights(2)
                add_up(1)
                weights(3)
                add_up(2)
                add_up(3)




def node_product(k, stage, chunks, fill, plan, evacuate, store=None):
    NT = k.NT
    with Scope(k.nc, stage) as s:
        cat = s.sb("cat", [P, 2, chunks * P])
        catT = s.sb("catT", [P, 2, chunks, P])
        junk = s.sb("junk", [P, 2, D])
        p_t, p_o = s.ps("p_t", [P, 2, 512]), s.ps("p_o", [P, 2, 512])
        filled, turned, copied, product, taken = (s.sems(n, 2) for n in ("filled", "turned", "copied", "product", "taken"))
        ticks, stored = s.sem("ticks"), s.sem("stored")
        block = s.block()

        @block.vector
        def _(v):
            def body(t, b, i, last):
                v.wait_ge(turned[b], i + 1)
                fill(v, t, cat[:, b, :]).then_inc(filled[b], 1)
                v.wait_ge(turned[b], i + 2)
                v.wait_ge(product[b], i + 1)
                v.tensor_copy(catT[:, b], p_t[:, b, 0:chunks * P].rearrange("p (a c) -> p a c", c=P)
                              ).then_inc(copied[b], 1)
            tile_loop(v, k, body)

        @block.tensor
        def _(pe):
            for b in range(2):
                pe.sem_inc(turned[b], 1)
                pe.sem_inc(product[b], 1)

            def body(t, b, i, last):
                pe.wait_ge(filled[b], i + 1)
                for a in range(chunks):
                    mm = pe.transpose(p_t[:, b, a * P:(a + 1) * P], cat[:, b, a * P:(a + 1) * P], k.ident[:, :])
                mm.then_inc(turned[b], 1)
                pe.wait_ge(copied[b], i + 1)
                pe.wait_ge(taken[b], i + 1)
                for n, (a, w, c0, cn) in enumerate(plan):
                    same = [m for m, x in enumerate(plan) if x[2] == c0]
                    lhs = k.ones[0:1, :] if a is None else catT[:, b, a, :]
                    mm = pe.matmul(p_o[:, b, c0:c0 + cn], lhs, w, start=(n == same[0]), stop=(n == same[-1]))
                mm.then_inc(product[b], 1)
            tile_loop(pe, k, body)

        @block.scalar
        def _(act):
            for b in range(2):
                act.sem_inc(taken[b], 1)

            def body(t, b, i, last):
                apart(act, product[b], i + 2, ticks)
                evacuate(act, t, p_o[:, b, 0:D], junk[:, b, :]).then_inc(taken[b], 1)
            tile_loop(act, k, body)

        if store is not None:
            @block.sync
            def _(sp):
                def body(t, b, i, last):
                    sp.wait_ge(taken[b], i + 2)
                    sp.dma_start(store[bass.ds(t * P, P), :], tile_of(k.AGG, t)).then_inc(stored, 16)
                tile_loop(sp, k, body)
                sp.wait_ge(stored, 16 * NT)


def keep(k):
    return lambda act, t, ps, junk: act.activation(tile_of(k.AGG, t), ps, ACT.Copy)


def first_linear(k):
    with Scope(k.nc, "l0d") as s:
        block = s.block()
        own = s.sem("own")

        @block.vector
        def _(v):
            me = Steps(v, own)
            me.done(v.tensor_scalar(k.rdeg[:, :], k.AGG[:, :, D], 1.0, None, ALU.max))
            me.sync()
            me.done(v.reciprocal(k.rdeg[:, :], k.rdeg[:, :]))

    def fill(v, t, dst):
        v.tensor_scalar(dst[:, 0:D], tile_of(k.AGG, t), col(k.rdeg, t), None, ALU.mult)
        return normed(k, v, t, dst[:, D:2 * D])

    def evacuate(act, t, ps, junk):
        act.activation(tile_of(k.AGG, t), ps, ACT.Copy)
        return act.activation(junk, ps, ACT.Square, accum_out=col(k.ssq, t))

    plan = [(a, (k.WlT if a < KK else k.WrT)[:, a % KK, :], 0, D) for a in range(2 * KK)]
    plan.append((None, k.b_l[0:1, :], 0, D))
    node_product(k, "l0", 2 * KK, fill, plan, evacuate)


def diagonal_plan(first, w):
    return [(first + h, w[:, h, :], h * P, P) for h in range(KK)]


def scale_rows(k):
    with Scope(k.nc, "l2") as s:
        own, rooted = s.sem("own"), s.sem("rooted")
        block = s.block()

        @block.scalar
        def _(act):
            act.activation(k.ssq[:, :], k.ssq[:, :], ACT.Sqrt).then_inc(rooted, 1)

        @block.vector
        def _(v):
            me = Steps(v, own)
            v.wait_ge(rooted, 1)
            me.done(v.tensor_scalar(k.ssq[:, :], k.ssq[:, :], 1e-12, None, ALU.max))
            me.sync()
            me.done(v.reciprocal(k.ssq[:, :], k.ssq[:, :]))
            me.sync()
            with v.Fori(0, k.NT) as t:
                v.tensor_scalar(tile_of(k.AGG, t), tile_of(k.AGG, t), col(k.ssq, t), None, ALU.mult)


def column_stats(k, stage, n):
    NT, r = k.NT, D - n
    with Scope(k.nc, stage) as s:
        sq = s.sb("sq", [P, 2, D])
        mu = s.sb("mu", [P, D])
        p_m, p_s = s.ps("p_m", [P, 512]), s.ps("p_s", [P, 512])
        summed, mu_ready, centred, var_ready, rooted, own, ticks = (
            s.sem(x) for x in ("summed", "mu_ready", "centred", "var_ready", "rooted", "own", "ticks"))
        squared, added = s.sems("squared", 2), s.sems("added", 2)
        block = s.block()

        def ones(last):
            return (k.ones_valid if last else k.ones)[:, :]

        @block.tensor
        def _(pe):
            def first(t, b, i, last):
                pe.matmul(p_m[:, 0:n], ones(last), tile_of(k.AGG, t, 0, n), start=False, stop=last)
            pe.matmul(p_m[:, 0:n], k.zeros[:, :], k.X[:, 0, 0:n], start=True, stop=False)
            tile_loop(pe, k, first)
            pe.matmul(p_m[:, 0:1], k.zeros[:, :], k.X[:, 0, 0:1], start=False, stop=True,
                      skip_group_check=True).then_inc(summed, 1)
            for b in range(2):
                pe.sem_inc(added[b], 1)

            def second(t, b, i, last):
                pe.wait_ge(squared[b], i + 1)
                pe.matmul(p_s[:, 0:D], ones(last), sq[:, b, :], start=False, stop=last).then_inc(added[b], 1)
            pe.matmul(p_s[:, 0:D], k.zeros[:, :], k.X[:, 0, 0:D], start=True, stop=False)
            tile_loop(pe, k, second)

        @block.vector
        def _(v):
            me = Steps(v, own)
            v.wait_ge(summed, 1)
            me.done(v.tensor_scalar(mu[:, 0:n], p_m[:, 0:n], 1.0 / k.N, None, ALU.mult))
            me.sync()
            with v.Fori(0, NT) as t:
                v.tensor_tensor(tile_of(k.AGG, t, 0, n), tile_of(k.AGG, t, 0, n), mu[:, 0:n],
                                ALU.subtract).then_inc(centred, 1)
            v.wait_ge(added[0], NT // 2 + 2)
            if r:
                me.done(v.tensor_copy(mu[:, n:D], p_s[:, n:D]))
                me.sync()
                me.done(v.tensor_tensor(mu[:, n:n + C], mu[:, n:n + C], mu[:, n + C:n + 2 * C], ALU.add))
                me.sync()
                me.done(v.tensor_tensor(mu[:, n:n + C], mu[:, n:n + C], mu[:, n + 2 * C:D], ALU.add))
                me.sync()
                me.done(v.tensor_scalar(k.cscale[:, n:D].rearrange("p (x c) -> p x c", c=C),
                                        mu[:, n:n + C].unsqueeze(1).to_broadcast([P, 3, C]),
                                        1.0 / (3 * k.N), 1e-5, ALU.mult, ALU.add))
            me.done(v.tensor_scalar(k.cscale[:, 0:n], p_s[:, 0:n], 1.0 / k.N, 1e-5, ALU.mult, ALU.add)
                    )
            me.sync()
            v.sem_inc(var_ready, 1)
            v.wait_ge(rooted, 1)
            me.done(v.reciprocal(k.cscale[:, :], k.cscale[:, :]))

        @block.scalar
        def _(act):
            def body(t, b, i, last):
                apart(act, centred, t + 1, ticks)
                apart(act, added[b], i + 1, ticks)
                act.activation(sq[:, b, :], tile_of(k.AGG, t), ACT.Square).then_inc(squared[b], 1)
            tile_loop(act, k, body)
            act.wait_ge(var_ready, 1)
            act.activation(k.cscale[:, :], k.cscale[:, :], ACT.Sqrt).then_inc(rooted, 1)


def add_normed(k, stage, gamma, beta, n, relu, channel_major):
    with Scope(k.nc, stage) as s:
        own = s.sem("own")
        block = s.block()

        @block.vector
        def _(v):
            me = Steps(v, own)
            me.done(v.tensor_tensor(k.cscale[:, :], k.cscale[:, :], gamma, ALU.mult))
            me.sync()

            def body(tiles, i, per):
                me.enter(i, per)
                for t in tiles:
                    me.done(v.tensor_tensor(tile_of(k.AGG, t), tile_of(k.AGG, t), k.cscale[:, :], ALU.mult))
                me.sync()
                for t in tiles:
                    me.done(v.tensor_tensor(tile_of(k.AGG, t, 0, n), tile_of(k.AGG, t, 0, n), beta, ALU.add))
                me.sync()
                for t in tiles:
                    if relu:
                        me.done(v.scalar_tensor_tensor(out=tile_of(k.X, t), in0=tile_of(k.AGG, t), scalar=0.0,
                                                       in1=tile_of(k.X, t), op0=ALU.max, op1=ALU.add))
                    elif channel_major:
                        me.done(v.tensor_tensor(tile_of(k.X, t, 0, C), tile_of(k.AGG, t, 0, C),
                                                tile_of(k.X, t, 0, C), ALU.add))
                        xv = tile_of(k.X, t, C, D).rearrange("p (c x) -> p x c", x=3)
                        me.done(v.tensor_tensor(xv, tile_of(k.AGG, t, C, D).rearrange("p (x c) -> p x c", x=3),
                                                xv, ALU.add))
            per = 3 if relu else 4
            with v.Fori(0, k.NT // 2) as i:
                body((2 * i, 2 * i + 1), i, 2 * per)
            me.leave(k.NT // 2)
            body((k.NT - 1,), 0, per)


def polynomial(k):
    NB = 7
    assert k.NT % NB == 0
    with Scope(k.nc, "po") as s:
        vv, sq3 = s.sb("vv", [P, NB, C]), s.sb("sq3", [P, NB, 3, C])
        a2 = s.sb("a2", [P, NB, C])
        f, g = s.sb("f", [P, NB, 2, C]), s.sb("g", [P, NB, 2, C])
        own, squared, used, ticks = s.sem("own"), s.sem("squared"), s.sem("used"), s.sem("ticks")
        block = s.block()

        def b(x):
            return x.unsqueeze(1).to_broadcast([P, NB] + list(x.shape[1:]))

        def two(x):
            return x.unsqueeze(2).to_broadcast([P, NB, 2, C])

        @block.scalar
        def _(act):
            with act.Fori(0, k.NT // NB) as i:
                apart(act, used, i + 1, ticks)
                act.activation(sq3[:, :, :, :].rearrange("p t x c -> p t (x c)"), k.AGG[:, bass.ds(i * NB, NB), C:D],
                               ACT.Square).then_inc(squared, 1)

        @block.vector
        def _(v):
            me = Steps(v, own)
            v.sem_inc(used, 1)
            with v.Fori(0, k.NT // NB) as i:
                me.enter(i, 11)
                A0 = k.AGG[:, bass.ds(i * NB, NB), 0:C]
                A1 = k.AGG[:, bass.ds(i * NB, NB), C:D].rearrange("p t (x c) -> p t x c", x=3)
                v.wait_ge(used, i + 1)
                me.done(v.tensor_tensor(a2[:, :, :], A0, A0, ALU.mult))
                me.done(v.tensor_tensor(f[:, :, :, :], two(A0), b(k.poly[:, 1]), ALU.mult))
                v.wait_ge(squared, i + 1)
                me.done(v.tensor_tensor(vv[:, :, :], sq3[:, :, 0, :], sq3[:, :, 1, :], ALU.add))
                me.sync()
                me.done(v.tensor_tensor(vv[:, :, :], vv[:, :, :], sq3[:, :, 2, :], ALU.add))
                me.done(v.tensor_tensor(g[:, :, :, :], two(a2[:, :, :]), b(k.poly[:, 2]), ALU.mult))
                me.done(v.tensor_tensor(f[:, :, :, :], f[:, :, :, :], b(k.poly[:, 0]), ALU.add))
                me.sync()
                me.done(v.tensor_tensor(f[:, :, :, :], f[:, :, :, :], g[:, :, :, :], ALU.add))
                me.sync()
                me.done(v.tensor_tensor(g[:, :, :, :], two(vv[:, :, :]), b(k.poly[:, 3]), ALU.mult))
                me.sync()
                me.done(v.tensor_tensor(f[:, :, :, :], f[:, :, :, :], g[:, :, :, :], ALU.add))
                me.done(v.tensor_tensor(a2[:, :, :], vv[:, :, :], b(k.poly_vv[:, :]), ALU.mult))
                me.sync()
                me.done(v.tensor_tensor(A0, A0, f[:, :, 0, :], ALU.mult))
                v.tensor_tensor(A1, A1, f[:, :, 1, :].unsqueeze(2).to_broadcast([P, NB, 3, C]), ALU.mult)
                me.sync()
                v.tensor_tensor(A0, A0, a2[:, :, :], ALU.add).then_inc(used, 1)
            me.leave(k.NT // NB)




def load_experts(k):
    with Scope(k.nc, "lw") as s:
        w_in = s.sem("w_in")
        block = s.block()

        @block.sync
        def _(sp):
            for e in range(k.E1):
                for i, w in enumerate((k.W1_1, k.W2_1, k.W3_1)):
                    sp.dma_start(k.WALL[:, e, i, :, :], w[e].rearrange("(kk p) n -> p kk n", p=P)).then_inc(w_in, 16)
            sp.wait_ge(w_in, 16 * 3 * k.E1)


def experts(k, stage, E, scales, biases, last_bias, top2, router, out=None):
    NT = k.NT
    full, rest = NT // CHUNK, NT % CHUNK
    with Scope(k.nc, stage) as s:
        xn, xT = s.sb("xn", [P, CHUNK, D]), s.sb("xT", [P, KK, CHUNK * P])
        h1, h2 = s.sb("h1", [P, 2, KK, CHUNK * P]), s.sb("h2", [P, 2, KK, CHUNK * P])
        rT = s.sb("rT", [P, CHUNK * P]) if top2 else None
        lg, ex, wt = (s.sb(n, [P, CHUNK, E]) for n in ("lg", "ex", "wt"))
        r1, r2, r3, r4 = (s.sb(n, [P, CHUNK, 1]) for n in ("r1", "r2", "r3", "r4"))
        s1, s2 = s.sb("s1", [P, CHUNK, E]), s.sb("s2", [P, CHUNK, E])
        wT = s.sb("wT", [E, CHUNK * P])
        p_x, p_1, p_2, p_y = (s.ps(n, [P, 2, 512]) for n in ("p_x", "p_1", "p_2", "p_y"))
        xn_ready, turned, xT_v, xT_a, r_mm, r_act, l_mm, ex_in, ex_out, w_ready, wT_mm, wT_v = (
            s.sem(n) for n in ("xn_ready", "turned", "xT_v", "xT_a", "r_mm", "r_act", "l_mm", "ex_in", "ex_out",
                               "w_ready", "wT_mm", "wT_v"))
        h1_mm, h1_act, h2_mm, h2_act, y_mm, y_added, own, stored = (
            s.sem(n) for n in ("h1_mm", "h1_act", "h2_mm", "h2_act", "y_mm", "y_added", "own", "stored"))
        block = s.block()
        w = k.WALL

        def chunks(eng, body, me=None, per=0):
            with eng.Fori(0, full) as c:
                if me:
                    me.enter(c, per)
                body(c, CHUNK)
            if me:
                me.leave(full)
                me.enter(0, per)
            if rest:
                body(full, rest)

        @block.vector
        def _(v):
            me = Steps(v, own)

            def body(c, nt):
                W = nt * P
                v.wait_ge(turned, c + 1)
                for j in range(nt):
                    last = normed(k, v, c * CHUNK + j, xn[:, j, :])
                last.then_inc(xn_ready, 1)
                v.wait_ge(turned, c + 2)
                v.tensor_copy(xT[:, 0, 0:W], p_x[:, 0, 0:W]).then_inc(xT_v, 1)
                L, X_, W_ = lg[:, 0:nt, :], ex[:, 0:nt, :], wt[:, 0:nt, :]
                a, b, c3, d = (r[:, 0:nt, :] for r in (r1, r2, r3, r4))
                S1, S2 = s1[:, 0:nt, :], s2[:, 0:nt, :]

                def wide(r):
                    return r.to_broadcast([P, nt, E])
                rb = router.bias.unsqueeze(1).to_broadcast([P, nt, E])
                v.wait_ge(l_mm, c + 1)
                me.done(v.tensor_tensor(L, p_x[:, 0, 0:nt * E].rearrange("p (j e) -> p j e", e=E), rb, ALU.add))
                me.sync()
                me.done(v.tensor_reduce(a, L, AX.X, ALU.max))
                me.sync()
                me.done(v.tensor_tensor(L, L, wide(a), ALU.subtract))
                me.sync()
                v.sem_inc(ex_in, 1)
                v.wait_ge(ex_out, c * (2 if top2 else 1) + 1)
                me.done(v.tensor_reduce(a, X_, AX.X, ALU.add))
                me.sync()
                me.done(v.reciprocal(b, a))
                me.sync()
                if not top2:
                    me.done(v.tensor_tensor(W_, X_, wide(b), ALU.mult))
                    me.sync()
                    v.sem_inc(w_ready, 1)
                else:
                    rank = k.rank[:, 0:E].unsqueeze(1).to_broadcast([P, nt, E])
                    me.done(v.tensor_tensor(L, X_, wide(b), ALU.mult))
                    me.sync()
                    for top, S in ((c3, S1), (d, S2)):
                        me.done(v.tensor_reduce(top, L, AX.X, ALU.max))
                        me.sync()
                        me.done(v.tensor_tensor(S, L, wide(top), ALU.is_equal))
                        me.sync()
                        me.done(v.tensor_tensor(S, S, rank, ALU.mult))
                        me.sync()
                        me.done(v.tensor_reduce(a, S, AX.X, ALU.max))
                        me.sync()
                        me.done(v.tensor_tensor(S, S, wide(a), ALU.is_equal))
                        me.sync()
                        if S is S1:
                            me.done(v.scalar_tensor_tensor(out=L, in0=S, scalar=-2.0, in1=L, op0=ALU.mult, op1=ALU.add))
                            me.sync()
                    me.done(v.tensor_tensor(a, d, c3, ALU.subtract))
                    me.sync()
                    v.sem_inc(ex_in, 1)
                    v.wait_ge(ex_out, c * 2 + 2)
                    me.done(v.tensor_scalar(b, d, 1.0, None, ALU.add))
                    me.sync()
                    me.done(v.reciprocal(b, b))
                    me.sync()
                    me.done(v.tensor_tensor(d, d, b, ALU.mult))
                    me.done(v.tensor_tensor(S1, S1, wide(b), ALU.mult))
                    me.sync()
                    me.done(v.tensor_tensor(S2, S2, wide(d), ALU.mult))
                    me.sync()
                    me.done(v.tensor_tensor(W_, S1, S2, ALU.add))
                    me.sync()
                    v.sem_inc(w_ready, 1)
                v.wait_ge(wT_mm, c + 1)
                v.tensor_copy(wT[:, 0:W], p_x[0:E, 1, 0:W]).then_inc(wT_v, 1)
                for e in range(-1, E):
                    v.wait_ge(y_mm, c * (E + 1) + e + 2)
                    if e >= 0:
                        v.wait_ge(y_added, c * (E + 1) + e + 2)
                    for j in range(nt):
                        y = p_y[:, j // 2, j % 2 * D:(j % 2 + 1) * D]
                        xt = tile_of(k.X, c * CHUNK + j)
                        if e < 0:
                            last = v.tensor_tensor(xt, y, xt, ALU.add)
                        else:
                            last = v.scalar_tensor_tensor(out=xt, in0=y, scalar=wt[:, j, e:e + 1], in1=xt,
                                                          op0=ALU.mult, op1=ALU.add)
                    last.then_inc(y_added, 1)
            v.sem_inc(y_added, 1)
            chunks(v, body, me, 6 if not top2 else 5 + 1 + 11 + 1 + 6)

        @block.scalar
        def _(act):
            act.sem_inc(h1_act, 2)
            act.sem_inc(h2_act, 2)

            def relu(dst, src, l, e, m):
                scale = scales[l][:, 2 * e + m:2 * e + m + 1] if scales else 1.0
                return act.activation(dst, src, ACT.Relu, bias=biases[l][:, 2 * e + m:2 * e + m + 1], scale=scale)

            def body(c, nt):
                W = nt * P
                act.wait_ge(turned, c + 2)
                act.activation(xT[:, 1, 0:W], p_x[:, 1, 0:W], ACT.Copy).then_inc(xT_a, 1)
                if top2:
                    act.wait_ge(r_mm, c + 1)
                    act.activation(rT[:, 0:W], p_x[:, 1, 0:W], ACT.Relu, bias=router.b1).then_inc(r_act, 1)
                act.wait_ge(ex_in, c * (2 if top2 else 1) + 1)
                act.activation(ex[:, 0:nt, :], lg[:, 0:nt, :], ACT.Exp).then_inc(ex_out, 1)
                for st in range(E + 1):
                    if st < E:
                        for m in range(2):
                            act.wait_ge(h1_mm, c * 2 * E + 2 * st + m + 1)
                            relu(h1[:, st % 2, m, 0:W], p_1[:, m, 0:W], 0, st, m).then_inc(h1_act, 1)
                    if st == 0 and top2:
                        act.wait_ge(ex_in, c * 2 + 2)
                        act.activation(r4[:, 0:nt, :], r1[:, 0:nt, :], ACT.Exp).then_inc(ex_out, 1)
                    if st >= 1:
                        for m in range(2):
                            act.wait_ge(h2_mm, c * 2 * E + 2 * (st - 1) + m + 1)
                            relu(h2[:, (st - 1) % 2, m, 0:W], p_2[:, m, 0:W], 1, st - 1, m).then_inc(h2_act, 1)
            chunks(act, body)

        @block.tensor
        def _(pe):
            pe.sem_inc(turned, 1)

            def body(c, nt):
                W = nt * P
                pe.wait_ge(xn_ready, c + 1)
                for kk in range(KK):
                    for j in range(nt):
                        mm = pe.transpose(p_x[:, kk, j * P:(j + 1) * P], xn[:, j, kk * P:(kk + 1) * P], k.ident[:, :])
                mm.then_inc(turned, 1)
                pe.wait_ge(xT_v, c + 1)
                pe.wait_ge(xT_a, c + 1)
                if top2:
                    for kk in range(KK):
                        mm = pe.matmul(p_x[:, 1, 0:W], router.w1[:, kk, :], xT[:, kk, 0:W], start=(kk == 0),
                                       stop=(kk == KK - 1))
                    mm.then_inc(r_mm, 1)
                    pe.wait_ge(r_act, c + 1)
                    for j in range(nt):
                        mm = pe.matmul(p_x[:, 0, j * E:(j + 1) * E], rT[:, j * P:(j + 1) * P], router.w2[:, :],
                                       start=True, stop=True)
                else:
                    for j in range(nt):
                        for kk in range(KK):
                            mm = pe.matmul(p_x[:, 0, j * E:(j + 1) * E], xT[:, kk, j * P:(j + 1) * P],
                                           router.w2[:, kk, :], start=(kk == 0), stop=(kk == KK - 1))
                mm.then_inc(l_mm, 1)

                def layer1(e):
                    for m in range(2):
                        pe.wait_ge(h1_act, c * 2 * E + 2 * e + m + 1)
                        for kk in range(KK):
                            mm = pe.matmul(p_1[:, m, 0:W], w[:, e, 0, kk, m * P:(m + 1) * P], xT[:, kk, 0:W],
                                           start=(kk == 0), stop=(kk == KK - 1))
                        mm.then_inc(h1_mm, 1)

                def layer2(e):
                    pe.wait_ge(h1_act, c * 2 * E + 2 * e + 4)
                    for m in range(2):
                        pe.wait_ge(h2_act, c * 2 * E + 2 * e + m + 1)
                        for kk in range(KK):
                            mm = pe.matmul(p_2[:, m, 0:W], w[:, e, 1, kk, m * P:(m + 1) * P], h1[:, e % 2, kk, 0:W],
                                           start=(kk == 0), stop=(kk == KK - 1))
                        mm.then_inc(h2_mm, 1)

                def layer3(e):
                    pe.wait_ge(h2_act, c * 2 * E + 2 * e + 4)
                    pe.wait_ge(y_added, c * (E + 1) + e + 2)
                    for j in range(nt):
                        for kk in range(KK):
                            mm = pe.matmul(p_y[:, j // 2, j % 2 * D:(j % 2 + 1) * D],
                                           h2[:, e % 2, kk, j * P:(j + 1) * P], w[:, e, 2, kk, :],
                                           start=(kk == 0), stop=(kk == KK - 1))
                    mm.then_inc(y_mm, 1)

                for st in range(E + 2):
                    if st < E:
                        layer1(st)
                    if 0 <= st - 1 < E:
                        layer2(st - 1)
                    if st == 1:
                        pe.wait_ge(w_ready, c + 1)
                        for j in range(nt):
                            mm = pe.transpose(p_x[0:E, 1, j * P:(j + 1) * P], wt[:, j, :], k.ident[:, :])
                        mm.then_inc(wT_mm, 1)
                        pe.wait_ge(wT_v, c + 1)
                        pe.wait_ge(y_added, c * (E + 1) + 1)
                        for j in range(nt):
                            mm = pe.matmul(p_y[:, j // 2, j % 2 * D:(j % 2 + 1) * D], wT[:, j * P:(j + 1) * P],
                                           last_bias, start=True, stop=True)
                        mm.then_inc(y_mm, 1)
                    if 0 <= st - 2 < E:
                        layer3(st - 2)
            chunks(pe, body)

        if out is not None:
            @block.sync
            def _(sp):
                with sp.Fori(0, full) as c:
                    sp.wait_ge(y_added, (c + 1) * (E + 1) + 1)
                    sp.dma_start(out[bass.ds(c * CHUNK * P, CHUNK * P), :].rearrange("(j p) d -> p j d", p=P),
                                 k.X[:, bass.ds(c * CHUNK, CHUNK), :]).then_inc(stored, 16)
                n = full
                sp.wait_ge(y_added, (full + (1 if rest else 0)) * (E + 1) + 1)
                for t in range(full * CHUNK, NT):
                    rows = P if t < NT - 1 else k.LAST
                    sp.dma_start(out[t * P:t * P + rows, :], k.X[0:rows, t, :]).then_inc(stored, 16)
                    n += 1
                sp.wait_ge(stored, 16 * n)




def program(nc, a, out):
    Scope.used.clear()
    k = Shared()
    k.nc = nc
    k.N = a["x"].shape[0]
    k.NT = -(-k.N // P)
    k.LAST = k.N - (k.NT - 1) * P
    k.NG = a["edges"].shape[0]
    k.NI_SORTED = -(-(k.NG + k.NT - 1) // SLOTS) * SLOTS
    k.NI_ALL = a["all_pairs"].shape[0]
    k.E0, k.E1 = a["L0_ffn_W1"].shape[0], a["L1_ffn_expert_w1"].shape[0]
    NT = k.NT
    k.x, k.edges, k.dst_line, k.all_pairs = a["x"], a["edges"], a["dst_line"], a["all_pairs"]
    k.attr16, k.attr4 = a["attr16"], a["attr4"]
    k.W1_0, k.W2_0, k.W3_0 = a["L0_ffn_W1"], a["L0_ffn_W2"], a["L0_ffn_Wo"]
    k.W1_1, k.W2_1, k.W3_1 = a["L1_ffn_expert_w1"], a["L1_ffn_expert_w2"], a["L1_ffn_expert_w3"]
    k.items = nc.dram_tensor("items", (k.NI_SORTED + k.NI_ALL, 4), I32).ap()
    k.meta = nc.dram_tensor("meta", (1, 4), I32).ap()
    k.xn_tab = nc.dram_tensor("xn_tab", (NT * P, D), F32).ap()
    k.up_tab = nc.dram_tensor("up_tab", (NT * P, D), F32).ap()
    k.hidden = nc.dram_tensor("hidden", (k.NG * SLOTS, P, HALF), F32).ap()

    with Scope(nc, "g") as s:
        k.X, k.AGG = s.sb("X", [P, NT, D]), s.sb("AGG", [P, NT, D + 1])
        k.mean, k.rstd, k.rdeg, k.ssq = (s.sb(n, [P, NT]) for n in ("mean", "rstd", "rdeg", "ssq"))
        k.lane, k.ident, k.ones, k.ones_valid, k.zeros = (
            s.sb(n, [P, P]) for n in ("lane", "ident", "ones", "ones_valid", "zeros"))
        k.cscale = s.sb("cscale", [P, D])
        k.b_l = s.sb("b_l", [1, D])
        k.M4 = s.sb("M4", [P, D])
        k.bn1, k.bn2 = s.sb("bn1", [P, 5, 2 * k.E0]), s.sb("bn2", [P, 5, 2 * k.E0])
        bo0, br0, wr0 = s.sb("bo0", [k.E0, D]), s.sb("br0", [P, k.E0]), s.sb("wr0", [P, KK, k.E0])
        bo1, rb2, rb1 = s.sb("bo1", [k.E1, D]), s.sb("rb2", [P, k.E1]), s.sb("rb1", [P, 1])
        rw1, rw2 = s.sb("rw1", [P, KK, P]), s.sb("rw2", [P, k.E1])
        eb1, eb2 = s.sb("eb1", [P, 2 * k.E1]), s.sb("eb2", [P, 2 * k.E1])
        k.rank = s.sb("rank", [P, 8])
        k.WALL = s.sb("WALL", [P, k.E0, 3, KK, D])

        k.gathered = s.sems("gathered_a", SLOTS), s.sems("gathered_b", SLOTS)
        Scope.used.clear()

        def rows(x):
            return x.rearrange("(kk p) n -> p kk n", p=P)

        def spread(x, n):
            return x.rearrange("(a d) -> a d", a=1).to_broadcast([P, n])

        loads = [(k.b_l[:, :], a["L0_gnn_b_l"].rearrange("(a d) -> a d", a=1)),
                 (bo0[:, :], a["L0_ffn_bo"]), (br0[:, :], spread(a["L0_ffn_br"], k.E0)),
                 (wr0[:, :, :], rows(a["L0_ffn_Wr"])),
                 (bo1[:, :], a["L1_ffn_expert_b3"]), (rb2[:, :], spread(a["L1_ffn_router_b2"], k.E1)),
                 (rb1[:, :], a["L1_ffn_router_b1"].rearrange("(p a) -> p a", a=1)),
                 (rw1[:, :, :], rows(a["L1_ffn_router_w1"])), (rw2[:, :], a["L1_ffn_router_w2"]),
                 (eb1[:, :], a["L1_ffn_expert_b1"]), (eb2[:, :], a["L1_ffn_expert_b2"]),
                 (k.rank[:, :], a["rank"].to_broadcast([P, 8]))]
        for bn, which in ((k.bn1, "1"), (k.bn2, "2")):
            for i, n in enumerate(("b", "g", "be", "m", "v")):
                loads.append((bn[:, i, :], a[f"L0_ffn_{n}{which}"]))
        for h in range(2):
            for to, of in enumerate((0, 3, 1, 2)):
                loads.append((k.M4[C * h:C * h + C, C * to:C * to + C], a["L1_gnn_M4"][:, C * of:C * of + C]))
        k.const_loads = loads


        def late_loads(stage, loads, zero=()):
            with Scope(nc, stage) as c:
                w_in, zeroed = c.sem("w_in"), c.sem("zeroed")
                block = c.block()

                @block.vector
                def _(v):
                    for z in zero:
                        last = v.memset(z[:], 0.0)
                    if zero:
                        last.then_inc(zeroed, 1)

                @block.sync
                def _(sp):
                    if zero:
                        sp.wait_ge(zeroed, 1)
                    for dst, src in loads:
                        sp.dma_start(dst, src).then_inc(w_in, 16)
                    sp.wait_ge(w_in, 16 * len(loads))

        with Scope(nc, "mlp") as m:
            k.M1, k.M2, k.M3 = m.sb("M1", [32, P]), m.sb("M2", [P, P]), m.sb("M3", [P, P])
            for h in range(2):
                loads.append((k.M1[16 * h:16 * h + 16, C * h:C * h + C], a["L1_gnn_M1"]))
                loads += [(w[C * h:C * h + C, C * h:C * h + C], a[n])
                          for w, n in ((k.M2, "L1_gnn_M2"), (k.M3, "L1_gnn_M3"))]
            k.cleared = [k.M1, k.M2, k.M3, k.zeros]
            setup(k)
            bn_roots(k)
            norm_stats(k, "n0")
            write_xn_table(k)
            first_edges(k)
        with Scope(nc, "w0") as w:
            k.WlT, k.WrT = w.sb("WlT", [P, KK, D]), w.sb("WrT", [P, KK, D])
            gamma, beta = w.sb("gamma", [P, D]), w.sb("beta", [P, D])
            late_loads("w0l", [(k.WlT[:, :, :], rows(a["L0_gnn_W_lT"])), (k.WrT[:, :, :], rows(a["L0_gnn_W_rT"])),
                               (gamma[:, :], spread(a["L0_gnn_gamma"], D)), (beta[:, :], spread(a["L0_gnn_beta"], D))])
            first_linear(k)
            scale_rows(k)
            column_stats(k, "c0", D)
            add_normed(k, "a0", gamma[:, :], beta[:, :], D, True, False)
        norm_stats(k, "n1")
        experts(k, "f0", k.E0, (k.bn1[:, 1, :], k.bn2[:, 1, :]), (k.bn1[:, 2, :], k.bn2[:, 2, :]), bo0[:, :], False,
                Router(w2=wr0, bias=br0[:, :]))
        load_experts(k)
        clear_semaphores(nc)
        norm_stats(k, "n2")
        with Scope(nc, "w1") as w:
            ups = w.sb("ups", [P, KK, P])
            late_loads("w1l", block_diagonal_loads(ups, a["L1_gnn_W_up0"], a["L1_gnn_W_up1"]), [ups])
            node_product(k, "up", KK, lambda v, t, dst: normed(k, v, t, dst, True), diagonal_plan(0, ups), keep(k),
                         store=k.up_tab)
        second_edges(k)
        clear_semaphores(nc)
        with Scope(nc, "w2") as w:
            lins, wbs, wscs = (w.sb(n, [P, KK, P]) for n in ("lins", "wbs", "wscs"))
            k.poly, k.poly_vv = w.sb("poly", [P, 4, 2, C]), w.sb("poly_vv", [P, C])
            gamma, beta = w.sb("gamma", [P, D]), w.sb("beta", [P, C])
            c0, c1 = a["L1_gnn_Wc0T"], a["L1_gnn_Wc1T"]

            def line(x):
                return x.to_broadcast([P, C])
            polys = [(k.poly[:, i, 0, :], line(c0[n:n + 1, :])) for i, n in enumerate((0, 1, 3, 4))]
            polys += [(k.poly[:, i, 1, :], line(c1[i:i + 1, :])) for i in range(4)]
            polys.append((k.poly_vv[:, :], line(c0[2:3, :])))
            gammas = [(gamma[:, 0:C], spread(a["L1_gnn_gamma0"], C)), (beta[:, :], spread(a["L1_gnn_beta0"], C))]
            gammas += [(gamma[:, C + C * x:2 * C + C * x], spread(a["L1_gnn_gamma1"], C)) for x in range(3)]
            late_loads("w2l", block_diagonal_loads(lins, a["L1_gnn_W_lin0"], a["L1_gnn_W_lin1"])
                       + block_diagonal_loads(wbs, a["L1_gnn_WB0"], a["L1_gnn_WB1"])
                       + block_diagonal_loads(wscs, a["L1_gnn_Wsc0"], a["L1_gnn_Wsc1"]) + polys + gammas,
                       [lins, wbs, wscs])
            node_product(k, "li", KK, lambda v, t, dst: v.tensor_copy(dst[:, 0:D], tile_of(k.AGG, t)),
                         diagonal_plan(0, lins), keep(k))
            polynomial(k)

            def fill(v, t, dst):
                v.tensor_copy(dst[:, 0:D], tile_of(k.AGG, t))
                return normed(k, v, t, dst[:, D:2 * D], True)
            node_product(k, "ob", 2 * KK, fill,
                         [x for h in range(KK) for x in (diagonal_plan(0, wbs)[h], diagonal_plan(KK, wscs)[h])],
                         keep(k))
            column_stats(k, "c1", C)
            add_normed(k, "a1", gamma[:, :], beta[:, :], C, False, True)
        norm_stats(k, "n3")
        experts(k, "f1", k.E1, None, (eb1[:, :], eb2[:, :]), bo1[:, :], True,
                Router(w1=rw1, b1=rb1[:, 0:1], w2=rw2, bias=rb2[:, :]), out=out)


def block_diagonal_loads(buf, w0, w1):
    return [(buf[0:C, 0, 0:C], w0), (buf[C:P, 0, C:P], w1), (buf[0:C, 1, 0:C], w1), (buf[C:P, 1, C:P], w1)]




def lay_out(inputs):
    import numpy as np

    a = {n: np.asarray(v) for n, v in inputs.items()}
    n, e = a["x"].shape[0], a["src"].shape[0]
    nt, ng = -(-n // P), e // GE + 1
    pad = ng * GE - e
    src = np.concatenate([a.pop("src"), np.zeros(pad, np.int32)]).astype(np.int32, copy=False)
    dst = np.concatenate([a.pop("dst"), np.full(pad + 1, NO_NODE, np.int32)]).astype(np.int32, copy=False)

    def by_group(v):
        return v.reshape(ng, G, P, -1).transpose(0, 2, 1, 3)
    a["dst_line"] = dst
    a["edges"] = np.concatenate([by_group(src)[..., 0], by_group(dst[:-1])[..., 0]], -1)
    attr4 = np.concatenate([a.pop("edge_attr_4"), np.zeros((pad, 4), np.float32)])
    a["attr4"] = by_group(attr4).reshape(ng, P, G * 4)
    attr16 = np.concatenate([a.pop("edge_attr_16"), np.zeros((pad, 16), np.float32)])
    a["attr16"] = attr16.reshape(ng, 2, HALF, 16).transpose(0, 1, 3, 2).reshape(ng, 32, HALF)
    pairs = np.zeros((-(-ng * nt // (SLOTS * 16)) * SLOTS * 16, 4), np.int32)
    pairs[:, 2] = nt * P
    i = np.arange(ng * nt)
    pairs[:ng * nt, 0], pairs[:ng * nt, 1], pairs[:ng * nt, 2] = i // nt, i % nt, i % nt * P
    a["all_pairs"] = pairs
    a["rank"] = np.arange(8, 0, -1, dtype=np.float32)[None]
    for w in ("W_l", "W_r"):
        a[f"L0_gnn_{w}T"] = a.pop(f"L0_gnn_{w}").T
    for w in ("Wc0", "Wc1"):
        a[f"L1_gnn_{w}T"] = a.pop(f"L1_gnn_{w}").T
    for name in [f"L0_ffn_{x}{i}" for x in ("b", "g", "be", "m", "v") for i in (1, 2)] + [
            "L1_ffn_expert_b1", "L1_ffn_expert_b2"]:
        ex = a[name].shape[0]
        a[name] = a[name].reshape(ex, 2, P).transpose(2, 0, 1).reshape(P, 2 * ex)
    return {n: np.ascontiguousarray(v) for n, v in a.items()}


def kernel(**inputs):
    import concourse.bacc as bacc
    from concourse.bass_utils import run_bass_kernel_spmd

    arrays = lay_out(inputs)
    nc = bacc.Bacc("TRN2", target_bir_lowering=False, num_devices=1)
    aps = {n: nc.dram_tensor(f"in_{n}", v.shape, mybir.dt.from_np(v.dtype), kind="ExternalInput").ap()
           for n, v in arrays.items()}
    out = nc.dram_tensor("out_dram", arrays["x"].shape, F32, kind="ExternalOutput").ap()
    program(nc, aps, out)
    r = run_bass_kernel_spmd(nc, [{f"in_{n}": v for n, v in arrays.items()}], core_ids=[0])
    return r.results[0]["out_dram"]
```

```python
from contextlib import ExitStack

import concourse.bass as bass
from concourse import mybir

F32 = mybir.dt.float32
F32R = mybir.dt.float32r
I32 = mybir.dt.int32
ALU = mybir.AluOpType
ACT = mybir.ActivationFunctionType
AX = mybir.AxisListType

P = 128
D = 256
C = 64
KK = D // P
G = 4
GE = G * P
HALF = GE // 2
SLOTS = 4
HALVES = 2
ROUND = HALVES * SLOTS
NO_NODE = 1 << 20
LN_EPS = 1e-5
CHUNK = 4


class Shared:
    pass


class Router:

    def __init__(self, w2, bias, w1=None, b1=None):
        self.w2, self.bias, self.w1, self.b1 = w2, bias, w1, b1


class Steps:

    def __init__(self, eng, sem):
        self.eng, self.sem, self.base, self.n = eng, sem, 0, 0

    def done(self, ins):
        self.n += 1
        return ins.then_inc(self.sem, 1)

    def sync(self):
        self.eng.wait_ge(self.sem, self.base + self.n)

    def enter(self, i, per):
        if self.n:
            self.base, self.n = self.base + self.n, 0
        self.start = self.base
        self.base = i * per + self.start
        self.per = per

    def leave(self, count):
        assert self.n == self.per, (self.n, self.per)
        self.base, self.n = self.start + count * self.per, 0


class Scope:

    used = []

    def __init__(self, nc, stage):
        self.nc, self.stage, self.stack = nc, stage, ExitStack()

    def __enter__(self):
        self.stack.__enter__()
        return self

    def __exit__(self, *a):
        return self.stack.__exit__(*a)

    def sb(self, name, shape, dt=F32):
        return self.stack.enter_context(self.nc.sbuf_tensor(f"{self.stage}_{name}", shape, dt))

    def ps(self, name, shape):
        return self.stack.enter_context(self.nc.psum_tensor(f"{self.stage}_{name}", shape, F32))

    def sem(self, name):
        h = self.stack.enter_context(self.nc.semaphore(f"{self.stage}_{name}"))
        self.used.append(h)
        return h

    def sems(self, name, n):
        return [self.sem(f"{name}{i}") for i in range(n)]

    def block(self):
        return self.stack.enter_context(self.nc.Block())


def clear_semaphores(nc):
    with nc.Block() as block:
        @block.gpsimd
        def _(pool):
            for h in Scope.used:
                pool.sem_clear(h)
    Scope.used.clear()


def apart(eng, sem, value, ticks):
    eng.wait_ge(sem, value)
    eng.sem_inc(ticks, 1)


def tile_loop(eng, k, body):
    assert k.NT % 2 == 1
    with eng.Fori(0, k.NT // 2) as i:
        for s in range(2):
            body(2 * i + s, s, i, False)
    body(k.NT - 1, 0, k.NT // 2, True)


def pipelined_tiles(eng, k, first, second):
    first(0, 0, 0)
    with eng.Fori(0, k.NT // 2) as i:
        first(2 * i + 1, 1, i)
        second(2 * i, 0, i)
        first(2 * i + 2, 0, i + 1)
        second(2 * i + 1, 1, i)
    second(k.NT - 1, 0, k.NT // 2)


SEVEN = 7


def seven_loop(eng, k):
    assert k.NT % SEVEN == 0
    return eng.Fori(0, k.NT // SEVEN)


def col(buf, t):
    return buf[:, bass.ds(t, 1)] if not isinstance(t, int) else buf[:, t:t + 1]


def tile_of(buf, t, a=0, b=D):
    v = buf[:, bass.ds(t, 1), a:b] if not isinstance(t, int) else buf[:, t:t + 1, a:b]
    return v.rearrange("p t d -> p (t d)")




def setup(k):
    nc, NT, NG = k.nc, k.NT, k.NG
    EC = NG * GE // P
    with Scope(nc, "su") as s:
        dst_a, dst_b = s.sb("dst_a", [P, EC], I32), s.sb("dst_b", [P, EC], I32)
        fa, fb = s.sb("fa", [P, EC]), s.sb("fb", [P, EC])
        falls = s.sb("falls", [P, 1])
        ends_i, ends = s.sb("ends_i", [1, 2, NG], I32), s.sb("ends", [1, 2, NG])
        more, before = s.sb("more", [1, NG]), s.sb("before", [1, NG])
        lane_i, part_i = s.sb("lane_i", [P, P], I32), s.sb("part_i", [P, 1], I32)
        part = s.sb("part", [P, 1])
        table = s.sb("table", [1, NG, 4], I32)
        mixed = s.sb("mixed", [1, 2])
        p_falls = s.ps("p_falls", [P, 512])
        x_in, w_in, dst_in, ends_in = (s.sem(n) for n in ("x_in", "w_in", "dst_in", "ends_in"))
        iota_done, zeroed, own, pe_done = (s.sem(n) for n in ("iota_done", "zeroed", "own", "pe_done"))
        falls_ready, table_ready, table_out = (s.sem(n) for n in ("falls_ready", "table_ready", "table_out"))
        block = s.block()

        @block.sync
        def _(sp):
            line = k.dst_line
            sp.wait_ge(zeroed, 1)
            sp.dma_start(k.X[:, 0:NT - 1, :], k.x[0:(NT - 1) * P, :].rearrange("(t p) d -> p t d", p=P)
                         ).then_inc(x_in, 16)
            sp.dma_start(k.X[0:k.LAST, NT - 1, :], k.x[(NT - 1) * P:, :]).then_inc(x_in, 16)
            sp.dma_start(dst_a[:, :], line[0:NG * GE].rearrange("(p c) -> p c", p=P)).then_inc(dst_in, 16)
            sp.dma_start(dst_b[:, :], line[1:NG * GE + 1].rearrange("(p c) -> p c", p=P)).then_inc(dst_in, 16)
            with nc.allow_non_contiguous_dma(reason="two words of each group"):
                for i, e in enumerate((0, GE - 1)):
                    sp.dma_start(ends_i[:, i, :], line[0:NG * GE].rearrange("(a g e) -> a g e", a=1, e=GE)[:, :, e]
                                 ).then_inc(ends_in, 16)
            sp.wait_ge(x_in, 32)
            sp.wait_ge(table_ready, 1)
            sp.dma_start(k.table.rearrange("(a i) f -> a i f", a=1), table[:, :, :]).then_inc(table_out, 16)
            sp.wait_ge(table_out, 16)

        @block.scalar
        def _(act):
            n = 0
            act.wait_ge(zeroed, 2)
            for dst, src in k.const_loads:
                act.dma_start(dst, src).then_inc(w_in, 16)
                n += 16
            act.wait_ge(w_in, n)

        @block.gpsimd
        def _(pool):
            pool.iota(lane_i[:, :], pattern=[[1, P]], base=0, channel_multiplier=0).then_inc(iota_done, 1)
            pool.iota(part_i[:, :], pattern=[[0, 1]], base=0, channel_multiplier=1).then_inc(iota_done, 1)

        @block.vector
        def _(v):
            me = Steps(v, own)
            v.memset(k.X[:, NT - 1, :], 0.0).then_inc(zeroed, 1)
            for buf in k.cleared:
                last = v.memset(buf[:], 0.0)
            last.then_inc(zeroed, 1)
            v.memset(k.ones_valid[:, :], 0.0)
            me.done(v.memset(k.ones[:, :], 1.0))
            me.sync()
            me.done(v.memset(k.ones_valid[0:k.LAST, :], 1.0))
            v.wait_ge(iota_done, 2)
            v.tensor_copy(k.lane[:, :], lane_i[:, :])
            me.done(v.tensor_copy(part[:, :], part_i[:, :]))
            me.sync()
            me.done(v.tensor_scalar(k.ident[:, :], k.lane[:, :], part[:, 0:1], None, ALU.is_equal))
            v.wait_ge(dst_in, 32)
            v.tensor_copy(fa[:, :], dst_a[:, :])
            me.done(v.tensor_copy(fb[:, :], dst_b[:, :]))
            me.sync()
            me.done(v.tensor_tensor(fa[:, :], fa[:, :], fb[:, :], ALU.is_gt))
            me.sync()
            v.reduce_sum(falls[:, :], fa[:, :], AX.X).then_inc(falls_ready, 1)
            v.wait_ge(ends_in, 32)
            me.done(v.tensor_scalar(ends_i[:, :, :], ends_i[:, :, :], P.bit_length() - 1, None, ALU.arith_shift_right))
            me.sync()
            me.done(v.tensor_copy(ends[:, :, :], ends_i[:, :, :]))
            me.sync()
            me.done(v.tensor_scalar(ends[:, :, :], ends[:, :, :], float(NT - 1), None, ALU.min))
            v.wait_ge(pe_done, 1)
            me.done(v.tensor_scalar(mixed[:, 0:1], p_falls[0:1, 0:1], 0.5, None, ALU.is_gt))
            me.sync()
            me.done(v.tensor_scalar(mixed[:, 1:2], mixed[:, 0:1], float(NT - 1), None, ALU.mult))
            me.done(v.tensor_scalar(mixed[:, 0:1], mixed[:, 0:1], -1.0, 1.0, ALU.mult, ALU.add))
            me.sync()
            me.done(v.tensor_scalar(ends[:, :, :], ends[:, :, :], mixed[:, 0:1], None, ALU.mult))
            me.sync()
            me.done(v.tensor_scalar(ends[:, 1, :], ends[:, 1, :], mixed[:, 1:2], None, ALU.add))
            me.sync()
            me.done(v.tensor_tensor(more[:, :], ends[:, 1, :], ends[:, 0, :], ALU.subtract))
            me.done(v.memset(before[:, 0:1], 0.0))
            me.sync()
            me.done(v.tensor_copy(before[:, 1:NG], more[:, 0:NG - 1]))
            me.sync()
            far, src, dst = 1, before, ends[:, 1, :]
            while far < NG:
                me.done(v.tensor_copy(dst[:, 0:far], src[:, 0:far]))
                me.done(v.tensor_tensor(dst[:, far:NG], src[:, far:NG], src[:, 0:NG - far], ALU.add))
                me.sync()
                src, dst, far = dst, src, 2 * far
            v.tensor_copy(table[:, :, 0], ends[:, 0, :])
            v.tensor_scalar(table[:, :, 1], ends[:, 0, :], float(P), None, ALU.mult)
            v.tensor_copy(table[:, :, 2], more[:, :])
            v.tensor_copy(table[:, :, 3], src[:, 0:NG]).then_inc(table_ready, 1)
            v.wait_ge(w_in, 16 * len(k.const_loads))
            batch_norm_constants(k, v, me)

        @block.tensor
        def _(pe):
            pe.wait_ge(own, 1)
            pe.wait_ge(falls_ready, 1)
            pe.matmul(p_falls[:, 0:1], k.ones[:, :], falls[:, :], start=True, stop=True).then_inc(pe_done, 1)


def batch_norm_constants(k, v, me):
    for b in (k.bn1, k.bn2):
        me.done(v.tensor_scalar(b[:, 4, :], b[:, 4, :], 1e-3, None, ALU.add))
        me.done(v.tensor_tensor(b[:, 3, :], b[:, 0, :], b[:, 3, :], ALU.subtract))
    me.done(v.tensor_scalar(k.M4[:, C:2 * C], k.M4[:, C:2 * C], float(1.0 / 3.0 ** 0.5), None, ALU.mult))


def bn_roots(k):
    with Scope(k.nc, "bn") as s:
        own, rooted = s.sem("own"), s.sem("rooted")
        block = s.block()

        @block.scalar
        def _(act):
            for b in (k.bn1, k.bn2):
                act.activation(b[:, 4, :], b[:, 4, :], ACT.Sqrt).then_inc(rooted, 1)

        @block.vector
        def _(v):
            me = Steps(v, own)
            v.wait_ge(rooted, 2)
            for b in (k.bn1, k.bn2):
                me.done(v.reciprocal(b[:, 4, :], b[:, 4, :]))
            me.sync()
            for b in (k.bn1, k.bn2):
                me.done(v.tensor_tensor(b[:, 1, :], b[:, 1, :], b[:, 4, :], ALU.mult))
            me.sync()
            for b in (k.bn1, k.bn2):
                me.done(v.tensor_tensor(b[:, 3, :], b[:, 3, :], b[:, 1, :], ALU.mult))
            me.sync()
            for b in (k.bn1, k.bn2):
                me.done(v.tensor_tensor(b[:, 2, :], b[:, 2, :], b[:, 3, :], ALU.add))




def norm_stats(k, stage):
    NT = k.NT
    with Scope(k.nc, stage) as s:
        st = s.sb("st", [P, NT, 6])
        a, b = s.sb("a", [P, NT]), s.sb("b", [P, NT])
        own, var_ready, rooted = s.sem("own"), s.sem("var_ready"), s.sem("rooted")
        block = s.block()

        @block.vector
        def _(v):
            me = Steps(v, own)
            with seven_loop(v, k) as i:
                me.enter(i, SEVEN)
                for j in range(SEVEN):
                    me.done(v.bn_stats(tile_of(st, i * SEVEN + j, 0, 6), tile_of(k.X, i * SEVEN + j)))
            me.leave(NT // SEVEN)
            me.sync()
            me.done(v.tensor_tensor(a[:, :], st[:, :, 1], st[:, :, 4], ALU.subtract))
            me.done(v.tensor_tensor(b[:, :], st[:, :, 2], st[:, :, 5], ALU.add))
            me.done(v.tensor_tensor(k.mean[:, :], st[:, :, 1], st[:, :, 4], ALU.add))
            me.sync()
            me.done(v.tensor_tensor(a[:, :], a[:, :], a[:, :], ALU.mult))
            me.done(v.tensor_scalar(b[:, :], b[:, :], 1.0 / D, LN_EPS, ALU.mult, ALU.add))
            me.done(v.tensor_scalar(k.mean[:, :], k.mean[:, :], 0.5, None, ALU.mult))
            me.sync()
            v.scalar_tensor_tensor(out=b[:, :], in0=a[:, :], scalar=0.25, in1=b[:, :], op0=ALU.mult,
                                   op1=ALU.add).then_inc(var_ready, 1)
            v.wait_ge(rooted, 1)
            v.reciprocal(k.rstd[:, :], b[:, :])

        @block.scalar
        def _(act):
            act.wait_ge(var_ready, 1)
            act.activation(b[:, :], b[:, :], ACT.Sqrt).then_inc(rooted, 1)


def normed(k, v, t, dst, channel_major=False):
    m, r = col(k.mean, t), col(k.rstd, t)
    if not channel_major:
        return v.tensor_scalar(dst, tile_of(k.X, t), m, r, ALU.subtract, ALU.mult)
    v.tensor_scalar(dst[:, 0:C], tile_of(k.X, t, 0, C), m, r, ALU.subtract, ALU.mult)
    return v.tensor_scalar(dst[:, C:D].rearrange("p (x c) -> p x c", x=3),
                           tile_of(k.X, t, C, D).rearrange("p (c x) -> p x c", x=3), m, r, ALU.subtract, ALU.mult)


def write_xn_table(k):
    NT = k.NT
    with Scope(k.nc, "xn") as s:
        ready, stored = s.sem("ready"), s.sem("stored")
        block = s.block()

        @block.vector
        def _(v):
            with seven_loop(v, k) as i:
                for j in range(SEVEN):
                    last = normed(k, v, i * SEVEN + j, tile_of(k.AGG, i * SEVEN + j))
                last.then_inc(ready, 1)

        @block.sync
        def _(sp):
            with seven_loop(sp, k) as i:
                sp.wait_ge(ready, i + 1)
                sp.dma_start(k.xn_tab[bass.ds(i * SEVEN * P, SEVEN * P), :].rearrange("(j p) d -> p j d", p=P),
                             k.AGG[:, bass.ds(i * SEVEN, SEVEN), 0:D]).then_inc(stored, 16)
            sp.wait_ge(stored, 16 * (NT // SEVEN))




class Group:

    def __init__(self, it, c):
        self.h, self.q, self.it = c % ROUND // SLOTS, c % SLOTS, it + c // ROUND
        self.c = c % ROUND
        self.n = it * HALVES + c // SLOTS


def edge_loop(k, eng):
    return eng.Fori(0, k.NG // ROUND)


def gather_groups(k, pool, table, edges, gx, edges_in, gathered, slot_free, ticks):
    with edge_loop(k, pool) as it:
        for c in range(ROUND):
            g = Group(it, c)
            if g.q == 0:
                apart(pool, edges_in[g.h], (it + 1) * 16 * 3, ticks)
            apart(pool, slot_free[g.q], g.n + 2, ticks)
            for j in range(G):
                pool.indirect_dma_start(gx[:, g.q, j, 0:D], None, table,
                                        bass.IndirectOffsetOnAxis(edges[:, g.h, g.q, j:j + 1], 0),
                                        bounds_check=k.NT * P - 1, oob_is_err=False).then_inc(gathered[g.q], 16)


def choose(k, v, g, edges, first, pick, ready):
    for j in range(G):
        last = v.tensor_scalar(pick[:, g.q, j, :], k.lane[:, :], first, edges[:, g.h, g.q, G + j:G + j + 1],
                               ALU.add, ALU.is_equal)
    last.then_inc(ready, 1)


def add_group(k, v, g, edges, row, pick, sums, width, here, sums_ready, added, slot_free, more_picked, more_summed):
    b = v.value_load(row[0:1, g.h, g.q, 0:1], min_val=0, max_val=k.NT - 1)
    more = v.value_load(row[0:1, g.h, g.q, 2:3], min_val=0, max_val=k.NT - 1)
    v.wait_ge(sums_ready[g.q], g.n + 1)
    v.wait_ge(added, g.it * ROUND + g.c + 1)
    tile = tile_of(k.AGG, b, 0, width)
    v.tensor_tensor(tile, tile, sums[:, g.q, 0:width], ALU.add).then_inc(added, 1)
    with v.If(more > 0):
        earlier = v.value_load(row[0:1, g.h, g.q, 3:4], min_val=0, max_val=k.NG * k.NT)
        v.tensor_copy(here[:, :], row[:, g.h, g.q, 1:2])
        with v.Fori(0, more) as i:
            v.drain()
            v.tensor_scalar(here[:, :], here[:, :], float(P), None, ALU.add)
            v.drain()
            choose(k, v, g, edges, here[:, 0:1], pick, more_picked)
            v.wait_ge(more_summed, earlier + i + 1)
            tile = tile_of(k.AGG, k.nc.s_assert_within(
                b + i + 1, 1, k.NT - 1, skip_runtime_bounds_check_because="a group's tiles end at NT - 1"), 0, width)
            v.tensor_tensor(tile, tile, sums[:, g.q, 0:width], ALU.add)
        v.drain()
    v.sem_inc(slot_free[g.q], 1)


def sum_group(k, pe, g, row, pick, parts, sums, width, arrived, sums_ready, more_picked, more_summed):
    more = pe.value_load(row[0:1, g.h, g.q, 2:3], min_val=0, max_val=k.NT - 1)
    for sem, value in arrived:
        pe.wait_ge(sem, value)

    def once():
        for j in range(G):
            for i, x in enumerate(parts(j)):
                mm = pe.matmul(sums[:, g.q, 0:width], pick[:, g.q, j, :], x, start=(j == 0 and i == 0),
                               stop=(j == G - 1 and i == len(parts(j)) - 1))
        return mm
    once().then_inc(sums_ready[g.q], 1)
    with pe.If(more > 0):
        earlier = pe.value_load(row[0:1, g.h, g.q, 3:4], min_val=0, max_val=k.NG * k.NT)
        with pe.Fori(0, more) as i:
            pe.wait_ge(more_picked, earlier + i + 1)
            once().then_inc(more_summed, 1)


def first_edges(k):
    with Scope(k.nc, "e0") as s:
        edges = s.sb("edges", [P, HALVES, SLOTS, 2 * G], I32)
        row = s.sb("row", [P, HALVES, SLOTS, 4], I32)
        attr = s.sb("attr", [32, HALVES, SLOTS * HALF])
        gx, pick = s.sb("gx", [P, SLOTS, G, D + 4]), s.sb("pick", [P, SLOTS, G, P])
        here = s.sb("here", [P, 1], I32)
        h1, h2, h3 = (s.sb(f"h{i}", [P, 2, 2 * HALF]) for i in (1, 2, 3))
        PAIRS = ROUND // 2
        sums, hid = s.ps("sums", [P, SLOTS, 512]), s.ps("hid", [P, PAIRS, 512])
        edges_in, slot_free = s.sems("edges_in", HALVES), s.sems("slot_free", SLOTS)
        gathered = k.gathered[0]
        pick_ready, sums_ready = s.sems("pick_ready", SLOTS), s.sems("sums_ready", SLOTS)
        hid_mm, hid_act, hid_out = s.sems("hid_mm", PAIRS), s.sems("hid_act", PAIRS), s.sems("hid_out", 2)
        added, more_picked, more_summed = s.sem("added"), s.sem("more_picked"), s.sem("more_summed")
        pool_ticks, act_ticks = s.sem("pool_ticks"), s.sem("act_ticks")
        block = s.block()

        hidden_before = [[(0, 0), (1, 0)], [(0, 1)], [(0, 2)], [(1, 1)], [(1, 2), (2, 0)], [(2, 1), (3, 0)], [(2, 2)],
                         [(3, 1)], [(3, 2)]]

        @block.sync
        def _(sp):
            load_experts(k, sp, k.W1_0, k.W2_0, k.W3_0)
            with edge_loop(k, sp) as it:
                for h in range(HALVES):
                    i = it * HALVES + h
                    sp.wait_ge(slot_free[SLOTS - 1], i + 1)
                    load_edges(k, sp, i, edges[:, h], row[:, h], edges_in[h])
                    sp.dma_start(attr[:, h, :], k.attr16[bass.ds(i, 1), :, :].rearrange("a p c -> (a p) c")
                                 ).then_inc(edges_in[h], 16)

        @block.gpsimd
        def _(pool):
            gather_groups(k, pool, k.xn_tab, edges, gx, edges_in, gathered, slot_free, pool_ticks)

        @block.vector
        def _(v):
            v.memset(k.AGG[:, :, :], 0.0).then_inc(added, 1)
            for q in range(SLOTS):
                v.memset(gx[:, q, :, D:D + 1], 1.0).then_inc(slot_free[q], 2)
            with edge_loop(k, v) as it:
                def pick_group(c):
                    g = Group(it, c)
                    if g.q == 0:
                        v.wait_ge(edges_in[g.h], (it + 1) * 16 * 3)
                    choose(k, v, g, edges, row[:, g.h, g.q, 1:2], pick, pick_ready[g.q])

                pick_group(0)
                pick_group(1)
                for c in range(ROUND):
                    if c + 2 < ROUND:
                        pick_group(c + 2)
                    add_group(k, v, Group(it, c), edges, row, pick, sums, D + 1, here, sums_ready, added, slot_free,
                              more_picked, more_summed)

        @block.tensor
        def _(pe):
            with edge_loop(k, pe) as it:
                def hidden(b, layer):
                    if layer == 0 and b % 2 == 0:
                        pe.wait_ge(edges_in[b // 2], (it + 1) * 16 * 3)
                    w, x = [(k.M1, attr[:, b // 2, b % 2 * 2 * HALF:(b % 2 + 1) * 2 * HALF]),
                            (k.M2, h1[:, b % 2, :]), (k.M3, h2[:, b % 2, :])][layer]
                    pe.wait_ge(hid_act[b], it * 3 + layer + 1)
                    pe.matmul(hid[:, b, :], w[:, :], x, start=True, stop=True).then_inc(hid_mm[b], 1)

                for c in range(ROUND + 1):
                    for b, layer in hidden_before[c]:
                        hidden(b, layer)
                    if c < ROUND:
                        g = Group(it, c)
                        sum_group(k, pe, g, row, pick, lambda j: [gx[:, g.q, j, 0:D + 1]], sums, D + 1,
                                  [(pick_ready[g.q], g.n + 1), (gathered[g.q], (g.n + 1) * 16 * G)],
                                  sums_ready, more_picked, more_summed)

        @block.scalar
        def _(act):
            for b in range(PAIRS):
                act.sem_inc(hid_act[b], 1)
            for i in range(2):
                act.sem_inc(hid_out[i], 16)
            with edge_loop(k, act) as it:
                for b, layer in [x for some in hidden_before for x in some]:
                    apart(act, hid_mm[b], it * 3 + layer + 1, act_ticks)
                    h = (h1, h2, h3)[layer][:, b % 2, :]
                    if layer == 2:
                        apart(act, hid_out[b % 2], (it * HALVES + b // 2 + 1) * 16, act_ticks)
                    act.activation(h, hid[:, b, :], ACT.Silu).then_inc(hid_act[b], 1)
                    if layer == 2:
                        act.wait_ge(hid_act[b], it * 3 + 4)
                        act.dma_start(k.hidden[bass.ds(it * HALVES + b // 2, 1), :,
                                               b % 2 * 2 * HALF:(b % 2 + 1) * 2 * HALF].rearrange("a p c -> (a p) c"),
                                      h).then_inc(hid_out[b % 2], 16)
            for i in range(2):
                act.wait_ge(hid_out[i], (k.NG // SLOTS + 1) * 16)


def load_edges(k, sp, i, edges, row, edges_in):
    sp.dma_start(edges.rearrange("p q e -> p (q e)"), k.edges[bass.ds(i, 1), :, :].rearrange("a p c -> (a p) c")
                 ).then_inc(edges_in, 16)
    sp.dma_start(row.rearrange("p q f -> p (q f)"),
                 k.table[bass.ds(i * SLOTS, SLOTS), :].rearrange("(a q) f -> a (q f)", a=1).to_broadcast([P, SLOTS * 4])
                 ).then_inc(edges_in, 16)


def second_edges(k):
    with Scope(k.nc, "e1") as s:
        edges = s.sb("edges", [P, HALVES, SLOTS, 2 * G], I32)
        row = s.sb("row", [P, HALVES, SLOTS, 4], I32)
        sh = s.sb("sh", [P, HALVES, SLOTS, G, 4])
        gx, pick = s.sb("gx", [P, SLOTS, G, D]), s.sb("pick", [P, SLOTS, G, P])
        here = s.sb("here", [P, 1], I32)
        hid = s.sb("hid", [P, SLOTS, HALF])
        xs = s.sb("xs", [P, 2, G, D])
        pr = s.sb("pr", [P, 2, G, 3, C])
        mb = s.sb("mb", [P, 2, G, D])
        spare = k.WALL[:, k.E1:k.E0].rearrange("p e i a n -> p (e i a n)")
        n = 2 * G * D
        ma = spare[:, 0:n].rearrange("p (r j d) -> p r j d", r=2, j=G)
        dot, t1x = (spare[:, n + i * n // 4:n + (i + 1) * n // 4].rearrange("p (r j d) -> p r j d", r=2, j=G)
                    for i in range(2))
        sums, tw = s.ps("sums", [P, SLOTS, 512]), s.ps("tw", [P, 2, G, D])
        edges_in, hid_in, slot_free = s.sems("edges_in", HALVES), s.sems("hid_in", 2), s.sems("slot_free", SLOTS)
        gathered = k.gathered[1]
        pick_ready, sums_ready = s.sems("pick_ready", SLOTS), s.sems("sums_ready", SLOTS)
        tw_ready, xs_ready, msg_ready = s.sems("tw_ready", SLOTS), s.sems("xs_ready", SLOTS), s.sems("msg_ready", SLOTS)
        added, more_picked, more_summed = s.sem("added"), s.sem("more_picked"), s.sem("more_summed")
        pool_ticks, own = s.sem("pool_ticks"), s.sem("own")
        block = s.block()
        PER = 3

        @block.sync
        def _(sp):
            load_experts(k, sp, k.W1_1, k.W2_1, k.W3_1)
            with edge_loop(k, sp) as it:
                for h in range(HALVES):
                    i = it * HALVES + h
                    sp.wait_ge(slot_free[SLOTS - 1], i + 1)
                    load_edges(k, sp, i, edges[:, h], row[:, h], edges_in[h])
                    sp.dma_start(sh[:, h].rearrange("p q j f -> p (q j f)"),
                                 k.attr4[bass.ds(i, 1), :, :].rearrange("a p c -> (a p) c")).then_inc(edges_in[h], 16)
                    for b in range(2):
                        sp.wait_ge(tw_ready[2 * b + 1], i + 1)
                        sp.dma_start(hid[:, 2 * b:2 * b + 2, :].rearrange("p q e -> p (q e)"),
                                     k.hidden[bass.ds(i, 1), :, b * 2 * HALF:(b + 1) * 2 * HALF
                                              ].rearrange("a p c -> (a p) c")).then_inc(hid_in[b], 16)

        @block.gpsimd
        def _(pool):
            gather_groups(k, pool, k.up_tab, edges, gx, edges_in, gathered, slot_free, pool_ticks)

        @block.scalar
        def _(act):
            with edge_loop(k, act) as it:
                for c in range(ROUND):
                    g, old = Group(it, c), Group(it, c - 2)
                    r = g.q % 2
                    act.wait_ge(msg_ready[old.q], old.n + 2)
                    act.wait_ge(gathered[g.q], (g.n + 1) * 16 * G)
                    for j in range(G):
                        act.activation(xs[:, r, j, :], gx[:, g.q, j, :], ACT.Copy, scale=sh[:, g.h, g.q, j, 0:1])
                        for x in range(3):
                            last = act.activation(pr[:, r, j, x, :], gx[:, g.q, j, C + C * x:2 * C + C * x],
                                                  ACT.Copy, scale=sh[:, g.h, g.q, j, 1 + x:2 + x])
                    last.then_inc(xs_ready[g.q], 1)

        @block.vector
        def _(v):
            me = Steps(v, own)
            for q in range(SLOTS):
                v.sem_inc(msg_ready[q], 1)
                v.sem_inc(slot_free[q], 2)
            v.memset(k.AGG[:, :, :], 0.0).then_inc(added, 1)
            with edge_loop(k, v) as it:
                me.enter(it, PER * ROUND)

                def messages(g):
                    r = g.q % 2
                    t0, t3, t1, t2 = (tw[:, r, :, C * i:C * i + C] for i in range(4))
                    if g.q == 0:
                        v.wait_ge(edges_in[g.h], (it + 1) * 16 * 3)
                    choose(k, v, g, edges, row[:, g.h, g.q, 1:2], pick, pick_ready[g.q])
                    v.wait_ge(xs_ready[g.q], g.n + 1)
                    me.done(v.tensor_tensor(dot[:, r], pr[:, r, :, 0, :], pr[:, r, :, 1, :], ALU.add))
                    v.wait_ge(tw_ready[g.q], g.n + 2)
                    v.tensor_tensor(ma[:, r, :, 0:C], t0, xs[:, r, :, 0:C], ALU.mult)
                    me.done(v.tensor_tensor(t1x[:, r], t1, gx[:, g.q, :, 0:C], ALU.mult))
                    me.sync()
                    me.done(v.tensor_tensor(dot[:, r], dot[:, r], pr[:, r, :, 2, :], ALU.add))
                    v.tensor_tensor(ma[:, r, :, C:D].rearrange("p j (x c) -> p j x c", x=3),
                                    t2.unsqueeze(2).to_broadcast([P, G, 3, C]),
                                    xs[:, r, :, C:D].rearrange("p j (x c) -> p j x c", x=3), ALU.mult)
                    v.tensor_tensor(mb[:, r, :, C:D].rearrange("p j (x c) -> p j x c", x=3),
                                    t1x[:, r].unsqueeze(2).to_broadcast([P, G, 3, C]),
                                    sh[:, g.h, g.q, :, 1:4].unsqueeze(3).to_broadcast([P, G, 3, C]), ALU.mult)
                    me.sync()
                    v.tensor_tensor(mb[:, r, :, 0:C], t3, dot[:, r], ALU.mult).then_inc(msg_ready[g.q], 1)

                def add(g):
                    add_group(k, v, g, edges, row, pick, sums, D, here, sums_ready, added, slot_free, more_picked,
                              more_summed)
                for c in range(ROUND):
                    messages(Group(it, c))
                    if c:
                        add(Group(it, c - 1))
                    else:
                        with v.If(it > 0):
                            add(Group(it, -1))
            me.leave(k.NG // ROUND)
            add(Group(k.NG // ROUND, -1))

        @block.tensor
        def _(pe):
            for q in range(SLOTS):
                pe.sem_inc(tw_ready[q], 1)

            def weights(g):
                r = g.q % 2
                if g.q == 0:
                    pe.wait_ge(edges_in[g.h], (g.it + 1) * 16 * 3)
                if g.q % 2 == 0:
                    pe.wait_ge(hid_in[g.q // 2], (g.n + 1) * 16)
                old = Group(g.it, g.c - 2)
                pe.wait_ge(msg_ready[old.q], old.n + 2)
                for j in (0, 2, 1, 3):
                    h, o = j // 2 * C, j % 2 * P
                    mm = pe.matmul(tw[:, r, j, :], hid[h:h + C, g.q, o:o + P], k.M4[h:h + C, :], start=True, stop=True)
                mm.then_inc(tw_ready[g.q], 1)

            def add_up(g):
                r = g.q % 2
                sum_group(k, pe, g, row, pick, lambda j: [ma[:, r, j, :], mb[:, r, j, :]], sums, D,
                          [(pick_ready[g.q], g.n + 1), (msg_ready[g.q], g.n + 2)],
                          sums_ready, more_picked, more_summed)
            with edge_loop(k, pe) as it:
                for c in range(ROUND):
                    weights(Group(it, c))
                    if c:
                        add_up(Group(it, c - 1))
                    else:
                        with pe.If(it > 0):
                            add_up(Group(it, -1))
            add_up(Group(k.NG // ROUND, -1))




def node_product(k, stage, chunks, fill, plan, evacuate, store=None):
    NT = k.NT
    with Scope(k.nc, stage) as s:
        cat = s.sb("cat", [P, 2, chunks * P])
        catT = s.sb("catT", [P, 2, chunks, P])
        junk = s.sb("junk", [P, 2, D])
        p_t, p_o = s.ps("p_t", [P, 2, 512]), s.ps("p_o", [P, 2, 512])
        filled, turned, copied, product, taken = (s.sems(n, 2) for n in ("filled", "turned", "copied", "product", "taken"))
        ticks, stored = s.sem("ticks"), s.sem("stored")
        block = s.block()

        @block.vector
        def _(v):
            def fill_tile(t, b, i):
                v.wait_ge(turned[b], i + 1)
                fill(v, t, cat[:, b, :]).then_inc(filled[b], 1)

            def copy_turned(t, b, i):
                v.wait_ge(turned[b], i + 2)
                v.wait_ge(product[b], i + 1)
                v.tensor_copy(catT[:, b], p_t[:, b, 0:chunks * P].rearrange("p (a c) -> p a c", c=P)
                              ).then_inc(copied[b], 1)
            pipelined_tiles(v, k, fill_tile, copy_turned)

        @block.tensor
        def _(pe):
            for b in range(2):
                pe.sem_inc(turned[b], 1)
                pe.sem_inc(product[b], 1)
                pe.sem_inc(copied[b], 1)

            def turn(t, b, i):
                pe.wait_ge(filled[b], i + 1)
                pe.wait_ge(copied[b], i + 1)
                for a in range(chunks):
                    mm = pe.transpose(p_t[:, b, a * P:(a + 1) * P], cat[:, b, a * P:(a + 1) * P], k.ident[:, :])
                mm.then_inc(turned[b], 1)

            def multiply(t, b, i):
                pe.wait_ge(copied[b], i + 2)
                pe.wait_ge(taken[b], i + 1)
                for n, (a, w, c0, cn) in enumerate(plan):
                    same = [m for m, x in enumerate(plan) if x[2] == c0]
                    lhs = k.ones[0:1, :] if a is None else catT[:, b, a, :]
                    mm = pe.matmul(p_o[:, b, c0:c0 + cn], lhs, w, start=(n == same[0]), stop=(n == same[-1]))
                mm.then_inc(product[b], 1)
            pipelined_tiles(pe, k, turn, multiply)

        @block.scalar
        def _(act):
            for b in range(2):
                act.sem_inc(taken[b], 1)

            def body(t, b, i, last):
                apart(act, product[b], i + 2, ticks)
                evacuate(act, t, p_o[:, b, 0:D], junk[:, b, :]).then_inc(taken[b], 1)
            tile_loop(act, k, body)

        if store is not None:
            @block.sync
            def _(sp):
                def body(t, b, i, last):
                    sp.wait_ge(taken[b], i + 2)
                    sp.dma_start(store[bass.ds(t * P, P), :], tile_of(k.AGG, t)).then_inc(stored, 16)
                tile_loop(sp, k, body)
                sp.wait_ge(stored, 16 * NT)


def keep(k):
    return lambda act, t, ps, junk: act.activation(tile_of(k.AGG, t), ps, ACT.Copy)


def first_linear(k):
    with Scope(k.nc, "l0d") as s:
        block = s.block()
        own = s.sem("own")

        @block.vector
        def _(v):
            me = Steps(v, own)
            me.done(v.tensor_scalar(k.rdeg[:, :], k.AGG[:, :, D], 1.0, None, ALU.max))
            me.sync()
            me.done(v.reciprocal(k.rdeg[:, :], k.rdeg[:, :]))

    def fill(v, t, dst):
        v.tensor_scalar(dst[:, 0:D], tile_of(k.AGG, t), col(k.rdeg, t), None, ALU.mult)
        return normed(k, v, t, dst[:, D:2 * D])

    def evacuate(act, t, ps, junk):
        act.activation(tile_of(k.AGG, t), ps, ACT.Copy)
        return act.activation(junk, ps, ACT.Square, accum_out=col(k.ssq, t))

    plan = [(a, (k.WlT if a < KK else k.WrT)[:, a % KK, :], 0, D) for a in range(2 * KK)]
    plan.append((None, k.b_l[0:1, :], 0, D))
    node_product(k, "l0", 2 * KK, fill, plan, evacuate)


def diagonal_plan(first, w):
    return [(first + h, w[:, h, :], h * P, P) for h in range(KK)]


def scale_rows(k):
    with Scope(k.nc, "l2") as s:
        own, rooted = s.sem("own"), s.sem("rooted")
        block = s.block()

        @block.scalar
        def _(act):
            act.activation(k.ssq[:, :], k.ssq[:, :], ACT.Sqrt).then_inc(rooted, 1)

        @block.vector
        def _(v):
            me = Steps(v, own)
            v.wait_ge(rooted, 1)
            me.done(v.tensor_scalar(k.ssq[:, :], k.ssq[:, :], 1e-12, None, ALU.max))
            me.sync()
            me.done(v.reciprocal(k.ssq[:, :], k.ssq[:, :]))
            me.sync()
            with seven_loop(v, k) as i:
                for t in (i * SEVEN + j for j in range(SEVEN)):
                    v.tensor_scalar(tile_of(k.AGG, t), tile_of(k.AGG, t), col(k.ssq, t), None, ALU.mult)


def column_stats(k, stage, n):
    NT, r = k.NT, D - n
    with Scope(k.nc, stage) as s:
        sq = s.sb("sq", [P, 2, D])
        mu = s.sb("mu", [P, D])
        p_m, p_s = s.ps("p_m", [P, 512]), s.ps("p_s", [P, 512])
        summed, mu_ready, centred, var_ready, rooted, own, ticks = (
            s.sem(x) for x in ("summed", "mu_ready", "centred", "var_ready", "rooted", "own", "ticks"))
        squared, added = s.sems("squared", 2), s.sems("added", 2)
        block = s.block()

        def ones(last):
            return (k.ones_valid if last else k.ones)[:, :]

        @block.tensor
        def _(pe):
            def first(t, b, i, last):
                pe.matmul(p_m[:, 0:n], ones(last), tile_of(k.AGG, t, 0, n), start=False, stop=last)
            pe.matmul(p_m[:, 0:n], k.zeros[:, :], k.X[:, 0, 0:n], start=True, stop=False)
            tile_loop(pe, k, first)
            pe.matmul(p_m[:, 0:1], k.zeros[:, :], k.X[:, 0, 0:1], start=False, stop=True,
                      skip_group_check=True).then_inc(summed, 1)
            for b in range(2):
                pe.sem_inc(added[b], 1)

            def second(t, b, i, last):
                pe.wait_ge(squared[b], i + 1)
                pe.matmul(p_s[:, 0:D], ones(last), sq[:, b, :], start=False, stop=last).then_inc(added[b], 1)
            pe.matmul(p_s[:, 0:D], k.zeros[:, :], k.X[:, 0, 0:D], start=True, stop=False)
            tile_loop(pe, k, second)

        @block.vector
        def _(v):
            me = Steps(v, own)
            v.wait_ge(summed, 1)
            me.done(v.tensor_scalar(mu[:, 0:n], p_m[:, 0:n], 1.0 / k.N, None, ALU.mult))
            me.sync()
            with v.Fori(0, NT) as t:
                v.tensor_tensor(tile_of(k.AGG, t, 0, n), tile_of(k.AGG, t, 0, n), mu[:, 0:n],
                                ALU.subtract).then_inc(centred, 1)
            v.wait_ge(added[0], NT // 2 + 2)
            if r:
                me.done(v.tensor_copy(mu[:, n:D], p_s[:, n:D]))
                me.sync()
                me.done(v.tensor_tensor(mu[:, n:n + C], mu[:, n:n + C], mu[:, n + C:n + 2 * C], ALU.add))
                me.sync()
                me.done(v.tensor_tensor(mu[:, n:n + C], mu[:, n:n + C], mu[:, n + 2 * C:D], ALU.add))
                me.sync()
                me.done(v.tensor_scalar(k.cscale[:, n:D].rearrange("p (x c) -> p x c", c=C),
                                        mu[:, n:n + C].unsqueeze(1).to_broadcast([P, 3, C]),
                                        1.0 / (3 * k.N), 1e-5, ALU.mult, ALU.add))
            me.done(v.tensor_scalar(k.cscale[:, 0:n], p_s[:, 0:n], 1.0 / k.N, 1e-5, ALU.mult, ALU.add)
                    )
            me.sync()
            v.sem_inc(var_ready, 1)
            v.wait_ge(rooted, 1)
            me.done(v.reciprocal(k.cscale[:, :], k.cscale[:, :]))

        @block.scalar
        def _(act):
            def body(t, b, i, last):
                apart(act, centred, t + 1, ticks)
                apart(act, added[b], i + 1, ticks)
                act.activation(sq[:, b, :], tile_of(k.AGG, t), ACT.Square).then_inc(squared[b], 1)
            tile_loop(act, k, body)
            act.wait_ge(var_ready, 1)
            act.activation(k.cscale[:, :], k.cscale[:, :], ACT.Sqrt).then_inc(rooted, 1)


def add_normed(k, stage, gamma, beta, n, relu, channel_major):
    with Scope(k.nc, stage) as s:
        own = s.sem("own")
        block = s.block()

        @block.vector
        def _(v):
            me = Steps(v, own)
            me.done(v.tensor_tensor(k.cscale[:, :], k.cscale[:, :], gamma, ALU.mult))
            me.sync()

            def body(tiles, i, per):
                me.enter(i, per)
                for t in tiles:
                    me.done(v.tensor_tensor(tile_of(k.AGG, t), tile_of(k.AGG, t), k.cscale[:, :], ALU.mult))
                me.sync()
                for t in tiles:
                    me.done(v.tensor_tensor(tile_of(k.AGG, t, 0, n), tile_of(k.AGG, t, 0, n), beta, ALU.add))
                me.sync()
                for t in tiles:
                    if relu:
                        me.done(v.scalar_tensor_tensor(out=tile_of(k.X, t), in0=tile_of(k.AGG, t), scalar=0.0,
                                                       in1=tile_of(k.X, t), op0=ALU.max, op1=ALU.add))
                    elif channel_major:
                        me.done(v.tensor_tensor(tile_of(k.X, t, 0, C), tile_of(k.AGG, t, 0, C),
                                                tile_of(k.X, t, 0, C), ALU.add))
                        xv = tile_of(k.X, t, C, D).rearrange("p (c x) -> p x c", x=3)
                        me.done(v.tensor_tensor(xv, tile_of(k.AGG, t, C, D).rearrange("p (x c) -> p x c", x=3),
                                                xv, ALU.add))
            per = SEVEN * (3 if relu else 4)
            with seven_loop(v, k) as i:
                body([i * SEVEN + j for j in range(SEVEN)], i, per)
            me.leave(k.NT // SEVEN)


def polynomial(k):
    NB = 7
    assert k.NT % NB == 0
    with Scope(k.nc, "po") as s:
        vv, sq3 = s.sb("vv", [P, NB, C]), s.sb("sq3", [P, NB, 3, C])
        a2 = s.sb("a2", [P, NB, C])
        f, g = s.sb("f", [P, NB, 2, C]), s.sb("g", [P, NB, 2, C])
        own, squared, used, ticks = s.sem("own"), s.sem("squared"), s.sem("used"), s.sem("ticks")
        block = s.block()

        def b(x):
            return x.unsqueeze(1).to_broadcast([P, NB] + list(x.shape[1:]))

        def two(x):
            return x.unsqueeze(2).to_broadcast([P, NB, 2, C])

        @block.scalar
        def _(act):
            with act.Fori(0, k.NT // NB) as i:
                apart(act, used, i + 1, ticks)
                act.activation(sq3[:, :, :, :].rearrange("p t x c -> p t (x c)"), k.AGG[:, bass.ds(i * NB, NB), C:D],
                               ACT.Square).then_inc(squared, 1)

        @block.vector
        def _(v):
            me = Steps(v, own)
            v.sem_inc(used, 1)
            with v.Fori(0, k.NT // NB) as i:
                me.enter(i, 11)
                A0 = k.AGG[:, bass.ds(i * NB, NB), 0:C]
                A1 = k.AGG[:, bass.ds(i * NB, NB), C:D].rearrange("p t (x c) -> p t x c", x=3)
                v.wait_ge(used, i + 1)
                me.done(v.tensor_tensor(a2[:, :, :], A0, A0, ALU.mult))
                me.done(v.tensor_tensor(f[:, :, :, :], two(A0), b(k.poly[:, 1]), ALU.mult))
                v.wait_ge(squared, i + 1)
                me.done(v.tensor_tensor(vv[:, :, :], sq3[:, :, 0, :], sq3[:, :, 1, :], ALU.add))
                me.sync()
                me.done(v.tensor_tensor(vv[:, :, :], vv[:, :, :], sq3[:, :, 2, :], ALU.add))
                me.done(v.tensor_tensor(g[:, :, :, :], two(a2[:, :, :]), b(k.poly[:, 2]), ALU.mult))
                me.done(v.tensor_tensor(f[:, :, :, :], f[:, :, :, :], b(k.poly[:, 0]), ALU.add))
                me.sync()
                me.done(v.tensor_tensor(f[:, :, :, :], f[:, :, :, :], g[:, :, :, :], ALU.add))
                me.sync()
                me.done(v.tensor_tensor(g[:, :, :, :], two(vv[:, :, :]), b(k.poly[:, 3]), ALU.mult))
                me.sync()
                me.done(v.tensor_tensor(f[:, :, :, :], f[:, :, :, :], g[:, :, :, :], ALU.add))
                me.done(v.tensor_tensor(a2[:, :, :], vv[:, :, :], b(k.poly_vv[:, :]), ALU.mult))
                me.sync()
                me.done(v.tensor_tensor(A0, A0, f[:, :, 0, :], ALU.mult))
                v.tensor_tensor(A1, A1, f[:, :, 1, :].unsqueeze(2).to_broadcast([P, NB, 3, C]), ALU.mult)
                me.sync()
                v.tensor_tensor(A0, A0, a2[:, :, :], ALU.add).then_inc(used, 1)
            me.leave(k.NT // NB)




def load_experts(k, sp, *weights):
    for e in range(weights[0].shape[0]):
        for i, w in enumerate(weights):
            sp.dma_start(k.WALL[:, e, i, :, :], w[e].rearrange("(kk p) n -> p kk n", p=P)).then_inc(k.experts_in, 16)


def top_bits(v, hi, x):
    return v.tensor_copy(hi, x)


def low_bits(v, lo, x, hi):
    return v.tensor_tensor(lo, x, hi, ALU.subtract)


def in_parts(lhs, rhs):
    (lh, ll), (rh, rl) = lhs, rhs
    return [(lh, rh), (lh, rl), (ll, rh)]


def experts(k, stage, E, scales, biases, last_bias, top2, router, out=None):
    NT = k.NT
    full, rest = NT // CHUNK, NT % CHUNK
    assert rest and full
    with Scope(k.nc, stage) as s:
        store = s.sb("w_hi", [P, k.STORE], F32R)
        w_hi = store[:, 0:k.E0 * 3 * KK * D].rearrange("p (e i a n) -> p e i a n", e=k.E0, i=3, a=KK)
        w_lo = s.sb("w_lo", [P, k.E0, 3, KK, D], F32R)
        xn = s.sb("xn", [P, CHUNK, D])
        xT = s.sb("xT", [P, 2, KK, CHUNK * P], F32R)
        raw = s.sb("raw", [P, KK, CHUNK * P])
        h1, h2 = s.sb("h1", [P, 2, 2, KK, CHUNK * P], F32R), s.sb("h2", [P, 2, 2, KK, CHUNK * P], F32R)
        rT = s.sb("rT", [P, CHUNK * P])
        wT = rT[0:E, :]
        r_w = router.w1 if top2 else router.w2
        r_hi, r_lo = s.sb("r_hi", list(r_w.shape), F32R), s.sb("r_lo", list(r_w.shape), F32R)
        lg, ex, wt = (s.sb(n, [P, CHUNK, E]) for n in ("lg", "ex", "wt"))
        r1, r2, r3, r4 = (s.sb(n, [P, CHUNK, 1]) for n in ("r1", "r2", "r3", "r4"))
        s1, s2 = s.sb("s1", [P, CHUNK, E]), s.sb("s2", [P, CHUNK, E])
        p_x, p_1, p_2, p_y = (s.ps(n, [P, 2, 512]) for n in ("p_x", "p_1", "p_2", "p_y"))
        xn_ready, turned, xT_own, xT_ready, xT_used, r_mm, r_act, l_mm, ex_in, ex_out, w_ready, wT_mm, wT_v = (
            s.sem(n) for n in ("xn_ready", "turned", "xT_own", "xT_ready", "xT_used", "r_mm", "r_act", "l_mm",
                               "ex_in", "ex_out", "w_ready", "wT_mm", "wT_v"))
        h1_mm, h1_act, h2_mm, h2_act, parts_done, y_mm, y_added, own, parts_own, w_parts, stored, ticks = (
            s.sem(n) for n in ("h1_mm", "h1_act", "h2_mm", "h2_act", "parts_done", "y_mm", "y_added",
                               "own", "parts_own", "w_parts", "stored", "ticks"))
        block = s.block()

        def chunks(eng, body, me=None, per=0):
            def first_ahead(f):
                f(1, 0, CHUNK)
            if me:
                me.enter(0, per)
            body(0, full * CHUNK, rest, first_ahead)
            if me:
                me.leave(1)
            with eng.Fori(0, full) as c:
                def ahead(f):
                    if full > 1:
                        with eng.If(c < full - 1):
                            f(c + 2, c * CHUNK + CHUNK, CHUNK)
                if me:
                    me.enter(c, per)
                body(c + 1, c * CHUNK, CHUNK, ahead)
            if me:
                me.leave(full)

        def part_number(n, layer, e):
            step = (0 if e == 0 else 2 * e - 1) if layer == 1 else min(2 * e + 2, 2 * E - 1)
            return n * 4 * E + 2 * step

        @block.vector
        def _(v):
            me = Steps(v, own)

            def norm_ahead(n, t, nt):
                v.wait_ge(turned, n + 1)
                for j in range(nt):
                    if not isinstance(t, int):
                        tile = k.nc.s_assert_within(t + j, 0, NT - 1, skip_runtime_bounds_check_because="a next chunk")
                    else:
                        tile = t + j
                    last = normed(k, v, tile, xn[:, j, :])
                last.then_inc(xn_ready, 1)

            def split_xT(n, t, nt):
                W = nt * P
                v.wait_ge(turned, n + 2)
                v.wait_ge(xT_used, n + 1)
                top_bits(v, xT[:, 0, :, 0:W], p_x[:, :, 0:W]).then_inc(xT_own, 1)
                v.wait_ge(xT_own, n + 1)
                low_bits(v, xT[:, 1, :, 0:W], p_x[:, :, 0:W], xT[:, 0, :, 0:W]).then_inc(xT_ready, 1)

            def split(layer, e, n, nt):
                h, acted = ((h1, h1_act), (h2, h2_act))[layer - 1]
                b, W = h[:, e % 2], nt * P
                for m in range(2):
                    v.wait_ge(acted, n * 2 * E + 2 * e + m + 3)
                    top_bits(v, b[:, 0, m, 0:W], raw[:, m, 0:W]).then_inc(parts_own, 1)
                for m in range(2):
                    v.wait_ge(parts_own, part_number(n, layer, e) + m + 1)
                    low_bits(v, b[:, 1, m, 0:W], raw[:, m, 0:W], b[:, 0, m, 0:W]).then_inc(parts_done, 1)

            def split_first(n, t, nt):
                split(1, 0, n, nt)

            def body(n, t0, nt, ahead):
                W = nt * P
                L, X_, W_ = lg[:, 0:nt, :], ex[:, 0:nt, :], wt[:, 0:nt, :]
                a, b, c3, d = (r[:, 0:nt, :] for r in (r1, r2, r3, r4))
                S1, S2 = s1[:, 0:nt, :], s2[:, 0:nt, :]

                def wide(r):
                    return r.to_broadcast([P, nt, E])

                def routing():
                    rb = router.bias.unsqueeze(1).to_broadcast([P, nt, E])
                    v.wait_ge(l_mm, n + 1)
                    me.done(v.tensor_tensor(L, p_x[:, 0, 0:nt * E].rearrange("p (j e) -> p j e", e=E), rb, ALU.add))
                    me.sync()
                    me.done(v.tensor_reduce(a, L, AX.X, ALU.max))
                    me.sync()
                    me.done(v.tensor_tensor(L, L, wide(a), ALU.subtract))
                    me.sync()
                    v.sem_inc(ex_in, 1)
                    v.wait_ge(ex_out, n * (2 if top2 else 1) + 1)
                    me.done(v.tensor_reduce(a, X_, AX.X, ALU.add))
                    me.sync()
                    me.done(v.reciprocal(b, a))
                    me.sync()
                    if not top2:
                        me.done(v.tensor_tensor(W_, X_, wide(b), ALU.mult))
                        me.sync()
                        v.sem_inc(w_ready, 1)
                        return
                    rank = k.rank[:, 0:E].unsqueeze(1).to_broadcast([P, nt, E])
                    me.done(v.tensor_tensor(L, X_, wide(b), ALU.mult))
                    me.sync()
                    for top, S in ((c3, S1), (d, S2)):
                        me.done(v.tensor_reduce(top, L, AX.X, ALU.max))
                        me.sync()
                        me.done(v.tensor_tensor(S, L, wide(top), ALU.is_equal))
                        me.sync()
                        me.done(v.tensor_tensor(S, S, rank, ALU.mult))
                        me.sync()
                        me.done(v.tensor_reduce(a, S, AX.X, ALU.max))
                        me.sync()
                        me.done(v.tensor_tensor(S, S, wide(a), ALU.is_equal))
                        me.sync()
                        if S is S1:
                            me.done(v.scalar_tensor_tensor(out=L, in0=S, scalar=-2.0, in1=L, op0=ALU.mult, op1=ALU.add))
                            me.sync()
                    me.done(v.tensor_tensor(a, d, c3, ALU.subtract))
                    me.sync()
                    v.sem_inc(ex_in, 1)

                def routing_end():
                    v.wait_ge(ex_out, n * 2 + 2)
                    me.done(v.tensor_scalar(b, d, 1.0, None, ALU.add))
                    me.sync()
                    me.done(v.reciprocal(b, b))
                    me.sync()
                    me.done(v.tensor_tensor(d, d, b, ALU.mult))
                    me.done(v.tensor_tensor(S1, S1, wide(b), ALU.mult))
                    me.sync()
                    me.done(v.tensor_tensor(S2, S2, wide(d), ALU.mult))
                    me.sync()
                    me.done(v.tensor_tensor(W_, S1, S2, ALU.add))
                    me.sync()
                    v.sem_inc(w_ready, 1)

                def add_y(e):
                    v.wait_ge(y_mm, n * (E + 1) + e + 2)
                    if e >= 0:
                        v.wait_ge(y_added, n * (E + 1) + e + 2)
                    for j in range(nt):
                        y = p_y[:, j // 2, j % 2 * D:(j % 2 + 1) * D]
                        xt = tile_of(k.X, t0 + j)
                        if e < 0:
                            last = v.tensor_tensor(xt, y, xt, ALU.add)
                        else:
                            last = v.scalar_tensor_tensor(out=xt, in0=y, scalar=wt[:, j, e:e + 1], in1=xt,
                                                          op0=ALU.mult, op1=ALU.add)
                    last.then_inc(y_added, 1)
                for st in range(E + 3):
                    if st == 2:
                        v.wait_ge(wT_mm, n + 1)
                        v.tensor_copy(wT[:, 0:W], p_x[0:E, 1, 0:W]).then_inc(wT_v, 1)
                        add_y(-1)
                    if 3 <= st < E + 2:
                        add_y(st - 3)
                    if 1 <= st < E:
                        split(1, st, n, nt)
                    if st == 0:
                        routing()
                    if st == 1 and top2:
                        routing_end()
                    if 1 <= st <= E:
                        split(2, st - 1, n, nt)
                    if st == E - 3:
                        ahead(norm_ahead)
                    if st == E:
                        ahead(split_xT)
                    if st == E + 1:
                        ahead(split_first)
                    if st == E + 2:
                        add_y(E - 1)
            v.sem_inc(y_added, 1)
            norm_ahead(0, full * CHUNK, rest)
            v.wait_ge(k.experts_in, 16 * 3 * (k.E0 + k.E1 if top2 else k.E0))
            me.done(top_bits(v, r_hi[:], r_w[:]))
            me.sync()
            me.done(low_bits(v, r_lo[:], r_w[:], r_hi[:]))
            split_xT(0, full * CHUNK, rest)
            for e in range(E):
                me.done(top_bits(v, w_hi[:, e], k.WALL[:, e]))
                me.sync()
                low_bits(v, w_lo[:, e], k.WALL[:, e], w_hi[:, e]).then_inc(w_parts, 1)
            split_first(0, 0, rest)
            chunks(v, body, me, 6 if not top2 else 5 + 1 + 11 + 1 + 6)

        @block.scalar
        def _(act):
            act.sem_inc(h1_act, 2)
            act.sem_inc(h2_act, 2)
            act.sem_inc(parts_done, 2)

            def relu(dst, src, l, e, m):
                scale = scales[l][:, 2 * e + m:2 * e + m + 1] if scales else 1.0
                return act.activation(dst, src, ACT.Relu, bias=biases[l][:, 2 * e + m:2 * e + m + 1], scale=scale)

            def body(n, t0, nt, ahead):
                W = nt * P
                if top2:
                    act.wait_ge(r_mm, n + 1)
                    act.activation(rT[:, 0:W], p_x[:, 1, 0:W], ACT.Relu, bias=router.b1).then_inc(r_act, 1)
                for st in range(E + 1):
                    if st < E:
                        for m in range(2):
                            apart(act, parts_done, part_number(n, 1, st) + m + 1, ticks)
                            act.wait_ge(h1_mm, n * 2 * E + 2 * st + m + 1)
                            relu(raw[:, m, 0:W], p_1[:, m, 0:W], 0, st, m).then_inc(h1_act, 1)
                    if st == 0:
                        act.wait_ge(ex_in, n * (2 if top2 else 1) + 1)
                        act.activation(ex[:, 0:nt, :], lg[:, 0:nt, :], ACT.Exp).then_inc(ex_out, 1)
                    if st == 1 and top2:
                        act.wait_ge(ex_in, n * 2 + 2)
                        act.activation(r4[:, 0:nt, :], r1[:, 0:nt, :], ACT.Exp).then_inc(ex_out, 1)
                    if st >= 1:
                        for m in range(2):
                            apart(act, parts_done, part_number(n, 2, st - 1) + m + 1, ticks)
                            act.wait_ge(h2_mm, n * 2 * E + 2 * (st - 1) + m + 1)
                            relu(raw[:, m, 0:W], p_2[:, m, 0:W], 1, st - 1, m).then_inc(h2_act, 1)
            chunks(act, body)

        @block.tensor
        def _(pe):
            pe.sem_inc(turned, 1)
            pe.sem_inc(xT_used, 1)

            def product(dst, pairs):
                terms = [x for lhs, rhs in pairs for x in in_parts(lhs, rhs)]
                for i, (a, b) in enumerate(terms):
                    mm = pe.matmul(dst, a, b, start=(i == 0), stop=(i == len(terms) - 1))
                return mm

            def turn_ahead(n, t, nt):
                pe.wait_ge(xn_ready, n + 1)
                if not isinstance(n, int) or n:
                    pe.wait_ge(wT_v, n)
                for kk in range(KK):
                    for j in range(nt):
                        mm = pe.transpose(p_x[:, kk, j * P:(j + 1) * P], xn[:, j, kk * P:(kk + 1) * P], k.ident[:, :])
                mm.then_inc(turned, 1)

            def x(kk, a, b):
                return tuple(xT[:, i, kk, a:b] for i in range(2))

            def weights(e, i, kk, a, b):
                return w_hi[:, e, i, kk, a:b], w_lo[:, e, i, kk, a:b]

            def layer1(e, n, nt):
                W = nt * P
                if isinstance(n, int):
                    pe.wait_ge(w_parts, e + 1)
                for m in range(2):
                    pe.wait_ge(h1_act, n * 2 * E + 2 * e + m + 1)
                    mm = product(p_1[:, m, 0:W], [(weights(e, 0, kk, m * P, (m + 1) * P), x(kk, 0, W))
                                                  for kk in range(KK)])
                    mm.then_inc(h1_mm, 1)
                if e == E - 1:
                    pe.sem_inc(xT_used, 1)

            def begin(n, t, nt):
                W = nt * P

                def rw(kk):
                    return r_hi[:, kk, :], r_lo[:, kk, :]
                pe.wait_ge(xT_ready, n + 1)
                if top2:
                    product(p_x[:, 1, 0:W], [(rw(kk), x(kk, 0, W)) for kk in range(KK)]).then_inc(r_mm, 1)
                else:
                    for j in range(nt):
                        mm = product(p_x[:, 0, j * E:(j + 1) * E],
                                     [(x(kk, j * P, (j + 1) * P), rw(kk)) for kk in range(KK)])
                    mm.then_inc(l_mm, 1)
                layer1(0, n, nt)

            def body(n, t0, nt, ahead):
                W = nt * P

                def layer2(e):
                    pe.wait_ge(parts_done, part_number(n, 1, e) + 4)
                    for m in range(2):
                        pe.wait_ge(h2_act, n * 2 * E + 2 * e + m + 1)
                        mm = product(p_2[:, m, 0:W], [(weights(e, 1, kk, m * P, (m + 1) * P),
                                                       tuple(h1[:, e % 2, i, kk, 0:W] for i in range(2)))
                                                      for kk in range(KK)])
                        mm.then_inc(h2_mm, 1)

                def layer3(e):
                    pe.wait_ge(parts_done, part_number(n, 2, e) + 4)
                    pe.wait_ge(y_added, n * (E + 1) + e + 2)
                    for j in range(nt):
                        mm = product(p_y[:, j // 2, j % 2 * D:(j % 2 + 1) * D],
                                     [(tuple(h2[:, e % 2, i, kk, j * P:(j + 1) * P] for i in range(2)),
                                       weights(e, 2, kk, 0, D)) for kk in range(KK)])
                    mm.then_inc(y_mm, 1)

                for st in range(E + 2):
                    if 1 <= st < E:
                        layer1(st, n, nt)
                    if st == E + 1:
                        ahead(begin)
                    if st == 0 and top2:
                        pe.wait_ge(r_act, n + 1)
                        for j in range(nt):
                            mm = pe.matmul(p_x[:, 0, j * E:(j + 1) * E], rT[:, j * P:(j + 1) * P],
                                           router.w2[:, :], start=True, stop=True)
                        mm.then_inc(l_mm, 1)
                    if st == 2:
                        pe.wait_ge(wT_v, n + 1)
                        pe.wait_ge(y_added, n * (E + 1) + 1)
                        for j in range(nt):
                            mm = pe.matmul(p_y[:, j // 2, j % 2 * D:(j % 2 + 1) * D], wT[:, j * P:(j + 1) * P],
                                           last_bias, start=True, stop=True)
                        mm.then_inc(y_mm, 1)
                    if 0 <= st - 1 < E:
                        layer2(st - 1)
                    if st == 1:
                        pe.wait_ge(w_ready, n + 1)
                        for j in range(nt):
                            mm = pe.transpose(p_x[0:E, 1, j * P:(j + 1) * P], wt[:, j, :], k.ident[:, :])
                        mm.then_inc(wT_mm, 1)
                    if 0 <= st - 2 < E:
                        layer3(st - 2)
                    if st == E - 2:
                        ahead(turn_ahead)
            turn_ahead(0, full * CHUNK, rest)
            begin(0, full * CHUNK, rest)
            chunks(pe, body)

        if out is not None:
            @block.sync
            def _(sp):
                n = 0
                sp.wait_ge(y_added, E + 2)
                for t in range(full * CHUNK, NT):
                    rows = P if t < NT - 1 else k.LAST
                    sp.dma_start(out[t * P:t * P + rows, :], k.X[0:rows, t, :]).then_inc(stored, 16)
                    n += 1
                with sp.Fori(0, full) as c:
                    sp.wait_ge(y_added, (c + 2) * (E + 1) + 1)
                    sp.dma_start(out[bass.ds(c * CHUNK * P, CHUNK * P), :].rearrange("(j p) d -> p j d", p=P),
                                 k.X[:, bass.ds(c * CHUNK, CHUNK), :]).then_inc(stored, 16)
                sp.wait_ge(stored, 16 * (n + full))




def program(nc, a, out):
    Scope.used.clear()
    k = Shared()
    k.nc = nc
    k.N = a["x"].shape[0]
    k.NT = -(-k.N // P)
    k.LAST = k.N - (k.NT - 1) * P
    k.NG = a["edges"].shape[0] * SLOTS
    k.E0, k.E1 = a["L0_ffn_W1"].shape[0], a["L1_ffn_expert_w1"].shape[0]
    NT = k.NT
    k.STORE = max(NT * (D + 1), k.E0 * 3 * KK * D)
    k.x, k.edges, k.dst_line = a["x"], a["edges"], a["dst_line"]
    k.attr16, k.attr4 = a["attr16"], a["attr4"]
    k.W1_0, k.W2_0, k.W3_0 = a["L0_ffn_W1"], a["L0_ffn_W2"], a["L0_ffn_Wo"]
    k.W1_1, k.W2_1, k.W3_1 = a["L1_ffn_expert_w1"], a["L1_ffn_expert_w2"], a["L1_ffn_expert_w3"]
    k.table = nc.dram_tensor("table", (k.NG, 4), I32).ap()
    k.xn_tab = nc.dram_tensor("xn_tab", (NT * P, D), F32).ap()
    k.up_tab = nc.dram_tensor("up_tab", (NT * P, D), F32).ap()
    k.hidden = nc.dram_tensor("hidden", (k.NG // SLOTS, P, SLOTS * HALF), F32).ap()

    with Scope(nc, "g") as s:
        k.X = s.sb("X", [P, NT, D])
        k.mean, k.rstd, k.rdeg, k.ssq = (s.sb(n, [P, NT]) for n in ("mean", "rstd", "rdeg", "ssq"))
        k.lane, k.ident, k.ones, k.ones_valid, k.zeros = (
            s.sb(n, [P, P]) for n in ("lane", "ident", "ones", "ones_valid", "zeros"))
        k.M4 = s.sb("M4", [P, D])
        k.bn1, k.bn2 = s.sb("bn1", [P, 5, 2 * k.E0]), s.sb("bn2", [P, 5, 2 * k.E0])
        bo0, br0, wr0 = s.sb("bo0", [k.E0, D]), s.sb("br0", [P, k.E0]), s.sb("wr0", [P, KK, k.E0])
        bo1, rb2, rb1 = s.sb("bo1", [k.E1, D]), s.sb("rb2", [P, k.E1]), s.sb("rb1", [P, 1])
        rw1, rw2 = s.sb("rw1", [P, KK, P]), s.sb("rw2", [P, k.E1])
        eb1, eb2 = s.sb("eb1", [P, 2 * k.E1]), s.sb("eb2", [P, 2 * k.E1])
        k.rank = s.sb("rank", [P, 8])

        k.gathered = s.sems("gathered_a", SLOTS), s.sems("gathered_b", SLOTS)
        k.experts_in = s.sem("experts_in")
        Scope.used.clear()

        def rows(x):
            return x.rearrange("(kk p) n -> p kk n", p=P)

        def spread(x, n):
            return x.rearrange("(a d) -> a d", a=1).to_broadcast([P, n])

        loads = [(bo0[:, :], a["L0_ffn_bo"]), (br0[:, :], spread(a["L0_ffn_br"], k.E0)),
                 (wr0[:, :, :], rows(a["L0_ffn_Wr"])),
                 (bo1[:, :], a["L1_ffn_expert_b3"]), (rb2[:, :], spread(a["L1_ffn_router_b2"], k.E1)),
                 (rb1[:, :], a["L1_ffn_router_b1"].rearrange("(p a) -> p a", a=1)),
                 (rw1[:, :, :], rows(a["L1_ffn_router_w1"])), (rw2[:, :], a["L1_ffn_router_w2"]),
                 (eb1[:, :], a["L1_ffn_expert_b1"]), (eb2[:, :], a["L1_ffn_expert_b2"]),
                 (k.rank[:, :], a["rank"].to_broadcast([P, 8]))]
        for bn, which in ((k.bn1, "1"), (k.bn2, "2")):
            for i, n in enumerate(("b", "g", "be", "m", "v")):
                loads.append((bn[:, i, :], a[f"L0_ffn_{n}{which}"]))
        for h in range(2):
            for to, of in enumerate((0, 3, 1, 2)):
                loads.append((k.M4[C * h:C * h + C, C * to:C * to + C], a["L1_gnn_M4"][:, C * of:C * of + C]))
        k.const_loads = loads


        def late_loads(stage, loads, zero=()):
            with Scope(nc, stage) as c:
                w_in, zeroed = c.sem("w_in"), c.sem("zeroed")
                block = c.block()

                @block.vector
                def _(v):
                    for z in zero:
                        last = v.memset(z[:], 0.0)
                    if zero:
                        last.then_inc(zeroed, 1)

                @block.sync
                def _(sp):
                    if zero:
                        sp.wait_ge(zeroed, 1)
                    for dst, src in loads:
                        sp.dma_start(dst, src).then_inc(w_in, 16)
                    sp.wait_ge(w_in, 16 * len(loads))

        def rooms(x):
            k.AGG = x.sb("AGG", [P, k.STORE])[:, 0:NT * (D + 1)].rearrange("p (t d) -> p t d", d=D + 1)
            k.WALL = x.sb("WALL", [P, k.E0, 3, KK, D])
            k.cscale = x.sb("cscale", [P, D])

        with Scope(nc, "g0") as x:
            rooms(x)
            with Scope(nc, "mlp") as m:
                k.M1, k.M2, k.M3 = m.sb("M1", [32, P]), m.sb("M2", [P, P]), m.sb("M3", [P, P])
                for h in range(2):
                    loads.append((k.M1[16 * h:16 * h + 16, C * h:C * h + C], a["L1_gnn_M1"]))
                    loads += [(w[C * h:C * h + C, C * h:C * h + C], a[n])
                              for w, n in ((k.M2, "L1_gnn_M2"), (k.M3, "L1_gnn_M3"))]
                k.cleared = [k.M1, k.M2, k.M3, k.zeros]
                setup(k)
                bn_roots(k)
                norm_stats(k, "n0")
                write_xn_table(k)
                first_edges(k)
            with Scope(nc, "w0") as w:
                k.WlT, k.WrT = w.sb("WlT", [P, KK, D]), w.sb("WrT", [P, KK, D])
                k.b_l = w.sb("b_l", [1, D])
                gamma, beta = w.sb("gamma", [P, D]), w.sb("beta", [P, D])
                late_loads("w0l", [(k.b_l[:, :], a["L0_gnn_b_l"].rearrange("(a d) -> a d", a=1)),
                                   (k.WlT[:, :, :], rows(a["L0_gnn_W_lT"])), (k.WrT[:, :, :], rows(a["L0_gnn_W_rT"])),
                                   (gamma[:, :], spread(a["L0_gnn_gamma"], D)), (beta[:, :], spread(a["L0_gnn_beta"], D))])
                first_linear(k)
                scale_rows(k)
                column_stats(k, "c0", D)
                add_normed(k, "a0", gamma[:, :], beta[:, :], D, True, False)
            norm_stats(k, "n1")
        experts(k, "f0", k.E0, (k.bn1[:, 1, :], k.bn2[:, 1, :]), (k.bn1[:, 2, :], k.bn2[:, 2, :]), bo0[:, :], False,
                Router(w2=wr0, bias=br0[:, :]))
        clear_semaphores(nc)
        with Scope(nc, "g1") as x:
            rooms(x)
            norm_stats(k, "n2")
            with Scope(nc, "w1") as w:
                ups = w.sb("ups", [P, KK, P])
                late_loads("w1l", block_diagonal_loads(ups, a["L1_gnn_W_up0"], a["L1_gnn_W_up1"]), [ups])
                node_product(k, "up", KK, lambda v, t, dst: normed(k, v, t, dst, True), diagonal_plan(0, ups), keep(k),
                             store=k.up_tab)
            second_edges(k)
            clear_semaphores(nc)
            with Scope(nc, "w2") as w:
                lins, wbs, wscs = (w.sb(n, [P, KK, P]) for n in ("lins", "wbs", "wscs"))
                k.poly, k.poly_vv = w.sb("poly", [P, 4, 2, C]), w.sb("poly_vv", [P, C])
                gamma, beta = w.sb("gamma", [P, D]), w.sb("beta", [P, C])
                c0, c1 = a["L1_gnn_Wc0T"], a["L1_gnn_Wc1T"]

                def line(x):
                    return x.to_broadcast([P, C])
                polys = [(k.poly[:, i, 0, :], line(c0[n:n + 1, :])) for i, n in enumerate((0, 1, 3, 4))]
                polys += [(k.poly[:, i, 1, :], line(c1[i:i + 1, :])) for i in range(4)]
                polys.append((k.poly_vv[:, :], line(c0[2:3, :])))
                gammas = [(gamma[:, 0:C], spread(a["L1_gnn_gamma0"], C)), (beta[:, :], spread(a["L1_gnn_beta0"], C))]
                gammas += [(gamma[:, C + C * x:2 * C + C * x], spread(a["L1_gnn_gamma1"], C)) for x in range(3)]
                late_loads("w2l", block_diagonal_loads(lins, a["L1_gnn_W_lin0"], a["L1_gnn_W_lin1"])
                           + block_diagonal_loads(wbs, a["L1_gnn_WB0"], a["L1_gnn_WB1"])
                           + block_diagonal_loads(wscs, a["L1_gnn_Wsc0"], a["L1_gnn_Wsc1"]) + polys + gammas,
                           [lins, wbs, wscs])
                node_product(k, "li", KK, lambda v, t, dst: v.tensor_copy(dst[:, 0:D], tile_of(k.AGG, t)),
                             diagonal_plan(0, lins), keep(k))
                polynomial(k)

                def fill(v, t, dst):
                    v.tensor_copy(dst[:, 0:D], tile_of(k.AGG, t))
                    return normed(k, v, t, dst[:, D:2 * D], True)
                node_product(k, "ob", 2 * KK, fill,
                             [x for h in range(KK) for x in (diagonal_plan(0, wbs)[h], diagonal_plan(KK, wscs)[h])],
                             keep(k))
                column_stats(k, "c1", C)
                add_normed(k, "a1", gamma[:, :], beta[:, :], C, False, True)
            norm_stats(k, "n3")
        experts(k, "f1", k.E1, None, (eb1[:, :], eb2[:, :]), bo1[:, :], True,
                Router(w1=rw1, b1=rb1[:, 0:1], w2=rw2, bias=rb2[:, :]), out=out)


def block_diagonal_loads(buf, w0, w1):
    return [(buf[0:C, 0, 0:C], w0), (buf[C:P, 0, C:P], w1), (buf[0:C, 1, 0:C], w1), (buf[C:P, 1, C:P], w1)]




def lay_out(inputs):
    import numpy as np

    a = {n: np.asarray(v) for n, v in inputs.items()}
    n, e = a["x"].shape[0], a["src"].shape[0]
    ng = -(-e // (GE * ROUND)) * ROUND
    pad = ng * GE - e
    src = np.concatenate([a.pop("src"), np.zeros(pad, np.int32)]).astype(np.int32, copy=False)
    dst = np.concatenate([a.pop("dst"), np.full(pad + 1, NO_NODE, np.int32)]).astype(np.int32, copy=False)

    def by_slots(v):
        return v.reshape(ng // SLOTS, SLOTS, G, P, -1).transpose(0, 3, 1, 2, 4)
    a["dst_line"] = dst
    a["edges"] = np.concatenate([by_slots(src)[..., 0], by_slots(dst[:-1])[..., 0]], -1).reshape(ng // SLOTS, P, -1)
    attr4 = np.concatenate([a.pop("edge_attr_4"), np.zeros((pad, 4), np.float32)])
    a["attr4"] = by_slots(attr4).reshape(ng // SLOTS, P, -1)
    attr16 = np.concatenate([a.pop("edge_attr_16"), np.zeros((pad, 16), np.float32)])
    a["attr16"] = attr16.reshape(ng // SLOTS, SLOTS, 2, HALF, 16).transpose(0, 2, 4, 1, 3).reshape(
        ng // SLOTS, 32, SLOTS * HALF)
    a["rank"] = np.arange(8, 0, -1, dtype=np.float32)[None]
    for w in ("W_l", "W_r"):
        a[f"L0_gnn_{w}T"] = a.pop(f"L0_gnn_{w}").T
    for w in ("Wc0", "Wc1"):
        a[f"L1_gnn_{w}T"] = a.pop(f"L1_gnn_{w}").T
    for name in [f"L0_ffn_{x}{i}" for x in ("b", "g", "be", "m", "v") for i in (1, 2)] + [
            "L1_ffn_expert_b1", "L1_ffn_expert_b2"]:
        ex = a[name].shape[0]
        a[name] = a[name].reshape(ex, 2, P).transpose(2, 0, 1).reshape(P, 2 * ex)
    return {n: np.ascontiguousarray(v) for n, v in a.items()}


def kernel(**inputs):
    import concourse.bacc as bacc
    from concourse.bass_utils import run_bass_kernel_spmd

    arrays = lay_out(inputs)
    nc = bacc.Bacc("TRN2", target_bir_lowering=False, num_devices=1)
    aps = {n: nc.dram_tensor(f"in_{n}", v.shape, mybir.dt.from_np(v.dtype), kind="ExternalInput").ap()
           for n, v in arrays.items()}
    out = nc.dram_tensor("out_dram", arrays["x"].shape, F32, kind="ExternalOutput").ap()
    program(nc, aps, out)
    r = run_bass_kernel_spmd(nc, [{f"in_{n}": v for n, v in arrays.items()}], core_ids=[0])
    return r.results[0]["out_dram"]
```

```python
from contextlib import ExitStack

import concourse.bass as bass
from concourse import mybir

F32 = mybir.dt.float32
F32R = mybir.dt.float32r
I32 = mybir.dt.int32
ALU = mybir.AluOpType
ACT = mybir.ActivationFunctionType
AX = mybir.AxisListType

P = 128
D = 256
C = 64
KK = D // P
G = 4
GE = G * P
HALF = GE // 2
SLOTS = 4
HALVES = 2
ROUND = HALVES * SLOTS
NO_NODE = 1 << 20
LN_EPS = 1e-5
CHUNK = 4


class Shared:
    pass


class Router:

    def __init__(self, w2, bias, w1=None, b1=None):
        self.w2, self.bias, self.w1, self.b1 = w2, bias, w1, b1


class Steps:

    def __init__(self, eng, sem):
        self.eng, self.sem, self.base, self.n = eng, sem, 0, 0

    def done(self, ins):
        self.n += 1
        return ins.then_inc(self.sem, 1)

    def sync(self):
        self.eng.wait_ge(self.sem, self.base + self.n)

    def enter(self, i, per):
        if self.n:
            self.base, self.n = self.base + self.n, 0
        self.start = self.base
        self.base = i * per + self.start
        self.per = per

    def leave(self, count):
        assert self.n == self.per, (self.n, self.per)
        self.base, self.n = self.start + count * self.per, 0


class Scope:

    used = []

    def __init__(self, nc, stage):
        self.nc, self.stage, self.stack = nc, stage, ExitStack()

    def __enter__(self):
        self.stack.__enter__()
        return self

    def __exit__(self, *a):
        return self.stack.__exit__(*a)

    def sb(self, name, shape, dt=F32):
        return self.stack.enter_context(self.nc.sbuf_tensor(f"{self.stage}_{name}", shape, dt))

    def ps(self, name, shape):
        return self.stack.enter_context(self.nc.psum_tensor(f"{self.stage}_{name}", shape, F32))

    def sem(self, name):
        h = self.stack.enter_context(self.nc.semaphore(f"{self.stage}_{name}"))
        self.used.append(h)
        return h

    def sems(self, name, n):
        return [self.sem(f"{name}{i}") for i in range(n)]

    def block(self):
        return self.stack.enter_context(self.nc.Block())


def clear_semaphores(nc):
    with nc.Block() as block:
        @block.gpsimd
        def _(pool):
            for h in Scope.used:
                pool.sem_clear(h)
    Scope.used.clear()


def apart(eng, sem, value, ticks):
    eng.wait_ge(sem, value)
    eng.sem_inc(ticks, 1)


def tile_loop(eng, k, body):
    assert k.NT % 2 == 1
    with eng.Fori(0, k.NT // 2) as i:
        for s in range(2):
            body(2 * i + s, s, i, False)
    body(k.NT - 1, 0, k.NT // 2, True)


def pipelined_tiles(eng, k, first, second):
    first(0, 0, 0)
    with eng.Fori(0, k.NT // 2) as i:
        first(2 * i + 1, 1, i)
        second(2 * i, 0, i)
        first(2 * i + 2, 0, i + 1)
        second(2 * i + 1, 1, i)
    second(k.NT - 1, 0, k.NT // 2)


SEVEN = 7


def seven_loop(eng, k):
    assert k.NT % SEVEN == 0
    return eng.Fori(0, k.NT // SEVEN)


def col(buf, t):
    return buf[:, bass.ds(t, 1)] if not isinstance(t, int) else buf[:, t:t + 1]


def tile_of(buf, t, a=0, b=D):
    v = buf[:, bass.ds(t, 1), a:b] if not isinstance(t, int) else buf[:, t:t + 1, a:b]
    return v.rearrange("p t d -> p (t d)")




def setup(k):
    nc, NT, NG = k.nc, k.NT, k.NG
    EC = NG * GE // P
    with Scope(nc, "su") as s:
        dst_a, dst_b = s.sb("dst_a", [P, EC], I32), s.sb("dst_b", [P, EC], I32)
        fa, fb = s.sb("fa", [P, EC]), s.sb("fb", [P, EC])
        falls = s.sb("falls", [P, 1])
        ends_i, ends = s.sb("ends_i", [1, 2, NG], I32), s.sb("ends", [1, 2, NG])
        more, before = s.sb("more", [1, NG]), s.sb("before", [1, NG])
        lane_i, part_i = s.sb("lane_i", [P, P], I32), s.sb("part_i", [P, 1], I32)
        part = s.sb("part", [P, 1])
        table = s.sb("table", [1, NG, 4], I32)
        mixed = s.sb("mixed", [1, 2])
        p_falls = s.ps("p_falls", [P, 512])
        x_in, w_in, dst_in, ends_in = (s.sem(n) for n in ("x_in", "w_in", "dst_in", "ends_in"))
        iota_done, zeroed, own, pe_done = (s.sem(n) for n in ("iota_done", "zeroed", "own", "pe_done"))
        falls_ready, table_ready, table_out = (s.sem(n) for n in ("falls_ready", "table_ready", "table_out"))
        block = s.block()

        @block.sync
        def _(sp):
            line = k.dst_line
            sp.wait_ge(zeroed, 1)
            sp.dma_start(k.X[:, 0:NT - 1, :], k.x[0:(NT - 1) * P, :].rearrange("(t p) d -> p t d", p=P)
                         ).then_inc(x_in, 16)
            sp.dma_start(k.X[0:k.LAST, NT - 1, :], k.x[(NT - 1) * P:, :]).then_inc(x_in, 16)
            sp.dma_start(dst_a[:, :], line[0:NG * GE].rearrange("(p c) -> p c", p=P)).then_inc(dst_in, 16)
            sp.dma_start(dst_b[:, :], line[1:NG * GE + 1].rearrange("(p c) -> p c", p=P)).then_inc(dst_in, 16)
            with nc.allow_non_contiguous_dma(reason="two words of each group"):
                for i, e in enumerate((0, GE - 1)):
                    sp.dma_start(ends_i[:, i, :], line[0:NG * GE].rearrange("(a g e) -> a g e", a=1, e=GE)[:, :, e]
                                 ).then_inc(ends_in, 16)
            sp.wait_ge(x_in, 32)
            sp.wait_ge(table_ready, 1)
            sp.dma_start(k.table.rearrange("(a i) f -> a i f", a=1), table[:, :, :]).then_inc(table_out, 16)
            sp.wait_ge(table_out, 16)

        @block.scalar
        def _(act):
            n = 0
            act.wait_ge(zeroed, 2)
            for dst, src in k.const_loads:
                act.dma_start(dst, src).then_inc(w_in, 16)
                n += 16
            act.wait_ge(w_in, n)

        @block.gpsimd
        def _(pool):
            pool.iota(lane_i[:, :], pattern=[[1, P]], base=0, channel_multiplier=0).then_inc(iota_done, 1)
            pool.iota(part_i[:, :], pattern=[[0, 1]], base=0, channel_multiplier=1).then_inc(iota_done, 1)

        @block.vector
        def _(v):
            me = Steps(v, own)
            v.memset(k.X[:, NT - 1, :], 0.0).then_inc(zeroed, 1)
            for buf in k.cleared:
                last = v.memset(buf[:], 0.0)
            last.then_inc(zeroed, 1)
            v.memset(k.ones_valid[:, :], 0.0)
            me.done(v.memset(k.ones[:, :], 1.0))
            me.sync()
            me.done(v.memset(k.ones_valid[0:k.LAST, :], 1.0))
            v.wait_ge(iota_done, 2)
            v.tensor_copy(k.lane[:, :], lane_i[:, :])
            me.done(v.tensor_copy(part[:, :], part_i[:, :]))
            me.sync()
            me.done(v.tensor_scalar(k.ident[:, :], k.lane[:, :], part[:, 0:1], None, ALU.is_equal))
            v.wait_ge(dst_in, 32)
            v.tensor_copy(fa[:, :], dst_a[:, :])
            me.done(v.tensor_copy(fb[:, :], dst_b[:, :]))
            me.sync()
            me.done(v.tensor_tensor(fa[:, :], fa[:, :], fb[:, :], ALU.is_gt))
            me.sync()
            v.reduce_sum(falls[:, :], fa[:, :], AX.X).then_inc(falls_ready, 1)
            v.wait_ge(ends_in, 32)
            me.done(v.tensor_scalar(ends_i[:, :, :], ends_i[:, :, :], P.bit_length() - 1, None, ALU.arith_shift_right))
            me.sync()
            me.done(v.tensor_copy(ends[:, :, :], ends_i[:, :, :]))
            me.sync()
            me.done(v.tensor_scalar(ends[:, :, :], ends[:, :, :], float(NT - 1), None, ALU.min))
            v.wait_ge(pe_done, 1)
            me.done(v.tensor_scalar(mixed[:, 0:1], p_falls[0:1, 0:1], 0.5, None, ALU.is_gt))
            me.sync()
            me.done(v.tensor_scalar(mixed[:, 1:2], mixed[:, 0:1], float(NT - 1), None, ALU.mult))
            me.done(v.tensor_scalar(mixed[:, 0:1], mixed[:, 0:1], -1.0, 1.0, ALU.mult, ALU.add))
            me.sync()
            me.done(v.tensor_scalar(ends[:, :, :], ends[:, :, :], mixed[:, 0:1], None, ALU.mult))
            me.sync()
            me.done(v.tensor_scalar(ends[:, 1, :], ends[:, 1, :], mixed[:, 1:2], None, ALU.add))
            me.sync()
            me.done(v.tensor_tensor(more[:, :], ends[:, 1, :], ends[:, 0, :], ALU.subtract))
            me.done(v.memset(before[:, 0:1], 0.0))
            me.sync()
            me.done(v.tensor_copy(before[:, 1:NG], more[:, 0:NG - 1]))
            me.sync()
            far, src, dst = 1, before, ends[:, 1, :]
            while far < NG:
                me.done(v.tensor_copy(dst[:, 0:far], src[:, 0:far]))
                me.done(v.tensor_tensor(dst[:, far:NG], src[:, far:NG], src[:, 0:NG - far], ALU.add))
                me.sync()
                src, dst, far = dst, src, 2 * far
            v.tensor_copy(table[:, :, 0], ends[:, 0, :])
            v.tensor_scalar(table[:, :, 1], ends[:, 0, :], float(P), None, ALU.mult)
            v.tensor_copy(table[:, :, 2], more[:, :])
            v.tensor_copy(table[:, :, 3], src[:, 0:NG]).then_inc(table_ready, 1)
            v.wait_ge(w_in, 16 * len(k.const_loads))
            batch_norm_constants(k, v, me)

        @block.tensor
        def _(pe):
            pe.wait_ge(own, 1)
            pe.wait_ge(falls_ready, 1)
            pe.matmul(p_falls[:, 0:1], k.ones[:, :], falls[:, :], start=True, stop=True).then_inc(pe_done, 1)


def batch_norm_constants(k, v, me):
    for b in (k.bn1, k.bn2):
        me.done(v.tensor_scalar(b[:, 4, :], b[:, 4, :], 1e-3, None, ALU.add))
        me.done(v.tensor_tensor(b[:, 3, :], b[:, 0, :], b[:, 3, :], ALU.subtract))
    me.done(v.tensor_scalar(k.M4[:, C:2 * C], k.M4[:, C:2 * C], float(1.0 / 3.0 ** 0.5), None, ALU.mult))


def bn_roots(k):
    with Scope(k.nc, "bn") as s:
        own, rooted = s.sem("own"), s.sem("rooted")
        block = s.block()

        @block.scalar
        def _(act):
            for b in (k.bn1, k.bn2):
                act.activation(b[:, 4, :], b[:, 4, :], ACT.Sqrt).then_inc(rooted, 1)

        @block.vector
        def _(v):
            me = Steps(v, own)
            v.wait_ge(rooted, 2)
            for b in (k.bn1, k.bn2):
                me.done(v.reciprocal(b[:, 4, :], b[:, 4, :]))
            me.sync()
            for b in (k.bn1, k.bn2):
                me.done(v.tensor_tensor(b[:, 1, :], b[:, 1, :], b[:, 4, :], ALU.mult))
            me.sync()
            for b in (k.bn1, k.bn2):
                me.done(v.tensor_tensor(b[:, 3, :], b[:, 3, :], b[:, 1, :], ALU.mult))
            me.sync()
            for b in (k.bn1, k.bn2):
                me.done(v.tensor_tensor(b[:, 2, :], b[:, 2, :], b[:, 3, :], ALU.add))




def norm_stats(k, stage):
    NT = k.NT
    with Scope(k.nc, stage) as s:
        st = s.sb("st", [P, NT, 6])
        a, b = s.sb("a", [P, NT]), s.sb("b", [P, NT])
        own, var_ready, rooted = s.sem("own"), s.sem("var_ready"), s.sem("rooted")
        block = s.block()

        @block.vector
        def _(v):
            me = Steps(v, own)
            with seven_loop(v, k) as i:
                me.enter(i, SEVEN)
                for j in range(SEVEN):
                    me.done(v.bn_stats(tile_of(st, i * SEVEN + j, 0, 6), tile_of(k.X, i * SEVEN + j)))
            me.leave(NT // SEVEN)
            me.sync()
            me.done(v.tensor_tensor(a[:, :], st[:, :, 1], st[:, :, 4], ALU.subtract))
            me.done(v.tensor_tensor(b[:, :], st[:, :, 2], st[:, :, 5], ALU.add))
            me.done(v.tensor_tensor(k.mean[:, :], st[:, :, 1], st[:, :, 4], ALU.add))
            me.sync()
            me.done(v.tensor_tensor(a[:, :], a[:, :], a[:, :], ALU.mult))
            me.done(v.tensor_scalar(b[:, :], b[:, :], 1.0 / D, LN_EPS, ALU.mult, ALU.add))
            me.done(v.tensor_scalar(k.mean[:, :], k.mean[:, :], 0.5, None, ALU.mult))
            me.sync()
            v.scalar_tensor_tensor(out=b[:, :], in0=a[:, :], scalar=0.25, in1=b[:, :], op0=ALU.mult,
                                   op1=ALU.add).then_inc(var_ready, 1)
            v.wait_ge(rooted, 1)
            v.reciprocal(k.rstd[:, :], b[:, :])

        @block.scalar
        def _(act):
            act.wait_ge(var_ready, 1)
            act.activation(b[:, :], b[:, :], ACT.Sqrt).then_inc(rooted, 1)


def normed(k, v, t, dst, channel_major=False):
    m, r = col(k.mean, t), col(k.rstd, t)
    if not channel_major:
        return v.tensor_scalar(dst, tile_of(k.X, t), m, r, ALU.subtract, ALU.mult)
    v.tensor_scalar(dst[:, 0:C], tile_of(k.X, t, 0, C), m, r, ALU.subtract, ALU.mult)
    return v.tensor_scalar(dst[:, C:D].rearrange("p (x c) -> p x c", x=3),
                           tile_of(k.X, t, C, D).rearrange("p (c x) -> p x c", x=3), m, r, ALU.subtract, ALU.mult)


def write_xn_table(k):
    NT = k.NT
    with Scope(k.nc, "xn") as s:
        ready, stored = s.sem("ready"), s.sem("stored")
        block = s.block()

        @block.vector
        def _(v):
            with seven_loop(v, k) as i:
                for j in range(SEVEN):
                    last = normed(k, v, i * SEVEN + j, tile_of(k.AGG, i * SEVEN + j))
                last.then_inc(ready, 1)

        @block.sync
        def _(sp):
            with seven_loop(sp, k) as i:
                sp.wait_ge(ready, i + 1)
                sp.dma_start(k.xn_tab[bass.ds(i * SEVEN * P, SEVEN * P), :].rearrange("(j p) d -> p j d", p=P),
                             k.AGG[:, bass.ds(i * SEVEN, SEVEN), 0:D]).then_inc(stored, 16)
            sp.wait_ge(stored, 16 * (NT // SEVEN))




class Group:

    def __init__(self, it, c):
        self.h, self.q, self.it = c % ROUND // SLOTS, c % SLOTS, it + c // ROUND
        self.c = c % ROUND
        self.n = it * HALVES + c // SLOTS


def edge_loop(k, eng):
    return eng.Fori(0, k.NG // ROUND)


def gather_groups(k, pool, table, edges, gx, edges_in, gathered, gx_free, credit, ticks):
    with edge_loop(k, pool) as it:
        for c in range(ROUND):
            g = Group(it, c)
            if g.q == 0:
                apart(pool, edges_in[g.h], (it + 1) * 16 * 3, ticks)
            apart(pool, gx_free[g.q], g.n + credit, ticks)
            for j in range(G):
                pool.indirect_dma_start(gx[:, g.q, j, 0:D], None, table,
                                        bass.IndirectOffsetOnAxis(edges[:, g.h, g.q, j:j + 1], 0),
                                        bounds_check=k.NT * P - 1, oob_is_err=False).then_inc(gathered[g.q], 16)


def choose(k, v, g, edges, first, pick, ready):
    for j in range(G):
        last = v.tensor_scalar(pick[:, j, :], k.lane[:, :], first, edges[:, g.h, g.q, G + j:G + j + 1],
                               ALU.add, ALU.is_equal)
    last.then_inc(ready, 1)


class Sums:

    def __init__(self, s, width, near):
        self.width, self.near = width, near
        self.pick = s.sb("pick", [P, near + 1, G, P])
        self.here = s.sb("here", [P, 1], I32)
        self.sums = s.ps("sums", [P, 3, 512])
        self.pick_ready, self.sums_ready = s.sems("pick_ready", SLOTS), s.sems("sums_ready", SLOTS)
        self.slot_free = s.sems("slot_free", SLOTS)
        self.added, self.more_picked, self.more_summed = s.sem("added"), s.sem("more_picked"), s.sem("more_summed")

    def pick_of(self, g):
        return self.pick[:, g.q % self.near]


def choose_group(k, v, g, edges, row, m):
    choose(k, v, g, edges, row[:, g.h, g.q, 1:2], m.pick_of(g), m.pick_ready[g.q])


def add_group(k, v, g, edges, row, m):
    b = v.value_load(row[0:1, g.h, g.q, 0:1], min_val=0, max_val=k.NT - 1)
    more = v.value_load(row[0:1, g.h, g.q, 2:3], min_val=0, max_val=k.NT - 1)

    def add_first():
        v.wait_ge(m.sums_ready[g.q], g.n + 1)
        v.wait_ge(m.added, g.it * ROUND + g.c + 2)
        tile = tile_of(k.AGG, b, 0, m.width)
        v.tensor_tensor(tile, tile, m.sums[:, g.q % 2, 0:m.width], ALU.add).then_inc(m.added, 1)

    def choose_more():
        v.drain()
        v.tensor_scalar(m.here[:, :], m.here[:, :], float(P), None, ALU.add)
        v.drain()
        choose(k, v, g, edges, m.here[:, 0:1], m.pick[:, m.near], m.more_picked)

    def add_more(i, count):
        v.wait_ge(m.more_summed, count)
        at = k.nc.s_assert_within(b + i, 1, k.NT - 1,
                                  skip_runtime_bounds_check_because="a group's tiles end at NT - 1")
        tile = tile_of(k.AGG, at, 0, m.width)
        v.tensor_tensor(tile, tile, m.sums[:, 2, 0:m.width], ALU.add)

    with v.If(more > 0):
        earlier = v.value_load(row[0:1, g.h, g.q, 3:4], min_val=0, max_val=k.NG * k.NT)
        v.tensor_copy(m.here[:, :], row[:, g.h, g.q, 1:2])
        choose_more()
        add_first()
        with v.If(more > 1):
            with v.Fori(1, more) as i:
                add_more(i, earlier + i)
                choose_more()
        add_more(more, earlier + more)
        v.drain()
    with v.Else():
        add_first()
    v.sem_inc(m.slot_free[g.q], 1)


def sum_group(k, pe, g, row, m, parts, arrived):
    more = pe.value_load(row[0:1, g.h, g.q, 2:3], min_val=0, max_val=k.NT - 1)
    for sem, value in arrived:
        pe.wait_ge(sem, value)

    def once(bank, pick):
        for j in range(G):
            for i, x in enumerate(parts(j)):
                mm = pe.matmul(m.sums[:, bank, 0:m.width], pick[:, j, :], x, start=(j == 0 and i == 0),
                               stop=(j == G - 1 and i == len(parts(j)) - 1))
        return mm
    once(g.q % 2, m.pick_of(g)).then_inc(m.sums_ready[g.q], 1)
    with pe.If(more > 0):
        earlier = pe.value_load(row[0:1, g.h, g.q, 3:4], min_val=0, max_val=k.NG * k.NT)
        with pe.Fori(0, more) as i:
            pe.wait_ge(m.more_picked, earlier + i + 1)
            once(2, m.pick[:, m.near]).then_inc(m.more_summed, 1)


def first_edges(k):
    with Scope(k.nc, "e0") as s:
        edges = s.sb("edges", [P, HALVES, SLOTS, 2 * G], I32)
        row = s.sb("row", [P, HALVES, SLOTS, 4], I32)
        attr = s.sb("attr", [32, HALVES, SLOTS * HALF])
        gx = s.sb("gx", [P, SLOTS, G, D + 4])
        m = Sums(s, D + 1, SLOTS)
        h1, h2, h3 = (s.sb(f"h{i}", [P, 2, 2 * HALF]) for i in (1, 2, 3))
        PAIRS = ROUND // 2
        hid = s.ps("hid", [P, PAIRS, 512])
        edges_in = s.sems("edges_in", HALVES)
        gathered = k.gathered[0]
        hid_mm, hid_act, hid_out = s.sems("hid_mm", PAIRS), s.sems("hid_act", PAIRS), s.sems("hid_out", 2)
        pool_ticks, act_ticks = s.sem("pool_ticks"), s.sem("act_ticks")
        block = s.block()

        hidden_before = [[(0, 0), (1, 0)], [(0, 1)], [(0, 2)], [(1, 1)], [(1, 2), (2, 0)], [(2, 1), (3, 0)], [(2, 2)],
                         [(3, 1)], [(3, 2)]]

        @block.sync
        def _(sp):
            load_experts(k, sp, k.W1_0, k.W2_0, k.W3_0)
            with edge_loop(k, sp) as it:
                for h in range(HALVES):
                    i = it * HALVES + h
                    sp.wait_ge(m.slot_free[SLOTS - 1], i + 1)
                    load_edges(k, sp, i, edges[:, h], row[:, h], edges_in[h])
                    sp.dma_start(attr[:, h, :], k.attr16[bass.ds(i, 1), :, :].rearrange("a p c -> (a p) c")
                                 ).then_inc(edges_in[h], 16)

        @block.gpsimd
        def _(pool):
            gather_groups(k, pool, k.xn_tab, edges, gx, edges_in, gathered, m.slot_free, 2, pool_ticks)

        @block.vector
        def _(v):
            v.memset(k.AGG[:, :, :], 0.0).then_inc(m.added, 2)
            for q in range(SLOTS):
                v.memset(gx[:, q, :, D:D + 1], 1.0).then_inc(m.slot_free[q], 2)
            with edge_loop(k, v) as it:
                def pick_group(c):
                    g = Group(it, c)
                    if g.q == 0:
                        v.wait_ge(edges_in[g.h], (it + 1) * 16 * 3)
                    choose_group(k, v, g, edges, row, m)

                pick_group(0)
                pick_group(1)
                for c in range(ROUND):
                    if c + 2 < ROUND:
                        pick_group(c + 2)
                    add_group(k, v, Group(it, c), edges, row, m)

        @block.tensor
        def _(pe):
            with edge_loop(k, pe) as it:
                def hidden(b, layer):
                    if layer == 0 and b % 2 == 0:
                        pe.wait_ge(edges_in[b // 2], (it + 1) * 16 * 3)
                    w, x = [(k.M1, attr[:, b // 2, b % 2 * 2 * HALF:(b % 2 + 1) * 2 * HALF]),
                            (k.M2, h1[:, b % 2, :]), (k.M3, h2[:, b % 2, :])][layer]
                    pe.wait_ge(hid_act[b], it * 3 + layer + 1)
                    pe.matmul(hid[:, b, :], w[:, :], x, start=True, stop=True).then_inc(hid_mm[b], 1)

                for c in range(ROUND + 1):
                    for b, layer in hidden_before[c]:
                        hidden(b, layer)
                    if c < ROUND:
                        g = Group(it, c)
                        sum_group(k, pe, g, row, m, lambda j: [gx[:, g.q, j, 0:D + 1]],
                                  [(m.pick_ready[g.q], g.n + 1), (m.added, it * ROUND + c + 1),
                                   (gathered[g.q], (g.n + 1) * 16 * G)])

        @block.scalar
        def _(act):
            for b in range(PAIRS):
                act.sem_inc(hid_act[b], 1)
            for i in range(2):
                act.sem_inc(hid_out[i], 16)
            with edge_loop(k, act) as it:
                for b, layer in [x for some in hidden_before for x in some]:
                    apart(act, hid_mm[b], it * 3 + layer + 1, act_ticks)
                    h = (h1, h2, h3)[layer][:, b % 2, :]
                    if layer == 2:
                        apart(act, hid_out[b % 2], (it * HALVES + b // 2 + 1) * 16, act_ticks)
                    act.activation(h, hid[:, b, :], ACT.Silu).then_inc(hid_act[b], 1)
                    if layer == 2:
                        act.wait_ge(hid_act[b], it * 3 + 4)
                        act.dma_start(k.hidden[bass.ds(it * HALVES + b // 2, 1), :,
                                               b % 2 * 2 * HALF:(b % 2 + 1) * 2 * HALF].rearrange("a p c -> (a p) c"),
                                      h).then_inc(hid_out[b % 2], 16)
            for i in range(2):
                act.wait_ge(hid_out[i], (k.NG // SLOTS + 1) * 16)


def load_edges(k, sp, i, edges, row, edges_in):
    sp.dma_start(edges.rearrange("p q e -> p (q e)"), k.edges[bass.ds(i, 1), :, :].rearrange("a p c -> (a p) c")
                 ).then_inc(edges_in, 16)
    sp.dma_start(row.rearrange("p q f -> p (q f)"),
                 k.table[bass.ds(i * SLOTS, SLOTS), :].rearrange("(a q) f -> a (q f)", a=1).to_broadcast([P, SLOTS * 4])
                 ).then_inc(edges_in, 16)


def second_edges(k):
    with Scope(k.nc, "e1") as s:
        edges = s.sb("edges", [P, HALVES, SLOTS, 2 * G], I32)
        row = s.sb("row", [P, HALVES, SLOTS, 4], I32)
        sh = s.sb("sh", [P, HALVES, SLOTS, G, 4])
        gx = s.sb("gx", [P, SLOTS, G, D])
        m = Sums(s, D, 2)
        hid = s.sb("hid", [P, SLOTS, HALF])
        xs = s.sb("xs", [P, 2, G, D])
        pr = s.sb("pr", [P, 2, G, 3, C])
        mb = s.sb("mb", [P, 2, G, D])
        spare = k.WALL[:, k.E1:k.E0].rearrange("p e i a n -> p (e i a n)")
        n = 2 * G * D
        ma = spare[:, 0:n].rearrange("p (r j d) -> p r j d", r=2, j=G)
        dot, t1x = (spare[:, n + i * n // 4:n + (i + 1) * n // 4].rearrange("p (r j d) -> p r j d", r=2, j=G)
                    for i in range(2))
        tw = s.ps("tw", [P, 2, G, D])
        edges_in, hid_in = s.sems("edges_in", HALVES), s.sems("hid_in", 2)
        gathered = k.gathered[1]
        tw_ready, xs_ready, msg_ready = s.sems("tw_ready", SLOTS), s.sems("xs_ready", SLOTS), s.sems("msg_ready", SLOTS)
        pool_ticks, own = s.sem("pool_ticks"), s.sem("own")
        block = s.block()
        PER = 3

        @block.sync
        def _(sp):
            load_experts(k, sp, k.W1_1, k.W2_1, k.W3_1)
            with edge_loop(k, sp) as it:
                for h in range(HALVES):
                    i = it * HALVES + h
                    sp.wait_ge(m.slot_free[SLOTS - 1], i + 1)
                    load_edges(k, sp, i, edges[:, h], row[:, h], edges_in[h])
                    sp.dma_start(sh[:, h].rearrange("p q j f -> p (q j f)"),
                                 k.attr4[bass.ds(i, 1), :, :].rearrange("a p c -> (a p) c")).then_inc(edges_in[h], 16)
                    for b in range(2):
                        sp.wait_ge(tw_ready[2 * b + 1], i + 1)
                        sp.dma_start(hid[:, 2 * b:2 * b + 2, :].rearrange("p q e -> p (q e)"),
                                     k.hidden[bass.ds(i, 1), :, b * 2 * HALF:(b + 1) * 2 * HALF
                                              ].rearrange("a p c -> (a p) c")).then_inc(hid_in[b], 16)

        @block.gpsimd
        def _(pool):
            gather_groups(k, pool, k.up_tab, edges, gx, edges_in, gathered, msg_ready, 1, pool_ticks)

        @block.scalar
        def _(act):
            with edge_loop(k, act) as it:
                for c in range(ROUND):
                    g, old = Group(it, c), Group(it, c - 2)
                    r = g.q % 2
                    act.wait_ge(msg_ready[old.q], old.n + 2)
                    act.wait_ge(gathered[g.q], (g.n + 1) * 16 * G)
                    for j in range(G):
                        act.activation(xs[:, r, j, :], gx[:, g.q, j, :], ACT.Copy, scale=sh[:, g.h, g.q, j, 0:1])
                        for x in range(3):
                            last = act.activation(pr[:, r, j, x, :], gx[:, g.q, j, C + C * x:2 * C + C * x],
                                                  ACT.Copy, scale=sh[:, g.h, g.q, j, 1 + x:2 + x])
                    last.then_inc(xs_ready[g.q], 1)

        @block.vector
        def _(v):
            me = Steps(v, own)
            for q in range(SLOTS):
                v.sem_inc(msg_ready[q], 1)
                v.sem_inc(m.slot_free[q], 2)
            v.memset(k.AGG[:, :, :], 0.0).then_inc(m.added, 2)
            with edge_loop(k, v) as it:
                me.enter(it, PER * ROUND)

                def messages(g):
                    r = g.q % 2
                    t0, t3, t1, t2 = (tw[:, r, :, C * i:C * i + C] for i in range(4))
                    if g.q == 0:
                        v.wait_ge(edges_in[g.h], (it + 1) * 16 * 3)
                    choose_group(k, v, g, edges, row, m)
                    v.wait_ge(xs_ready[g.q], g.n + 1)
                    me.done(v.tensor_tensor(dot[:, r], pr[:, r, :, 0, :], pr[:, r, :, 1, :], ALU.add))
                    v.wait_ge(tw_ready[g.q], g.n + 2)
                    v.tensor_tensor(ma[:, r, :, 0:C], t0, xs[:, r, :, 0:C], ALU.mult)
                    me.done(v.tensor_tensor(t1x[:, r], t1, gx[:, g.q, :, 0:C], ALU.mult))
                    me.sync()
                    me.done(v.tensor_tensor(dot[:, r], dot[:, r], pr[:, r, :, 2, :], ALU.add))
                    v.tensor_tensor(ma[:, r, :, C:D].rearrange("p j (x c) -> p j x c", x=3),
                                    t2.unsqueeze(2).to_broadcast([P, G, 3, C]),
                                    xs[:, r, :, C:D].rearrange("p j (x c) -> p j x c", x=3), ALU.mult)
                    v.tensor_tensor(mb[:, r, :, C:D].rearrange("p j (x c) -> p j x c", x=3),
                                    t1x[:, r].unsqueeze(2).to_broadcast([P, G, 3, C]),
                                    sh[:, g.h, g.q, :, 1:4].unsqueeze(3).to_broadcast([P, G, 3, C]), ALU.mult)
                    me.sync()
                    v.tensor_tensor(mb[:, r, :, 0:C], t3, dot[:, r], ALU.mult).then_inc(msg_ready[g.q], 1)

                def add(g):
                    add_group(k, v, g, edges, row, m)
                for c in range(ROUND):
                    messages(Group(it, c))
                    if c:
                        add(Group(it, c - 1))
                    else:
                        with v.If(it > 0):
                            add(Group(it, -1))
            me.leave(k.NG // ROUND)
            add(Group(k.NG // ROUND, -1))

        @block.tensor
        def _(pe):
            for q in range(SLOTS):
                pe.sem_inc(tw_ready[q], 1)

            def weights(g):
                r = g.q % 2
                if g.q == 0:
                    pe.wait_ge(edges_in[g.h], (g.it + 1) * 16 * 3)
                if g.q % 2 == 0:
                    pe.wait_ge(hid_in[g.q // 2], (g.n + 1) * 16)
                old = Group(g.it, g.c - 2)
                pe.wait_ge(msg_ready[old.q], old.n + 2)
                for j in (0, 2, 1, 3):
                    h, o = j // 2 * C, j % 2 * P
                    mm = pe.matmul(tw[:, r, j, :], hid[h:h + C, g.q, o:o + P], k.M4[h:h + C, :], start=True, stop=True)
                mm.then_inc(tw_ready[g.q], 1)

            def add_up(g):
                r = g.q % 2
                sum_group(k, pe, g, row, m, lambda j: [ma[:, r, j, :], mb[:, r, j, :]],
                          [(m.pick_ready[g.q], g.n + 1), (msg_ready[g.q], g.n + 2)])
            with edge_loop(k, pe) as it:
                for c in range(ROUND):
                    weights(Group(it, c))
                    if c:
                        add_up(Group(it, c - 1))
                    else:
                        with pe.If(it > 0):
                            add_up(Group(it, -1))
            add_up(Group(k.NG // ROUND, -1))




def node_product(k, stage, chunks, fill, plan, evacuate, store=None):
    NT = k.NT
    with Scope(k.nc, stage) as s:
        cat = s.sb("cat", [P, 2, chunks * P])
        catT = s.sb("catT", [P, 2, chunks, P])
        junk = s.sb("junk", [P, 2, D])
        p_t, p_o = s.ps("p_t", [P, 2, 512]), s.ps("p_o", [P, 2, 512])
        filled, turned, copied, product, taken = (
            s.sems(n, 2) for n in ("filled", "turned", "copied", "product", "taken"))
        ticks, stored = s.sem("ticks"), s.sem("stored")
        block = s.block()

        @block.vector
        def _(v):
            def fill_tile(t, b, i):
                v.wait_ge(turned[b], i + 1)
                fill(v, t, cat[:, b, :]).then_inc(filled[b], 1)

            def copy_turned(t, b, i):
                v.wait_ge(turned[b], i + 2)
                v.wait_ge(product[b], i + 1)
                v.tensor_copy(catT[:, b], p_t[:, b, 0:chunks * P].rearrange("p (a c) -> p a c", c=P)
                              ).then_inc(copied[b], 1)
            pipelined_tiles(v, k, fill_tile, copy_turned)

        @block.tensor
        def _(pe):
            for b in range(2):
                pe.sem_inc(turned[b], 1)
                pe.sem_inc(product[b], 1)
                pe.sem_inc(copied[b], 1)

            def turn(t, b, i):
                pe.wait_ge(filled[b], i + 1)
                pe.wait_ge(copied[b], i + 1)
                for a in range(chunks):
                    mm = pe.transpose(p_t[:, b, a * P:(a + 1) * P], cat[:, b, a * P:(a + 1) * P], k.ident[:, :])
                mm.then_inc(turned[b], 1)

            def multiply(t, b, i):
                pe.wait_ge(copied[b], i + 2)
                pe.wait_ge(taken[b], i + 1)
                for n, (a, w, c0, cn) in enumerate(plan):
                    same = [m for m, x in enumerate(plan) if x[2] == c0]
                    lhs = k.ones[0:1, :] if a is None else catT[:, b, a, :]
                    mm = pe.matmul(p_o[:, b, c0:c0 + cn], lhs, w, start=(n == same[0]), stop=(n == same[-1]))
                mm.then_inc(product[b], 1)
            pipelined_tiles(pe, k, turn, multiply)

        @block.scalar
        def _(act):
            for b in range(2):
                act.sem_inc(taken[b], 1)

            def body(t, b, i, last):
                apart(act, product[b], i + 2, ticks)
                evacuate(act, t, p_o[:, b, 0:D], junk[:, b, :]).then_inc(taken[b], 1)
            tile_loop(act, k, body)

        if store is not None:
            @block.sync
            def _(sp):
                def body(t, b, i, last):
                    sp.wait_ge(taken[b], i + 2)
                    sp.dma_start(store[bass.ds(t * P, P), :], tile_of(k.AGG, t)).then_inc(stored, 16)
                tile_loop(sp, k, body)
                sp.wait_ge(stored, 16 * NT)


def keep(k):
    return lambda act, t, ps, junk: act.activation(tile_of(k.AGG, t), ps, ACT.Copy)


def first_linear(k):
    with Scope(k.nc, "l0d") as s:
        block = s.block()
        own = s.sem("own")

        @block.vector
        def _(v):
            me = Steps(v, own)
            me.done(v.tensor_scalar(k.rdeg[:, :], k.AGG[:, :, D], 1.0, None, ALU.max))
            me.sync()
            me.done(v.reciprocal(k.rdeg[:, :], k.rdeg[:, :]))

    def fill(v, t, dst):
        v.tensor_scalar(dst[:, 0:D], tile_of(k.AGG, t), col(k.rdeg, t), None, ALU.mult)
        return normed(k, v, t, dst[:, D:2 * D])

    def evacuate(act, t, ps, junk):
        act.activation(tile_of(k.AGG, t), ps, ACT.Copy)
        return act.activation(junk, ps, ACT.Square, accum_out=col(k.ssq, t))

    plan = [(a, (k.WlT if a < KK else k.WrT)[:, a % KK, :], 0, D) for a in range(2 * KK)]
    plan.append((None, k.b_l[0:1, :], 0, D))
    node_product(k, "l0", 2 * KK, fill, plan, evacuate)


def diagonal_plan(first, w):
    return [(first + h, w[:, h, :], h * P, P) for h in range(KK)]


def scale_rows(k):
    with Scope(k.nc, "l2") as s:
        own, rooted = s.sem("own"), s.sem("rooted")
        block = s.block()

        @block.scalar
        def _(act):
            act.activation(k.ssq[:, :], k.ssq[:, :], ACT.Sqrt).then_inc(rooted, 1)

        @block.vector
        def _(v):
            me = Steps(v, own)
            v.wait_ge(rooted, 1)
            me.done(v.tensor_scalar(k.ssq[:, :], k.ssq[:, :], 1e-12, None, ALU.max))
            me.sync()
            me.done(v.reciprocal(k.ssq[:, :], k.ssq[:, :]))
            me.sync()
            with seven_loop(v, k) as i:
                for t in (i * SEVEN + j for j in range(SEVEN)):
                    v.tensor_scalar(tile_of(k.AGG, t), tile_of(k.AGG, t), col(k.ssq, t), None, ALU.mult)


def column_stats(k, stage, n):
    NT, r = k.NT, D - n
    with Scope(k.nc, stage) as s:
        sq = s.sb("sq", [P, SEVEN, D])
        mu = s.sb("mu", [P, D])
        p_m, p_s = s.ps("p_m", [P, 512]), s.ps("p_s", [P, 512])
        summed, mu_ready, centred, var_ready, rooted, own, ticks = (
            s.sem(x) for x in ("summed", "mu_ready", "centred", "var_ready", "rooted", "own", "ticks"))
        squared, added = s.sem("squared"), s.sem("added")
        block = s.block()
        passes = NT // SEVEN

        @block.tensor
        def _(pe):
            def over_tiles(body):
                if passes > 1:
                    with pe.Fori(0, passes - 1) as i:
                        for j in range(SEVEN):
                            body(i * SEVEN + j, j, i, k.ones[:, :])
                for j in range(SEVEN):
                    t = (passes - 1) * SEVEN + j
                    body(t, j, passes - 1, (k.ones if t < NT - 1 else k.ones_valid)[:, :])

            def first(t, j, i, ones):
                pe.matmul(p_m[:, 0:n], ones, tile_of(k.AGG, t, 0, n), start=False, stop=False)
            pe.matmul(p_m[:, 0:n], k.zeros[:, :], k.X[:, 0, 0:n], start=True, stop=False)
            over_tiles(first)
            pe.matmul(p_m[:, 0:n], k.zeros[:, :], k.X[:, 0, 0:n], start=False, stop=True).then_inc(summed, 1)
            pe.sem_inc(added, SEVEN)

            def second(t, j, i, ones):
                pe.wait_ge(squared, i * SEVEN + j + 1)
                pe.matmul(p_s[:, 0:D], ones, sq[:, j, :], start=False, stop=False).then_inc(added, 1)
            pe.matmul(p_s[:, 0:D], k.zeros[:, :], k.X[:, 0, 0:D], start=True, stop=False)
            over_tiles(second)
            pe.matmul(p_s[:, 0:D], k.zeros[:, :], k.X[:, 0, 0:D], start=False, stop=True).then_inc(added, 1)

        @block.vector
        def _(v):
            me = Steps(v, own)
            v.wait_ge(summed, 1)
            me.done(v.tensor_scalar(mu[:, 0:n], p_m[:, 0:n], 1.0 / k.N, None, ALU.mult))
            me.sync()
            with seven_loop(v, k) as i:
                a = k.AGG[:, bass.ds(i * SEVEN, SEVEN), 0:n]
                v.tensor_tensor(a, a, mu[:, 0:n].unsqueeze(1).to_broadcast([P, SEVEN, n]),
                                ALU.subtract).then_inc(centred, 1)
            v.wait_ge(added, SEVEN + NT + 1)
            if r:
                me.done(v.tensor_copy(mu[:, n:D], p_s[:, n:D]))
                me.sync()
                me.done(v.tensor_tensor(mu[:, n:n + C], mu[:, n:n + C], mu[:, n + C:n + 2 * C], ALU.add))
                me.sync()
                me.done(v.tensor_tensor(mu[:, n:n + C], mu[:, n:n + C], mu[:, n + 2 * C:D], ALU.add))
                me.sync()
                me.done(v.tensor_scalar(k.cscale[:, n:D].rearrange("p (x c) -> p x c", c=C),
                                        mu[:, n:n + C].unsqueeze(1).to_broadcast([P, 3, C]),
                                        1.0 / (3 * k.N), 1e-5, ALU.mult, ALU.add))
            me.done(v.tensor_scalar(k.cscale[:, 0:n], p_s[:, 0:n], 1.0 / k.N, 1e-5, ALU.mult, ALU.add))
            me.sync()
            v.sem_inc(var_ready, 1)
            v.wait_ge(rooted, 1)
            me.done(v.reciprocal(k.cscale[:, :], k.cscale[:, :]))

        @block.scalar
        def _(act):
            with seven_loop(act, k) as i:
                apart(act, centred, i + 1, ticks)
                for j in range(SEVEN):
                    apart(act, added, i * SEVEN + j + 1, ticks)
                    act.activation(sq[:, j, :], tile_of(k.AGG, i * SEVEN + j), ACT.Square).then_inc(squared, 1)
            act.wait_ge(var_ready, 1)
            act.activation(k.cscale[:, :], k.cscale[:, :], ACT.Sqrt).then_inc(rooted, 1)


def add_normed(k, stage, gamma, beta, n, relu, channel_major):
    with Scope(k.nc, stage) as s:
        own = s.sem("own")
        block = s.block()

        @block.vector
        def _(v):
            me = Steps(v, own)
            me.done(v.tensor_tensor(k.cscale[:, :], k.cscale[:, :], gamma, ALU.mult))
            me.sync()

            def body(tiles, i, per):
                me.enter(i, per)
                for t in tiles:
                    me.done(v.tensor_tensor(tile_of(k.AGG, t), tile_of(k.AGG, t), k.cscale[:, :], ALU.mult))
                me.sync()
                for t in tiles:
                    me.done(v.tensor_tensor(tile_of(k.AGG, t, 0, n), tile_of(k.AGG, t, 0, n), beta, ALU.add))
                me.sync()
                for t in tiles:
                    if relu:
                        me.done(v.scalar_tensor_tensor(out=tile_of(k.X, t), in0=tile_of(k.AGG, t), scalar=0.0,
                                                       in1=tile_of(k.X, t), op0=ALU.max, op1=ALU.add))
                    elif channel_major:
                        me.done(v.tensor_tensor(tile_of(k.X, t, 0, C), tile_of(k.AGG, t, 0, C),
                                                tile_of(k.X, t, 0, C), ALU.add))
                        xv = tile_of(k.X, t, C, D).rearrange("p (c x) -> p x c", x=3)
                        me.done(v.tensor_tensor(xv, tile_of(k.AGG, t, C, D).rearrange("p (x c) -> p x c", x=3),
                                                xv, ALU.add))
            per = SEVEN * (3 if relu else 4)
            with seven_loop(v, k) as i:
                body([i * SEVEN + j for j in range(SEVEN)], i, per)
            me.leave(k.NT // SEVEN)


def polynomial(k):
    NB = 7
    assert k.NT % NB == 0
    with Scope(k.nc, "po") as s:
        vv, sq3 = s.sb("vv", [P, NB, C]), s.sb("sq3", [P, NB, 3, C])
        a2 = s.sb("a2", [P, NB, C])
        f, g = s.sb("f", [P, NB, 2, C]), s.sb("g", [P, NB, 2, C])
        own, squared, used, ticks = s.sem("own"), s.sem("squared"), s.sem("used"), s.sem("ticks")
        block = s.block()

        def b(x):
            return x.unsqueeze(1).to_broadcast([P, NB] + list(x.shape[1:]))

        def two(x):
            return x.unsqueeze(2).to_broadcast([P, NB, 2, C])

        @block.scalar
        def _(act):
            with act.Fori(0, k.NT // NB) as i:
                apart(act, used, i + 1, ticks)
                act.activation(sq3[:, :, :, :].rearrange("p t x c -> p t (x c)"), k.AGG[:, bass.ds(i * NB, NB), C:D],
                               ACT.Square).then_inc(squared, 1)

        @block.vector
        def _(v):
            me = Steps(v, own)
            v.sem_inc(used, 1)
            with v.Fori(0, k.NT // NB) as i:
                me.enter(i, 11)
                A0 = k.AGG[:, bass.ds(i * NB, NB), 0:C]
                A1 = k.AGG[:, bass.ds(i * NB, NB), C:D].rearrange("p t (x c) -> p t x c", x=3)
                v.wait_ge(used, i + 1)
                me.done(v.tensor_tensor(a2[:, :, :], A0, A0, ALU.mult))
                me.done(v.tensor_tensor(f[:, :, :, :], two(A0), b(k.poly[:, 1]), ALU.mult))
                v.wait_ge(squared, i + 1)
                me.done(v.tensor_tensor(vv[:, :, :], sq3[:, :, 0, :], sq3[:, :, 1, :], ALU.add))
                me.sync()
                me.done(v.tensor_tensor(vv[:, :, :], vv[:, :, :], sq3[:, :, 2, :], ALU.add))
                me.done(v.tensor_tensor(g[:, :, :, :], two(a2[:, :, :]), b(k.poly[:, 2]), ALU.mult))
                me.done(v.tensor_tensor(f[:, :, :, :], f[:, :, :, :], b(k.poly[:, 0]), ALU.add))
                me.sync()
                me.done(v.tensor_tensor(f[:, :, :, :], f[:, :, :, :], g[:, :, :, :], ALU.add))
                me.sync()
                me.done(v.tensor_tensor(g[:, :, :, :], two(vv[:, :, :]), b(k.poly[:, 3]), ALU.mult))
                me.sync()
                me.done(v.tensor_tensor(f[:, :, :, :], f[:, :, :, :], g[:, :, :, :], ALU.add))
                me.done(v.tensor_tensor(a2[:, :, :], vv[:, :, :], b(k.poly_vv[:, :]), ALU.mult))
                me.sync()
                me.done(v.tensor_tensor(A0, A0, f[:, :, 0, :], ALU.mult))
                v.tensor_tensor(A1, A1, f[:, :, 1, :].unsqueeze(2).to_broadcast([P, NB, 3, C]), ALU.mult)
                me.sync()
                v.tensor_tensor(A0, A0, a2[:, :, :], ALU.add).then_inc(used, 1)
            me.leave(k.NT // NB)




def load_experts(k, sp, *weights):
    for e in range(weights[0].shape[0]):
        for i, w in enumerate(weights):
            sp.dma_start(k.WALL[:, e, i, :, :], w[e].rearrange("(kk p) n -> p kk n", p=P)).then_inc(k.experts_in, 16)


def top_bits(v, hi, x):
    return v.tensor_copy(hi, x)


def low_bits(v, lo, x, hi):
    return v.tensor_tensor(lo, x, hi, ALU.subtract)


def in_parts(lhs, rhs):
    (lh, ll), (rh, rl) = lhs, rhs
    return [(lh, rh), (lh, rl), (ll, rh)]


def experts(k, stage, E, scales, biases, last_bias, top2, router, out=None):
    NT = k.NT
    SMALL = CHUNK - 1
    small = (-NT) % CHUNK or CHUNK
    full = (NT - small * SMALL) // CHUNK
    assert full > 0
    with Scope(k.nc, stage) as s:
        store = s.sb("w_hi", [P, k.STORE], F32R)
        w_hi = store[:, 0:k.E0 * 3 * KK * D].rearrange("p (e i a n) -> p e i a n", e=k.E0, i=3, a=KK)
        w_lo = s.sb("w_lo", [P, k.E0, 3, KK, D], F32R)
        xn = s.sb("xn", [P, CHUNK, D])
        xT = s.sb("xT", [P, 2, KK, CHUNK * P], F32R)
        raw = s.sb("raw", [P, KK, CHUNK * P])
        h1, h2 = s.sb("h1", [P, 2, 2, KK, CHUNK * P], F32R), s.sb("h2", [P, 2, 2, KK, CHUNK * P], F32R)
        rT = s.sb("rT", [P, CHUNK * P])
        wT = rT[0:E, :]
        r_w = router.w1 if top2 else router.w2
        r_hi, r_lo = s.sb("r_hi", list(r_w.shape), F32R), s.sb("r_lo", list(r_w.shape), F32R)
        lg, ex, wt = (s.sb(n, [P, CHUNK, E]) for n in ("lg", "ex", "wt"))
        r1, r2, r3, r4 = (s.sb(n, [P, CHUNK, 1]) for n in ("r1", "r2", "r3", "r4"))
        s1, s2 = s.sb("s1", [P, CHUNK, E]), s.sb("s2", [P, CHUNK, E])
        p_x, p_1, p_2, p_y = (s.ps(n, [P, 2, 512]) for n in ("p_x", "p_1", "p_2", "p_y"))
        xn_ready, turned, xT_own, xT_ready, xT_used, r_mm, r_act, l_mm, ex_in, ex_out, w_ready, wT_mm, wT_v = (
            s.sem(n) for n in ("xn_ready", "turned", "xT_own", "xT_ready", "xT_used", "r_mm", "r_act", "l_mm",
                               "ex_in", "ex_out", "w_ready", "wT_mm", "wT_v"))
        h1_mm, h1_act, h2_mm, h2_act, parts_done, y_mm, y_added, own, parts_own, w_own, w_parts, stored, ticks = (
            s.sem(n) for n in ("h1_mm", "h1_act", "h2_mm", "h2_act", "parts_done", "y_mm", "y_added",
                               "own", "parts_own", "w_own", "w_parts", "stored", "ticks"))
        block = s.block()

        def chunks(eng, body, me=None, per=0):
            for n in range(small):
                def ahead_small(f):
                    f(n + 1, (n + 1) * SMALL, SMALL if n + 1 < small else CHUNK)
                if me:
                    me.enter(0, per)
                body(n, n * SMALL, SMALL, ahead_small)
                if me:
                    me.leave(1)
            with eng.Fori(0, full) as c:
                def ahead(f):
                    if full > 1:
                        with eng.If(c < full - 1):
                            f(c + small + 1, c * CHUNK + CHUNK + small * SMALL, CHUNK)
                if me:
                    me.enter(c, per)
                body(c + small, c * CHUNK + small * SMALL, CHUNK, ahead)
            if me:
                me.leave(full)

        def share(n, e):
            return n * (E + 1) + (e + 1 if e > 0 else -e)

        def part_number(n, layer, e):
            step = (0 if e == 0 else 2 * e - 1) if layer == 1 else min(2 * e + 2, 2 * E - 1)
            return n * 4 * E + 2 * step

        @block.vector
        def _(v):
            me = Steps(v, own)

            def norm_ahead(n, t, nt):
                v.wait_ge(turned, n + 1)
                for j in range(nt):
                    if not isinstance(t, int):
                        tile = k.nc.s_assert_within(t + j, 0, NT - 1, skip_runtime_bounds_check_because="a next chunk")
                    else:
                        tile = t + j
                    last = normed(k, v, tile, xn[:, j, :])
                last.then_inc(xn_ready, 1)

            def split_xT(n, t, nt):
                W = nt * P
                v.wait_ge(turned, n + 2)
                v.wait_ge(xT_used, n + 1)
                top_bits(v, xT[:, 0, :, 0:W], p_x[:, :, 0:W]).then_inc(xT_own, 1)
                v.wait_ge(xT_own, n + 1)
                low_bits(v, xT[:, 1, :, 0:W], p_x[:, :, 0:W], xT[:, 0, :, 0:W]).then_inc(xT_ready, 1)

            def split(layer, e, n, nt):
                h, acted = ((h1, h1_act), (h2, h2_act))[layer - 1]
                b, W = h[:, e % 2], nt * P
                for m in range(2):
                    v.wait_ge(acted, n * 2 * E + 2 * e + m + 3)
                    top_bits(v, b[:, 0, m, 0:W], raw[:, m, 0:W]).then_inc(parts_own, 1)
                for m in range(2):
                    v.wait_ge(parts_own, part_number(n, layer, e) + m + 1)
                    low_bits(v, b[:, 1, m, 0:W], raw[:, m, 0:W], b[:, 0, m, 0:W]).then_inc(parts_done, 1)

            def split_weights(e):
                top_bits(v, w_hi[:, e], k.WALL[:, e]).then_inc(w_own, 1)
                v.wait_ge(w_own, e + 1)
                low_bits(v, w_lo[:, e], k.WALL[:, e], w_hi[:, e]).then_inc(w_parts, 1)

            def split_first(n, t, nt):
                split(1, 0, n, nt)

            def body(n, t0, nt, ahead):
                W = nt * P
                L, X_, W_ = lg[:, 0:nt, :], ex[:, 0:nt, :], wt[:, 0:nt, :]
                a, b, c3, d = (r[:, 0:nt, :] for r in (r1, r2, r3, r4))
                S1, S2 = s1[:, 0:nt, :], s2[:, 0:nt, :]

                def wide(r):
                    return r.to_broadcast([P, nt, E])

                def routing():
                    rb = router.bias.unsqueeze(1).to_broadcast([P, nt, E])
                    v.wait_ge(l_mm, n + 1)
                    me.done(v.tensor_tensor(L, p_x[:, 0, 0:nt * E].rearrange("p (j e) -> p j e", e=E), rb, ALU.add))
                    me.sync()
                    me.done(v.tensor_reduce(a, L, AX.X, ALU.max))
                    me.sync()
                    me.done(v.tensor_tensor(L, L, wide(a), ALU.subtract))
                    me.sync()
                    v.sem_inc(ex_in, 1)
                    v.wait_ge(ex_out, n * (2 if top2 else 1) + 1)
                    me.done(v.tensor_reduce(a, X_, AX.X, ALU.add))
                    me.sync()
                    me.done(v.reciprocal(b, a))
                    me.sync()
                    if not top2:
                        me.done(v.tensor_tensor(W_, X_, wide(b), ALU.mult))
                        me.sync()
                        v.sem_inc(w_ready, 1)
                        return
                    rank = k.rank[:, 0:E].unsqueeze(1).to_broadcast([P, nt, E])
                    me.done(v.tensor_tensor(L, X_, wide(b), ALU.mult))
                    me.sync()
                    for top, S in ((c3, S1), (d, S2)):
                        me.done(v.tensor_reduce(top, L, AX.X, ALU.max))
                        me.sync()
                        me.done(v.tensor_tensor(S, L, wide(top), ALU.is_equal))
                        me.sync()
                        me.done(v.tensor_tensor(S, S, rank, ALU.mult))
                        me.sync()
                        me.done(v.tensor_reduce(a, S, AX.X, ALU.max))
                        me.sync()
                        me.done(v.tensor_tensor(S, S, wide(a), ALU.is_equal))
                        me.sync()
                        if S is S1:
                            me.done(v.scalar_tensor_tensor(out=L, in0=S, scalar=-2.0, in1=L, op0=ALU.mult, op1=ALU.add))
                            me.sync()
                    me.done(v.tensor_tensor(a, d, c3, ALU.subtract))
                    me.sync()
                    v.sem_inc(ex_in, 1)

                def routing_end():
                    v.wait_ge(ex_out, n * 2 + 2)
                    me.done(v.tensor_scalar(b, d, 1.0, None, ALU.add))
                    me.sync()
                    me.done(v.reciprocal(b, b))
                    me.sync()
                    me.done(v.tensor_tensor(d, d, b, ALU.mult))
                    me.done(v.tensor_tensor(S1, S1, wide(b), ALU.mult))
                    me.sync()
                    me.done(v.tensor_tensor(S2, S2, wide(d), ALU.mult))
                    me.sync()
                    me.done(v.tensor_tensor(W_, S1, S2, ALU.add))
                    me.sync()
                    v.sem_inc(w_ready, 1)

                def add_y(e):
                    v.wait_ge(y_mm, share(n, e) + 1)
                    v.wait_ge(y_added, share(n, e) + 1)
                    for j in range(nt):
                        y = p_y[:, j // 2, j % 2 * D:(j % 2 + 1) * D]
                        xt = tile_of(k.X, t0 + j)
                        if e < 0:
                            last = v.tensor_tensor(xt, y, xt, ALU.add)
                        else:
                            last = v.scalar_tensor_tensor(out=xt, in0=y, scalar=wt[:, j, e:e + 1], in1=xt,
                                                          op0=ALU.mult, op1=ALU.add)
                    last.then_inc(y_added, 1)
                for st in range(E + 3):
                    if 3 <= st < E + 2:
                        add_y(st - 3)
                    if 1 <= st < E:
                        split(1, st, n, nt)
                    if st == 2:
                        v.wait_ge(wT_mm, n + 1)
                        v.tensor_copy(wT[:, 0:W], p_x[0:E, 1, 0:W]).then_inc(wT_v, 1)
                    if st == 3:
                        add_y(-1)
                    if st == 0:
                        routing()
                    if st == 1 and top2:
                        routing_end()
                    if st == E:
                        ahead(split_xT)
                    if 1 <= st <= E:
                        split(2, st - 1, n, nt)
                    if st == E - 3:
                        ahead(norm_ahead)
                    if isinstance(n, int) and n == 0 and st + 2 < E:
                        split_weights(st + 2)
                    if st == E + 1:
                        ahead(split_first)
                    if st == E + 2:
                        add_y(E - 1)
            v.sem_inc(y_added, 1)
            norm_ahead(0, 0, SMALL)
            v.wait_ge(k.experts_in, 16 * 3 * (k.E0 + k.E1 if top2 else k.E0))
            me.done(top_bits(v, r_hi[:], r_w[:]))
            me.sync()
            me.done(low_bits(v, r_lo[:], r_w[:], r_hi[:]))
            split_xT(0, 0, SMALL)
            split_weights(0)
            split_weights(1)
            split_first(0, 0, SMALL)
            chunks(v, body, me, 6 if not top2 else 5 + 1 + 11 + 1 + 6)

        @block.scalar
        def _(act):
            act.sem_inc(h1_act, 2)
            act.sem_inc(h2_act, 2)
            act.sem_inc(parts_done, 2)

            def relu(dst, src, l, e, m):
                scale = scales[l][:, 2 * e + m:2 * e + m + 1] if scales else 1.0
                return act.activation(dst, src, ACT.Relu, bias=biases[l][:, 2 * e + m:2 * e + m + 1], scale=scale)

            def body(n, t0, nt, ahead):
                W = nt * P
                if top2:
                    act.wait_ge(r_mm, n + 1)
                    act.activation(rT[:, 0:W], p_x[:, 1, 0:W], ACT.Relu, bias=router.b1).then_inc(r_act, 1)
                for st in range(E + 1):
                    if st < E:
                        for m in range(2):
                            apart(act, parts_done, part_number(n, 1, st) + m + 1, ticks)
                            act.wait_ge(h1_mm, n * 2 * E + 2 * st + m + 1)
                            relu(raw[:, m, 0:W], p_1[:, m, 0:W], 0, st, m).then_inc(h1_act, 1)
                    if st == 0:
                        act.wait_ge(ex_in, n * (2 if top2 else 1) + 1)
                        act.activation(ex[:, 0:nt, :], lg[:, 0:nt, :], ACT.Exp).then_inc(ex_out, 1)
                    if st == 1 and top2:
                        act.wait_ge(ex_in, n * 2 + 2)
                        act.activation(r4[:, 0:nt, :], r1[:, 0:nt, :], ACT.Exp).then_inc(ex_out, 1)
                    if st >= 1:
                        for m in range(2):
                            apart(act, parts_done, part_number(n, 2, st - 1) + m + 1, ticks)
                            act.wait_ge(h2_mm, n * 2 * E + 2 * (st - 1) + m + 1)
                            relu(raw[:, m, 0:W], p_2[:, m, 0:W], 1, st - 1, m).then_inc(h2_act, 1)
            chunks(act, body)

        @block.tensor
        def _(pe):
            pe.sem_inc(turned, 1)
            pe.sem_inc(xT_used, 1)

            def product(dst, pairs):
                terms = [x for lhs, rhs in pairs for x in in_parts(lhs, rhs)]
                for i, (a, b) in enumerate(terms):
                    mm = pe.matmul(dst, a, b, start=(i == 0), stop=(i == len(terms) - 1))
                return mm

            def turn_ahead(n, t, nt):
                pe.wait_ge(xn_ready, n + 1)
                if not isinstance(n, int) or n:
                    pe.wait_ge(wT_v, n)
                for kk in range(KK):
                    for j in range(nt):
                        mm = pe.transpose(p_x[:, kk, j * P:(j + 1) * P], xn[:, j, kk * P:(kk + 1) * P], k.ident[:, :])
                mm.then_inc(turned, 1)

            def x(kk, a, b):
                return tuple(xT[:, i, kk, a:b] for i in range(2))

            def weights(e, i, kk, a, b):
                return w_hi[:, e, i, kk, a:b], w_lo[:, e, i, kk, a:b]

            def layer1(e, n, nt):
                W = nt * P
                if isinstance(n, int) and n == 0:
                    pe.wait_ge(w_parts, e + 1)
                for m in range(2):
                    pe.wait_ge(h1_act, n * 2 * E + 2 * e + m + 1)
                    mm = product(p_1[:, m, 0:W], [(weights(e, 0, kk, m * P, (m + 1) * P), x(kk, 0, W))
                                                  for kk in range(KK)])
                    mm.then_inc(h1_mm, 1)
                if e == E - 1:
                    pe.sem_inc(xT_used, 1)

            def begin(n, t, nt):
                W = nt * P

                def rw(kk):
                    return r_hi[:, kk, :], r_lo[:, kk, :]
                pe.wait_ge(xT_ready, n + 1)
                if top2:
                    product(p_x[:, 1, 0:W], [(rw(kk), x(kk, 0, W)) for kk in range(KK)]).then_inc(r_mm, 1)
                else:
                    for j in range(nt):
                        mm = product(p_x[:, 0, j * E:(j + 1) * E],
                                     [(x(kk, j * P, (j + 1) * P), rw(kk)) for kk in range(KK)])
                    mm.then_inc(l_mm, 1)
                layer1(0, n, nt)

            def body(n, t0, nt, ahead):
                W = nt * P

                def layer2(e):
                    pe.wait_ge(parts_done, part_number(n, 1, e) + 4)
                    for m in range(2):
                        pe.wait_ge(h2_act, n * 2 * E + 2 * e + m + 1)
                        mm = product(p_2[:, m, 0:W], [(weights(e, 1, kk, m * P, (m + 1) * P),
                                                       tuple(h1[:, e % 2, i, kk, 0:W] for i in range(2)))
                                                      for kk in range(KK)])
                        mm.then_inc(h2_mm, 1)

                def layer3(e):
                    pe.wait_ge(parts_done, part_number(n, 2, e) + 4)
                    pe.wait_ge(y_added, share(n, e) + 1)
                    for j in range(nt):
                        mm = product(p_y[:, j // 2, j % 2 * D:(j % 2 + 1) * D],
                                     [(tuple(h2[:, e % 2, i, kk, j * P:(j + 1) * P] for i in range(2)),
                                       weights(e, 2, kk, 0, D)) for kk in range(KK)])
                    mm.then_inc(y_mm, 1)

                for st in range(E + 2):
                    if 1 <= st < E:
                        layer1(st, n, nt)
                    if st == E + 1:
                        ahead(begin)
                    if st == 0 and top2:
                        pe.wait_ge(r_act, n + 1)
                        for j in range(nt):
                            mm = pe.matmul(p_x[:, 0, j * E:(j + 1) * E], rT[:, j * P:(j + 1) * P],
                                           router.w2[:, :], start=True, stop=True)
                        mm.then_inc(l_mm, 1)
                    if st == 2:
                        pe.wait_ge(w_ready, n + 1)
                        for j in range(nt):
                            mm = pe.transpose(p_x[0:E, 1, j * P:(j + 1) * P], wt[:, j, :], k.ident[:, :])
                        mm.then_inc(wT_mm, 1)
                    if st == 3:
                        pe.wait_ge(wT_v, n + 1)
                        pe.wait_ge(y_added, share(n, -1) + 1)
                        for j in range(nt):
                            mm = pe.matmul(p_y[:, j // 2, j % 2 * D:(j % 2 + 1) * D], wT[:, j * P:(j + 1) * P],
                                           last_bias, start=True, stop=True)
                        mm.then_inc(y_mm, 1)
                    if 0 <= st - 1 < E:
                        layer2(st - 1)
                    if 0 <= st - 2 < E:
                        layer3(st - 2)
                    if st == E - 2:
                        ahead(turn_ahead)
            turn_ahead(0, 0, SMALL)
            begin(0, 0, SMALL)
            chunks(pe, body)

        if out is not None:
            @block.sync
            def _(sp):
                def store(t, nt):
                    sp.dma_start(out[bass.ds(t * P, nt * P), :].rearrange("(j p) d -> p j d", p=P),
                                 k.X[:, bass.ds(t, nt), :]).then_inc(stored, 16)
                for n in range(small):
                    sp.wait_ge(y_added, (n + 1) * (E + 1) + 1)
                    store(n * SMALL, SMALL)
                if full > 1:
                    with sp.Fori(0, full - 1) as c:
                        sp.wait_ge(y_added, (c + small + 1) * (E + 1) + 1)
                        store(c * CHUNK + small * SMALL, CHUNK)
                sp.wait_ge(y_added, (small + full) * (E + 1) + 1)
                store(NT - CHUNK, CHUNK - 1)
                sp.dma_start(out[(NT - 1) * P:, :], k.X[0:k.LAST, NT - 1, :]).then_inc(stored, 16)
                sp.wait_ge(stored, 16 * (small + full + 1))




def program(nc, a, out):
    Scope.used.clear()
    k = Shared()
    k.nc = nc
    k.N = a["x"].shape[0]
    k.NT = -(-k.N // P)
    k.LAST = k.N - (k.NT - 1) * P
    k.NG = a["edges"].shape[0] * SLOTS
    k.E0, k.E1 = a["L0_ffn_W1"].shape[0], a["L1_ffn_expert_w1"].shape[0]
    NT = k.NT
    k.STORE = max(NT * (D + 1), k.E0 * 3 * KK * D)
    k.x, k.edges, k.dst_line = a["x"], a["edges"], a["dst_line"]
    k.attr16, k.attr4 = a["attr16"], a["attr4"]
    k.W1_0, k.W2_0, k.W3_0 = a["L0_ffn_W1"], a["L0_ffn_W2"], a["L0_ffn_Wo"]
    k.W1_1, k.W2_1, k.W3_1 = a["L1_ffn_expert_w1"], a["L1_ffn_expert_w2"], a["L1_ffn_expert_w3"]
    k.table = nc.dram_tensor("table", (k.NG, 4), I32).ap()
    k.xn_tab = nc.dram_tensor("xn_tab", (NT * P, D), F32).ap()
    k.up_tab = nc.dram_tensor("up_tab", (NT * P, D), F32).ap()
    k.hidden = nc.dram_tensor("hidden", (k.NG // SLOTS, P, SLOTS * HALF), F32).ap()

    with Scope(nc, "g") as s:
        k.X = s.sb("X", [P, NT, D])
        k.mean, k.rstd, k.rdeg, k.ssq = (s.sb(n, [P, NT]) for n in ("mean", "rstd", "rdeg", "ssq"))
        k.lane, k.ident, k.ones, k.ones_valid, k.zeros = (
            s.sb(n, [P, P]) for n in ("lane", "ident", "ones", "ones_valid", "zeros"))
        k.M4 = s.sb("M4", [P, D])
        k.bn1, k.bn2 = s.sb("bn1", [P, 5, 2 * k.E0]), s.sb("bn2", [P, 5, 2 * k.E0])
        bo0, br0, wr0 = s.sb("bo0", [k.E0, D]), s.sb("br0", [P, k.E0]), s.sb("wr0", [P, KK, k.E0])
        bo1, rb2, rb1 = s.sb("bo1", [k.E1, D]), s.sb("rb2", [P, k.E1]), s.sb("rb1", [P, 1])
        rw1, rw2 = s.sb("rw1", [P, KK, P]), s.sb("rw2", [P, k.E1])
        eb1, eb2 = s.sb("eb1", [P, 2 * k.E1]), s.sb("eb2", [P, 2 * k.E1])
        k.rank = s.sb("rank", [P, 8])

        k.gathered = s.sems("gathered_a", SLOTS), s.sems("gathered_b", SLOTS)
        k.experts_in = s.sem("experts_in")
        Scope.used.clear()

        def rows(x):
            return x.rearrange("(kk p) n -> p kk n", p=P)

        def spread(x, n):
            return x.rearrange("(a d) -> a d", a=1).to_broadcast([P, n])

        loads = [(bo0[:, :], a["L0_ffn_bo"]), (br0[:, :], spread(a["L0_ffn_br"], k.E0)),
                 (wr0[:, :, :], rows(a["L0_ffn_Wr"])),
                 (bo1[:, :], a["L1_ffn_expert_b3"]), (rb2[:, :], spread(a["L1_ffn_router_b2"], k.E1)),
                 (rb1[:, :], a["L1_ffn_router_b1"].rearrange("(p a) -> p a", a=1)),
                 (rw1[:, :, :], rows(a["L1_ffn_router_w1"])), (rw2[:, :], a["L1_ffn_router_w2"]),
                 (eb1[:, :], a["L1_ffn_expert_b1"]), (eb2[:, :], a["L1_ffn_expert_b2"]),
                 (k.rank[:, :], a["rank"].to_broadcast([P, 8]))]
        for bn, which in ((k.bn1, "1"), (k.bn2, "2")):
            for i, n in enumerate(("b", "g", "be", "m", "v")):
                loads.append((bn[:, i, :], a[f"L0_ffn_{n}{which}"]))
        for h in range(2):
            for to, of in enumerate((0, 3, 1, 2)):
                loads.append((k.M4[C * h:C * h + C, C * to:C * to + C], a["L1_gnn_M4"][:, C * of:C * of + C]))
        k.const_loads = loads


        def late_loads(stage, loads, zero=()):
            with Scope(nc, stage) as c:
                w_in, zeroed = c.sem("w_in"), c.sem("zeroed")
                block = c.block()

                @block.vector
                def _(v):
                    for z in zero:
                        last = v.memset(z[:], 0.0)
                    if zero:
                        last.then_inc(zeroed, 1)

                @block.sync
                def _(sp):
                    if zero:
                        sp.wait_ge(zeroed, 1)
                    for dst, src in loads:
                        sp.dma_start(dst, src).then_inc(w_in, 16)
                    sp.wait_ge(w_in, 16 * len(loads))

        def rooms(x):
            k.AGG = x.sb("AGG", [P, k.STORE])[:, 0:NT * (D + 1)].rearrange("p (t d) -> p t d", d=D + 1)
            k.WALL = x.sb("WALL", [P, k.E0, 3, KK, D])
            k.cscale = x.sb("cscale", [P, D])

        with Scope(nc, "g0") as x:
            rooms(x)
            with Scope(nc, "mlp") as m:
                k.M1, k.M2, k.M3 = m.sb("M1", [32, P]), m.sb("M2", [P, P]), m.sb("M3", [P, P])
                for h in range(2):
                    loads.append((k.M1[16 * h:16 * h + 16, C * h:C * h + C], a["L1_gnn_M1"]))
                    loads += [(w[C * h:C * h + C, C * h:C * h + C], a[n])
                              for w, n in ((k.M2, "L1_gnn_M2"), (k.M3, "L1_gnn_M3"))]
                k.cleared = [k.M1, k.M2, k.M3, k.zeros]
                setup(k)
                bn_roots(k)
                norm_stats(k, "n0")
                write_xn_table(k)
                first_edges(k)
            with Scope(nc, "w0") as w:
                k.WlT, k.WrT = w.sb("WlT", [P, KK, D]), w.sb("WrT", [P, KK, D])
                k.b_l = w.sb("b_l", [1, D])
                gamma, beta = w.sb("gamma", [P, D]), w.sb("beta", [P, D])
                late_loads("w0l", [(k.b_l[:, :], a["L0_gnn_b_l"].rearrange("(a d) -> a d", a=1)),
                                   (k.WlT[:, :, :], rows(a["L0_gnn_W_lT"])), (k.WrT[:, :, :], rows(a["L0_gnn_W_rT"])),
                                   (gamma[:, :], spread(a["L0_gnn_gamma"], D)),
                                   (beta[:, :], spread(a["L0_gnn_beta"], D))])
                first_linear(k)
                scale_rows(k)
                column_stats(k, "c0", D)
                add_normed(k, "a0", gamma[:, :], beta[:, :], D, True, False)
            norm_stats(k, "n1")
        experts(k, "f0", k.E0, (k.bn1[:, 1, :], k.bn2[:, 1, :]), (k.bn1[:, 2, :], k.bn2[:, 2, :]), bo0[:, :], False,
                Router(w2=wr0, bias=br0[:, :]))
        clear_semaphores(nc)
        with Scope(nc, "g1") as x:
            rooms(x)
            norm_stats(k, "n2")
            with Scope(nc, "w1") as w:
                ups = w.sb("ups", [P, KK, P])
                late_loads("w1l", block_diagonal_loads(ups, a["L1_gnn_W_up0"], a["L1_gnn_W_up1"]), [ups])
                node_product(k, "up", KK, lambda v, t, dst: normed(k, v, t, dst, True), diagonal_plan(0, ups), keep(k),
                             store=k.up_tab)
            second_edges(k)
            clear_semaphores(nc)
            with Scope(nc, "w2") as w:
                lins, wbs, wscs = (w.sb(n, [P, KK, P]) for n in ("lins", "wbs", "wscs"))
                k.poly, k.poly_vv = w.sb("poly", [P, 4, 2, C]), w.sb("poly_vv", [P, C])
                gamma, beta = w.sb("gamma", [P, D]), w.sb("beta", [P, C])
                c0, c1 = a["L1_gnn_Wc0T"], a["L1_gnn_Wc1T"]

                def line(x):
                    return x.to_broadcast([P, C])
                polys = [(k.poly[:, i, 0, :], line(c0[n:n + 1, :])) for i, n in enumerate((0, 1, 3, 4))]
                polys += [(k.poly[:, i, 1, :], line(c1[i:i + 1, :])) for i in range(4)]
                polys.append((k.poly_vv[:, :], line(c0[2:3, :])))
                gammas = [(gamma[:, 0:C], spread(a["L1_gnn_gamma0"], C)), (beta[:, :], spread(a["L1_gnn_beta0"], C))]
                gammas += [(gamma[:, C + C * x:2 * C + C * x], spread(a["L1_gnn_gamma1"], C)) for x in range(3)]
                late_loads("w2l", block_diagonal_loads(lins, a["L1_gnn_W_lin0"], a["L1_gnn_W_lin1"])
                           + block_diagonal_loads(wbs, a["L1_gnn_WB0"], a["L1_gnn_WB1"])
                           + block_diagonal_loads(wscs, a["L1_gnn_Wsc0"], a["L1_gnn_Wsc1"]) + polys + gammas,
                           [lins, wbs, wscs])
                node_product(k, "li", KK, lambda v, t, dst: v.tensor_copy(dst[:, 0:D], tile_of(k.AGG, t)),
                             diagonal_plan(0, lins), keep(k))
                polynomial(k)

                def fill(v, t, dst):
                    v.tensor_copy(dst[:, 0:D], tile_of(k.AGG, t))
                    return normed(k, v, t, dst[:, D:2 * D], True)
                node_product(k, "ob", 2 * KK, fill,
                             [x for h in range(KK) for x in (diagonal_plan(0, wbs)[h], diagonal_plan(KK, wscs)[h])],
                             keep(k))
                column_stats(k, "c1", C)
                add_normed(k, "a1", gamma[:, :], beta[:, :], C, False, True)
            norm_stats(k, "n3")
        experts(k, "f1", k.E1, None, (eb1[:, :], eb2[:, :]), bo1[:, :], True,
                Router(w1=rw1, b1=rb1[:, 0:1], w2=rw2, bias=rb2[:, :]), out=out)


def block_diagonal_loads(buf, w0, w1):
    return [(buf[0:C, 0, 0:C], w0), (buf[C:P, 0, C:P], w1), (buf[0:C, 1, 0:C], w1), (buf[C:P, 1, C:P], w1)]




def lay_out(inputs):
    import numpy as np

    a = {n: np.asarray(v) for n, v in inputs.items()}
    n, e = a["x"].shape[0], a["src"].shape[0]
    ng = -(-e // (GE * ROUND)) * ROUND
    pad = ng * GE - e
    src = np.concatenate([a.pop("src"), np.zeros(pad, np.int32)]).astype(np.int32, copy=False)
    dst = np.concatenate([a.pop("dst"), np.full(pad + 1, NO_NODE, np.int32)]).astype(np.int32, copy=False)

    def by_slots(v):
        return v.reshape(ng // SLOTS, SLOTS, G, P, -1).transpose(0, 3, 1, 2, 4)
    a["dst_line"] = dst
    a["edges"] = np.concatenate([by_slots(src)[..., 0], by_slots(dst[:-1])[..., 0]], -1).reshape(ng // SLOTS, P, -1)
    attr4 = np.concatenate([a.pop("edge_attr_4"), np.zeros((pad, 4), np.float32)])
    a["attr4"] = by_slots(attr4).reshape(ng // SLOTS, P, -1)
    attr16 = np.concatenate([a.pop("edge_attr_16"), np.zeros((pad, 16), np.float32)])
    a["attr16"] = attr16.reshape(ng // SLOTS, SLOTS, 2, HALF, 16).transpose(0, 2, 4, 1, 3).reshape(
        ng // SLOTS, 32, SLOTS * HALF)
    a["rank"] = np.arange(8, 0, -1, dtype=np.float32)[None]
    for w in ("W_l", "W_r"):
        a[f"L0_gnn_{w}T"] = a.pop(f"L0_gnn_{w}").T
    for w in ("Wc0", "Wc1"):
        a[f"L1_gnn_{w}T"] = a.pop(f"L1_gnn_{w}").T
    for name in [f"L0_ffn_{x}{i}" for x in ("b", "g", "be", "m", "v") for i in (1, 2)] + [
            "L1_ffn_expert_b1", "L1_ffn_expert_b2"]:
        ex = a[name].shape[0]
        a[name] = a[name].reshape(ex, 2, P).transpose(2, 0, 1).reshape(P, 2 * ex)
    return {n: np.ascontiguousarray(v) for n, v in a.items()}


def kernel(**inputs):
    import concourse.bacc as bacc
    from concourse.bass_utils import run_bass_kernel_spmd

    arrays = lay_out(inputs)
    nc = bacc.Bacc("TRN2", target_bir_lowering=False, num_devices=1)
    aps = {n: nc.dram_tensor(f"in_{n}", v.shape, mybir.dt.from_np(v.dtype), kind="ExternalInput").ap()
           for n, v in arrays.items()}
    out = nc.dram_tensor("out_dram", arrays["x"].shape, F32, kind="ExternalOutput").ap()
    program(nc, aps, out)
    r = run_bass_kernel_spmd(nc, [{f"in_{n}": v for n, v in arrays.items()}], core_ids=[0])
    return r.results[0]["out_dram"]
```
